# Optimizing a Trainium2 kernel written in Bass

```python
import numpy as np
import jax
import jax.numpy as jnp

def _softmax(x, axis=-1):
    return jax.nn.softmax(x, axis=axis)

def _gelu(x):
    return jax.nn.gelu(x, approximate=True)

def _silu(x):
    return jax.nn.silu(x)

def _sigmoid(x):
    return jax.nn.sigmoid(x)

def _layernorm(x, axis=-1, eps=1e-05):
    m = jnp.mean(x, axis=axis, keepdims=True)
    v = jnp.var(x, axis=axis, keepdims=True)
    return (x - m) / jnp.sqrt(v + eps)

def _scatter_add(tgt, idx, src, axis=0):
    return tgt.at[idx].add(src)

def _segment_sum(src, seg, n):
    return jax.ops.segment_sum(src, seg, n)
kernel_name = 'mk_adaln_d2_jaxref_r8_9878aa'

def setup_inputs(seed: int=0):
    np.random.seed(seed)
    _w = jnp.asarray

    def _L0_attn_setup():
        import jax, jax.numpy as jnp
        import numpy as np
        EMBED_DIM = 256
        NUM_HEADS = 16
        HEAD_DIM = EMBED_DIM // NUM_HEADS
        WINDOW = 64

        def _sliding_window_attn(q, k, v, window):
            B, H, S, d = q.shape
            C = window
            nc = S // C
            qc = q.reshape(B, H, nc, C, d)

            def two_chunks(t):
                tc = t.reshape(B, H, nc, C, d)
                prev = jnp.pad(tc[:, :, :-1], ((0, 0), (0, 0), (1, 0), (0, 0), (0, 0)))
                return jnp.concatenate([prev, tc], axis=3)
            kc = two_chunks(k)
            vc = two_chunks(v)
            scale = 1.0 / np.sqrt(d).astype(np.float32)
            scores = jnp.einsum('bhnid,bhnjd->bhnij', qc, kc) * scale
            i = jnp.arange(C)[:, None]
            j = jnp.arange(2 * C)[None, :]
            band = (j >= i) & (j <= i + C)
            kv_global = (jnp.arange(nc)[:, None, None] - 1) * C + j[None]
            mask = band[None] & (kv_global >= 0)
            scores = jnp.where(mask[None, None], scores, jnp.finfo(scores.dtype).min)
            probs = jax.nn.softmax(scores, axis=-1)
            out = jnp.einsum('bhnij,bhnjd->bhnid', probs, vc)
            return out.reshape(B, H, S, d)
        key = jax.random.key(seed)
        k1, k2, k3 = jax.random.split(key, 3)
        B, S = (2, 512)
        x = jax.random.normal(k1, (B, S, EMBED_DIM), dtype=jnp.float32)
        w_qkv = jax.random.normal(k2, (3 * EMBED_DIM, EMBED_DIM), dtype=jnp.float32) * 0.02
        w_out = jax.random.normal(k3, (EMBED_DIM, EMBED_DIM), dtype=jnp.float32) * 0.02
        return {'x': x, 'w_qkv': w_qkv, 'w_out': w_out}
    _L0_attn_in = _L0_attn_setup()

    def _L0_ffn_setup():
        import jax, jax.numpy as jnp
        import numpy as np
        DIM = 256
        INTER = 176
        E = 16
        TOPK = 4
        G = 4
        TOPK_G = 2
        N_SHARED = 2
        SHARED_INTER = N_SHARED * INTER
        ROUTE_SCALE = 1.0

        def _moe_forward(x, Wg, W1, W3, W2, Ws1, Ws3, Ws2):
            B, S, D = x.shape
            xt = x.reshape(-1, D)
            T = xt.shape[0]
            scores = jax.nn.softmax(xt @ Wg.T, axis=-1)
            sg = scores.reshape(T, G, E // G)
            group_scores = sg.max(axis=-1)
            gidx = jax.lax.top_k(group_scores, TOPK_G)[1]
            gmask = jax.nn.one_hot(gidx, G, dtype=jnp.float32).sum(axis=1) > 0
            masked = jnp.where(gmask[:, :, None], sg, -jnp.inf).reshape(T, E)
            topi = jax.lax.top_k(masked, TOPK)[1]
            weights = jnp.take_along_axis(scores, topi, axis=1) * ROUTE_SCALE
            combine = jnp.zeros((T, E), xt.dtype).at[jnp.arange(T)[:, None], topi].add(weights)
            h = jax.nn.silu(jnp.einsum('td,eid->eti', xt, W1)) * jnp.einsum('td,eid->eti', xt, W3)
            expert_out = jnp.einsum('eti,edi->etd', h, W2)
            y = jnp.einsum('etd,te->td', expert_out, combine)
            z = jax.nn.silu(xt @ Ws1.T) * (xt @ Ws3.T) @ Ws2.T
            return (y + z).reshape(B, S, D)
        key = jax.random.key(seed)
        ks = jax.random.split(key, 8)
        s = 0.02
        x = jax.random.normal(ks[0], (1, 256, DIM), dtype=jnp.float32)
        Wg = jax.random.normal(ks[1], (E, DIM), dtype=jnp.float32) * s
        W1 = jax.random.normal(ks[2], (E, INTER, DIM), dtype=jnp.float32) * s
        W3 = jax.random.normal(ks[3], (E, INTER, DIM), dtype=jnp.float32) * s
        W2 = jax.random.normal(ks[4], (E, DIM, INTER), dtype=jnp.float32) * s
        Ws1 = jax.random.normal(ks[5], (SHARED_INTER, DIM), dtype=jnp.float32) * s
        Ws3 = jax.random.normal(ks[6], (SHARED_INTER, DIM), dtype=jnp.float32) * s
        Ws2 = jax.random.normal(ks[7], (DIM, SHARED_INTER), dtype=jnp.float32) * s
        return {'x': x, 'Wg': Wg, 'W1': W1, 'W3': W3, 'W2': W2, 'Ws1': Ws1, 'Ws3': Ws3, 'Ws2': Ws2}
    _L0_ffn_in = _L0_ffn_setup()
    _L0_c = _w((lambda *s: np.random.randn(*s).astype(np.float32) * 0.05)(2, 256))
    _L0_wmod = _w((lambda *s: np.random.randn(*s).astype(np.float32) * 0.05)(256, 6 * 256) * 256 ** (-0.5))

    def _L1_attn_setup():
        import jax, jax.numpy as jnp
        import numpy as np
        D_MODEL = 256
        N_HEADS = 16
        HEAD_DIM = D_MODEL // N_HEADS
        NEG_BIG = -1e+30
        key = jax.random.key(seed)
        ks = jax.random.split(key, 9)
        B, T = (2, 256)
        s_in = 1.0 / np.sqrt(D_MODEL)
        s_hd = 1.0 / np.sqrt(D_MODEL)
        return {'q_input': jax.random.normal(ks[0], (B, T, D_MODEL), dtype=jnp.float32), 'Wq': jax.random.normal(ks[1], (D_MODEL, D_MODEL), dtype=jnp.float32) * s_in, 'bq': jnp.zeros((D_MODEL,), dtype=jnp.float32), 'Wk': jax.random.normal(ks[2], (HEAD_DIM, D_MODEL), dtype=jnp.float32) * s_in, 'bk': jnp.zeros((HEAD_DIM,), dtype=jnp.float32), 'Wv': jax.random.normal(ks[3], (HEAD_DIM, D_MODEL), dtype=jnp.float32) * s_in, 'bv': jnp.zeros((HEAD_DIM,), dtype=jnp.float32), 'Wo': jax.random.normal(ks[4], (D_MODEL, D_MODEL), dtype=jnp.float32) * s_hd, 'bo': jnp.zeros((D_MODEL,), dtype=jnp.float32)}
    _L1_attn_in = _L1_attn_setup()

    def _L1_ffn_setup():
        import jax, jax.numpy as jnp
        import numpy as np
        B, S, D = (2, 256, 256)
        E = 8
        TOPK = 2
        H_SHARED = 1024
        H_ROUTED = 128
        STD = 0.02
        key = jax.random.key(seed)
        ks = jax.random.split(key, 7)
        return {'x': jax.random.normal(ks[0], (B, S, D), jnp.float32), 'w12': jax.random.normal(ks[1], (E, 2 * H_ROUTED, D), jnp.float32) * STD, 'w3': jax.random.normal(ks[2], (E, D, H_ROUTED), jnp.float32) * STD, 'router_w': jax.random.normal(ks[3], (E, D), jnp.float32) * STD, 'expert_bias': jnp.zeros((E,), jnp.float32), 'sw1': jax.random.normal(ks[4], (H_SHARED, D), jnp.float32) * STD, 'sw2': jax.random.normal(ks[5], (H_SHARED, D), jnp.float32) * STD, 'sw3': jax.random.normal(ks[6], (D, H_SHARED), jnp.float32) * STD}
    _L1_ffn_in = _L1_ffn_setup()
    _L1_c = _w((lambda *s: np.random.randn(*s).astype(np.float32) * 0.05)(2, 256))
    _L1_wmod = _w((lambda *s: np.random.randn(*s).astype(np.float32) * 0.05)(256, 6 * 256) * 256 ** (-0.5))
    _d = {'L0_attn_x': _L0_attn_in['x'], 'L0_attn_w_qkv': _L0_attn_in['w_qkv'], 'L0_attn_w_out': _L0_attn_in['w_out'], 'L0_ffn_Wg': _L0_ffn_in['Wg'], 'L0_ffn_W1': _L0_ffn_in['W1'], 'L0_ffn_W3': _L0_ffn_in['W3'], 'L0_ffn_W2': _L0_ffn_in['W2'], 'L0_ffn_Ws1': _L0_ffn_in['Ws1'], 'L0_ffn_Ws3': _L0_ffn_in['Ws3'], 'L0_ffn_Ws2': _L0_ffn_in['Ws2'], 'L0_c': _L0_c, 'L0_wmod': _L0_wmod, 'L1_attn_Wq': _L1_attn_in['Wq'], 'L1_attn_bq': _L1_attn_in['bq'], 'L1_attn_Wk': _L1_attn_in['Wk'], 'L1_attn_bk': _L1_attn_in['bk'], 'L1_attn_Wv': _L1_attn_in['Wv'], 'L1_attn_bv': _L1_attn_in['bv'], 'L1_attn_Wo': _L1_attn_in['Wo'], 'L1_attn_bo': _L1_attn_in['bo'], 'L1_ffn_w12': _L1_ffn_in['w12'], 'L1_ffn_w3': _L1_ffn_in['w3'], 'L1_ffn_router_w': _L1_ffn_in['router_w'], 'L1_ffn_expert_bias': _L1_ffn_in['expert_bias'], 'L1_ffn_sw1': _L1_ffn_in['sw1'], 'L1_ffn_sw2': _L1_ffn_in['sw2'], 'L1_ffn_sw3': _L1_ffn_in['sw3'], 'L1_c': _L1_c, 'L1_wmod': _L1_wmod}
    _x0 = _d['L0_attn_x']
    _d['L0_attn_x'] = jax.random.normal(jax.random.fold_in(jax.random.key(seed), 1), (2, 512, 256), dtype=_x0.dtype)
    del _x0
    return _d

def reference(L0_attn_x, L0_attn_w_qkv, L0_attn_w_out, L0_ffn_Wg, L0_ffn_W1, L0_ffn_W3, L0_ffn_W2, L0_ffn_Ws1, L0_ffn_Ws3, L0_ffn_Ws2, L0_c, L0_wmod, L1_attn_Wq, L1_attn_bq, L1_attn_Wk, L1_attn_bk, L1_attn_Wv, L1_attn_bv, L1_attn_Wo, L1_attn_bo, L1_ffn_w12, L1_ffn_w3, L1_ffn_router_w, L1_ffn_expert_bias, L1_ffn_sw1, L1_ffn_sw2, L1_ffn_sw3, L1_c, L1_wmod):

    def _L0_attn_ref(x, w_qkv, w_out):
        import jax, jax.numpy as jnp
        import numpy as np
        EMBED_DIM = 256
        NUM_HEADS = 16
        HEAD_DIM = EMBED_DIM // NUM_HEADS
        WINDOW = 64

        def _sliding_window_attn(q, k, v, window):
            B, H, S, d = q.shape
            C = window
            nc = S // C
            qc = q.reshape(B, H, nc, C, d)

            def two_chunks(t):
                tc = t.reshape(B, H, nc, C, d)
                prev = jnp.pad(tc[:, :, :-1], ((0, 0), (0, 0), (1, 0), (0, 0), (0, 0)))
                return jnp.concatenate([prev, tc], axis=3)
            kc = two_chunks(k)
            vc = two_chunks(v)
            scale = 1.0 / np.sqrt(d).astype(np.float32)
            scores = jnp.einsum('bhnid,bhnjd->bhnij', qc, kc) * scale
            i = jnp.arange(C)[:, None]
            j = jnp.arange(2 * C)[None, :]
            band = (j >= i) & (j <= i + C)
            kv_global = (jnp.arange(nc)[:, None, None] - 1) * C + j[None]
            mask = band[None] & (kv_global >= 0)
            scores = jnp.where(mask[None, None], scores, jnp.finfo(scores.dtype).min)
            probs = jax.nn.softmax(scores, axis=-1)
            out = jnp.einsum('bhnij,bhnjd->bhnid', probs, vc)
            return out.reshape(B, H, S, d)
        B, S, E = x.shape
        qkv = jnp.einsum('bse,fe->bsf', x, w_qkv)
        qkv = qkv.reshape(B, S, 3, NUM_HEADS, HEAD_DIM)
        qkv = jnp.transpose(qkv, (2, 0, 3, 1, 4))
        q, k, v = (qkv[0], qkv[1], qkv[2])
        attn = _sliding_window_attn(q, k, v, WINDOW)
        attn = jnp.transpose(attn, (0, 2, 1, 3)).reshape(B, S, E)
        return jnp.einsum('bse,fe->bsf', attn, w_out)

    def _L0_ffn_ref(x, Wg, W1, W3, W2, Ws1, Ws3, Ws2):
        import jax, jax.numpy as jnp
        import numpy as np
        DIM = 256
        INTER = 176
        E = 16
        TOPK = 4
        G = 4
        TOPK_G = 2
        N_SHARED = 2
        SHARED_INTER = N_SHARED * INTER
        ROUTE_SCALE = 1.0

        def _moe_forward(x, Wg, W1, W3, W2, Ws1, Ws3, Ws2):
            B, S, D = x.shape
            xt = x.reshape(-1, D)
            T = xt.shape[0]
            scores = jax.nn.softmax(xt @ Wg.T, axis=-1)
            sg = scores.reshape(T, G, E // G)
            group_scores = sg.max(axis=-1)
            gidx = jax.lax.top_k(group_scores, TOPK_G)[1]
            gmask = jax.nn.one_hot(gidx, G, dtype=jnp.float32).sum(axis=1) > 0
            masked = jnp.where(gmask[:, :, None], sg, -jnp.inf).reshape(T, E)
            topi = jax.lax.top_k(masked, TOPK)[1]
            weights = jnp.take_along_axis(scores, topi, axis=1) * ROUTE_SCALE
            combine = jnp.zeros((T, E), xt.dtype).at[jnp.arange(T)[:, None], topi].add(weights)
            h = jax.nn.silu(jnp.einsum('td,eid->eti', xt, W1)) * jnp.einsum('td,eid->eti', xt, W3)
            expert_out = jnp.einsum('eti,edi->etd', h, W2)
            y = jnp.einsum('etd,te->td', expert_out, combine)
            z = jax.nn.silu(xt @ Ws1.T) * (xt @ Ws3.T) @ Ws2.T
            return (y + z).reshape(B, S, D)
        return _moe_forward(x, Wg, W1, W3, W2, Ws1, Ws3, Ws2)

    def _L1_attn_ref(q_input, Wq, bq, Wk, bk, Wv, bv, Wo, bo):
        import jax, jax.numpy as jnp
        import numpy as np
        D_MODEL = 256
        N_HEADS = 16
        HEAD_DIM = D_MODEL // N_HEADS
        NEG_BIG = -1e+30
        B, T, _ = q_input.shape
        scale = 1.0 / np.sqrt(HEAD_DIM)
        q = (q_input @ Wq.T + bq).reshape(B, T, N_HEADS, HEAD_DIM).transpose(0, 2, 1, 3)
        k = q_input @ Wk.T + bk
        v = q_input @ Wv.T + bv
        pos = jnp.arange(T)
        mask = pos[None, :] < pos[:, None]
        scores = jnp.einsum('bhtd,bsd->bhts', q, k) * scale
        scores = jnp.where(mask[None, None, :, :], scores, NEG_BIG)
        attn = jax.nn.softmax(scores, axis=-1)
        row_valid = jnp.any(mask, axis=-1)
        attn = attn * row_valid[None, None, :, None].astype(attn.dtype)
        out = jnp.einsum('bhts,bsd->bhtd', attn, v)
        out = out.transpose(0, 2, 1, 3).reshape(B, T, D_MODEL)
        out = out @ Wo.T + bo
        return out

    def _L1_ffn_ref(x, w12, w3, router_w, expert_bias, sw1, sw2, sw3):
        import jax, jax.numpy as jnp
        import numpy as np
        B, S, D = (2, 256, 256)
        E = 8
        TOPK = 2
        H_SHARED = 1024
        H_ROUTED = 128
        STD = 0.02
        b, s, d = x.shape
        g = x @ sw1.T
        u = x @ sw2.T
        shared_out = jax.nn.silu(g) * u @ sw3.T
        scores = jax.nn.sigmoid(x @ router_w.T)
        selection_scores = scores + expert_bias
        _, top_idx = jax.lax.top_k(selection_scores, TOPK)
        top_scores = jnp.take_along_axis(scores, top_idx, axis=-1)
        top_scores = top_scores / (top_scores.sum(-1, keepdims=True) + 1e-09)
        flat_x = x.reshape(-1, d)
        T = flat_x.shape[0]
        flat_idx = top_idx.reshape(T, TOPK)
        flat_sc = top_scores.reshape(T, TOPK)
        combine = jnp.zeros((T, E), x.dtype).at[jnp.arange(T)[:, None], flat_idx].add(flat_sc)
        h12 = jnp.einsum('td,ehd->teh', flat_x, w12)
        h1, h2 = jnp.split(h12, 2, axis=-1)
        h = jax.nn.silu(h1) * h2
        out_e = jnp.einsum('teh,edh->ted', h, w3)
        routed_out = jnp.einsum('ted,te->td', out_e, combine).reshape(b, s, d)
        return shared_out + routed_out
    x = L0_attn_x
    mod = (_silu(L0_c) @ L0_wmod).reshape(L0_c.shape[0], 6, 1, -1)
    sa, ca, ga, sb, cb, gb = (mod[:, 0], mod[:, 1], mod[:, 2], mod[:, 3], mod[:, 4], mod[:, 5])
    ga = (2 * (ga >= 0) - 1) * jnp.maximum(jnp.abs(ga), 0.25)
    gb = (2 * (gb >= 0) - 1) * jnp.maximum(jnp.abs(gb), 0.25)
    h = _layernorm(x, axis=-1) * (1 + ca) + sa
    x = x + ga * _L0_attn_ref(h, L0_attn_w_qkv, L0_attn_w_out)
    h = _layernorm(x, axis=-1) * (1 + cb) + sb
    x = x + gb * _L0_ffn_ref(h, L0_ffn_Wg, L0_ffn_W1, L0_ffn_W3, L0_ffn_W2, L0_ffn_Ws1, L0_ffn_Ws3, L0_ffn_Ws2)
    mod = (_silu(L1_c) @ L1_wmod).reshape(L1_c.shape[0], 6, 1, -1)
    sa, ca, ga, sb, cb, gb = (mod[:, 0], mod[:, 1], mod[:, 2], mod[:, 3], mod[:, 4], mod[:, 5])
    ga = (2 * (ga >= 0) - 1) * jnp.maximum(jnp.abs(ga), 0.25)
    gb = (2 * (gb >= 0) - 1) * jnp.maximum(jnp.abs(gb), 0.25)
    h = _layernorm(x, axis=-1) * (1 + ca) + sa
    x = x + ga * _L1_attn_ref(h, L1_attn_Wq, L1_attn_bq, L1_attn_Wk, L1_attn_bk, L1_attn_Wv, L1_attn_bv, L1_attn_Wo, L1_attn_bo)
    h = _layernorm(x, axis=-1) * (1 + cb) + sb
    x = x + gb * _L1_ffn_ref(h, L1_ffn_w12, L1_ffn_w3, L1_ffn_router_w, L1_ffn_expert_bias, L1_ffn_sw1, L1_ffn_sw2, L1_ffn_sw3)
    return x

_drawn_inputs = setup_inputs


def setup_inputs(seed=0):
    import zlib

    import numpy as np

    out = dict(_drawn_inputs(seed))
    spreads = {'L1_attn_bq': (0.0, 2.0),
     'L1_attn_bk': (0.0, 2.0),
     'L1_attn_bv': (0.0, 0.305),
     'L1_attn_bo': (0.0, 0.332),
     'L1_ffn_expert_bias': (0.0, 0.8)}
    factors = {'L0_attn_w_qkv': 8.0,
     'L0_attn_w_out': 8.0,
     'L0_ffn_Wg': 8.0,
     'L0_ffn_W1': 8.0,
     'L0_ffn_W3': 8.0,
     'L0_ffn_W2': 8.0,
     'L0_ffn_Ws1': 8.0,
     'L0_ffn_Ws3': 8.0,
     'L0_ffn_Ws2': 8.0,
     'L0_c': 8.0,
     'L0_wmod': 8.0,
     'L1_ffn_w12': 8.0,
     'L1_ffn_w3': 8.0,
     'L1_ffn_router_w': 8.0,
     'L1_ffn_sw1': 6.789,
     'L1_ffn_sw2': 6.726,
     'L1_ffn_sw3': 6.714}
    for name, (base, spread) in spreads.items():
        noise = np.random.default_rng([zlib.crc32(name.encode()), seed]).standard_normal(out[name].shape)
        drawn = base * np.exp(spread * noise) if base else spread * noise
        out[name] = jnp.asarray(drawn.astype(out[name].dtype))
    for name, factor in factors.items():
        out[name] = (out[name] * factor).astype(out[name].dtype)
    return out
```

```python
from contextlib import ExitStack

import numpy as np
import concourse.bass as bass
from concourse import mybir

F32 = mybir.dt.float32
F32R = mybir.dt.float32r
I32 = mybir.dt.int32
ACT = mybir.ActivationFunctionType
ALU = mybir.AluOpType
X = mybir.AxisListType.X

P = 128
B, S, D = 2, 512, 256
KC = D // P
NT = S // P
H, DH = 16, 16
UNITS = B * H
WIN = 64
KEYS0 = P + WIN
NEG = -2.0 ** 100
EPS = 1e-5
SCALE = DH ** -0.5
VW = 2 * DH
OC = H * VW // P
ROWS = 4 * DH
ROWSM = ROWS + 2
SLOTS = 4
QUADS = UNITS // SLOTS
BQ = QUADS // B
WIDTH1 = [2 * P, 2 * P, 3 * P, 4 * P]
BANK1 = [(0, 0), (0, 2 * P), (1, 0), (2, 0)]
ORDER1 = [0, 1, 3, 2]
SPAN1 = sum((NT - kb) * P for kb in range(NT))
START1 = {kb: sum((NT - j) * P for j in ORDER1[:i]) for i, kb in enumerate(ORDER1)}
EXPERTS = [16, 8]
INTER = [176, 128]
SHARED = [352, 1024]
TILES = [-(-(EXPERTS[l] * INTER[l] + SHARED[l]) // P) for l in range(2)]
TW = 2 * D + D
SELK = 64
SELW = TW + P
ONES_ROW = 48
CONSTS = 25
RSQRT_MAGIC = float(0x5F3759DF)


def build(nc, io, out):
    ctx = ExitStack()
    with ctx:
        def sb(name, shape, dt=F32):
            return ctx.enter_context(nc.sbuf_tensor(name, shape, dt))

        def sem(name):
            return ctx.enter_context(nc.semaphore(name))

        PS = ctx.enter_context(nc.psum_tensor("PS", [P, 8, 512], F32))
        qk0_scr = nc.dram_tensor("qk0_scr", [UNITS, ROWS, 2, S], F32, kind="Internal").ap()
        q1_scr = nc.dram_tensor("q1_scr", [UNITS, ROWS, S], F32, kind="Internal").ap()
        k1_scr = nc.dram_tensor("k1_scr", [B, 2, DH, S], F32, kind="Internal").ap()
        mx_scr = [nc.dram_tensor(f"mx{l}_scr", [UNITS, 2, S], F32, kind="Internal").ap() for l in range(2)]

        x = sb("x", [P, B, NT, D])
        ident = sb("ident", [P, P])
        identR = sb("identR", [P, P], F32R)
        maskR = sb("maskR", [P, 3 * KEYS0 + 3 * P], F32R)
        mask0 = [maskR[:, KEYS0:2 * KEYS0], maskR[:, 0:KEYS0]]
        mask0T = maskR[:, 2 * KEYS0:3 * KEYS0]
        mask1 = maskR[:, 3 * KEYS0:3 * KEYS0 + 2 * P]
        mask1T = maskR[:, 3 * KEYS0 + 2 * P:]
        zeroR = sb("zeroR", [P, P], F32R)
        tri = sb("tri", [P, 16, 16])
        esel = sb("esel", [P, P + 1])
        ct = sb("ct", [P, 2, KC, B])
        sc = sb("sc", [P, 2, KC, B])
        wmod = [sb(f"wmod{l}", [P, KC, 6 * D]) for l in range(2)]
        modT = sb("modT", [P, 2, 8, B])
        gate = sb("gate", [P, 2, 2, B, D])
        gsign, gabs = (wmod[l][:, :, :].rearrange("p k n -> p (k n)")[:, 0:2 * 2 * B * D] for l in range(2))
        cmpA, cmpB = (wmod[l][:, :, :].rearrange("p k n -> p (k n)")[:, 0:NT * 16 * 16]
                      .rearrange("p (t a b) -> p t a b", a=16, b=16) for l in range(2))
        w_raw = sb("w_raw", [P, KC, 3 * D])
        w_flat = w_raw[:, :, :].rearrange("p k n -> p (k n)").rearrange("p (c n) -> p c n", n=D)
        wqkv = [sb(f"wqkv_{n}", [P, KC, 3 * D], F32R) for n in ("hi", "lo")]
        wout = [[sb(f"wout{l}_{n}", [P, OC, D], F32R) for n in ("hi", "lo")] for l in range(2)]
        wq1 = [sb(f"wq1_{n}", [P, KC, D], F32R) for n in ("hi", "lo")]
        wkv1 = sb("wkv1", [P, KC, 2 * DH])
        wg = [sb(f"wg{l}", [P, KC, EXPERTS[l]]) for l in range(2)]
        bq = sb("bq", [P, KC])
        bqs = sb("bqs", [P, KC])
        bk = sb("bk", [DH, 1])
        bv = sb("bv", [P, DH])
        bo = sb("bo", [P, D])
        ebias = sb("ebias", [P, EXPERTS[1]])
        stats = sb("stats", [P, B, NT, 6])
        mv = sb("mv", [P, B, NT, 2])
        ve = sb("ve", [P, B, NT])
        rs = sb("rs", [P, B, NT])
        nt_ = sb("nt", [P, B, NT])
        xn = sb("xn", [P, NT, D])
        hF = sb("hF", [P, KC, B, S])
        hR = [sb(f"h_{n}", [P, KC, B, S], F32R) for n in ("hi", "lo")]
        qkR = [sb(f"qk_{n}", [P, 4, S], F32R) for n in ("hi", "lo")]
        qF = w_raw[:, :, :].rearrange("p k n -> p (k n)").rearrange("p (m t) -> p m t", t=S)
        qk = [sb(f"qk_slot{s}", [P, 2 * S + WIN], F32R) for s in range(SLOTS)]
        k1 = sb("k1", [P, B, S], F32R)
        V = sb("V", [P, NT, UNITS, DH])
        Vs = [sb(f"V_slot{s}", [P, NT, VW]) for s in range(SLOTS)]
        V1 = sb("V1", [P, NT, B, VW])
        nmx = sb("nmx", [P, UNITS * NT])
        mxT = [sb(f"mxT_{n}", [H * NT, B, P], F32R) for n in ("hi", "lo")]
        pr = [sb(f"pr{s}", [P, SPAN1]) for s in range(2)]
        scb = pr[0][:, 0:2 * KC * B * P].rearrange("p (n q) -> p n q", q=P)
        oF = sb("oF", [P, S])
        oN = sb("oN", [P, S])
        oT = [[w[:, :, :, :].rearrange("p k b t -> p (k b t)").rearrange("p (c t) -> p c t", t=S) for w in hR],
              [w[:, :, :] for w in qkR]]
        mask_raw = pr[1][:, 0:3 * KEYS0 + 3 * P]
        ytmp = xn
        lg = sb("lg", [P, NT, 16])
        ez = sb("ez", [P, NT, 16])
        prob = sb("prob", [P, NT, 16])
        r4 = [sb(f"r4_{i}", [P, NT]) for i in range(2)]
        gs = sb("gs", [P, NT, 4])
        rank = sb("rank", [P, NT, 16])
        masked = sb("masked", [P, NT, 16])
        cR = sb("cR", [P, NT, 16], F32R)
        cparts = sb("cparts", [P, B, NT, SELK])
        cT = sb("cT", [SELK, B, S], F32R)
        fw = [sb(f"fw_raw{s}", [P, SELW]) for s in range(2)]
        fwR = [[wqkv[s][:, :, :].rearrange("p k n -> p (k n)")[:, a * TW:(a + 1) * TW] for a in range(2)] for s in range(2)]
        fsel = [sb(f"fsel{s}", [SELK, P], F32R) for s in range(2)]
        gact = [pr[b][:, 0:S] for b in range(B)]
        gu = [pr[b][:, S:2 * S] for b in range(B)]
        hid = [xn[:, 2 * b:2 * b + 2, :].rearrange("p t d -> p (t d)") for b in range(B)]
        hidR = [[qkR[a][:, b, :] for a in range(2)] for b in range(B)]

        in_names = ["ct", "wmod0", "wmod1", "x0", "x1", "wqkv", "ident", "mask", "tri", "esel", "wout0", "wq1",
                    "wkv1", "wout1", "wg0", "wg1", "bq", "bk", "bv", "bo", "ebias"]
        loaded = {n: sem(f"ld_{n}") for n in in_names}
        consts = sem("consts")
        split = sem("split")
        pool_order = sem("pool_order")
        dve_order = sem("dve_order")
        act_order = sem("act_order")
        sc_done = sem("sc_done")
        scb_done = sem("scb_done")
        mod_ps = sem("mod_ps")
        modT_taken = sem("modT_taken")
        gate_taken = sem("gate_taken")
        xn_ready = sem("xn_ready")
        xt_ready = sem("xt_ready")
        h_ready = sem("h_ready")
        hi_ready = sem("hi_ready")
        hl_ready = sem("hl_ready")
        proj = sem("proj")
        qhi = sem("qhi")
        qlo = sem("qlo")
        v_taken = sem("v_taken")
        v1_taken = sem("v1_taken")
        qF_ready = sem("qF_ready")
        scr0_written = [sem(f"scr0_written{m}") for m in range(4)]
        scr1_written = sem("scr1_written")
        q_cleared = sem("q_cleared")
        k1_loaded = sem("k1_loaded")
        o_first = sem("o_first")
        y_ps = sem("y_ps")
        x_new = sem("x_new")
        lg_ps = sem("lg_ps")
        z_ready = sem("z_ready")
        ez_ready = sem("ez_ready")
        cp_ready = sem("cp_ready")
        cT_ps = sem("cT_ps")
        cT_ready = sem("cT_ready")
        out_written = sem("out_written")
        at = []
        for l in range(2):
            at.append({n: sem(f"at{l}_{n}") for n in (
                "qk0", "qk1", "qk2", "qk3", "s", "mxd", "mt", "mhi", "mlo", "mw0", "mw1", "st", "p", "vs", "o", "oe", "den",
                "rd", "od", "oh", "ol")})
        ff = []
        for l in range(2):
            ff.append({n: sem(f"ff{l}_{n}") for n in (
                "w0", "w1", "hi_w", "split", "g", "u", "c", "silu", "gu", "hid", "hi", "lo", "w2")})

        block = ctx.enter_context(nc.Block())

        @block.sync
        def _(sp):
            def load(name, dst, src):
                sp.dma_start(dst, src).then_inc(loaded[name], 16)

            load("ct", ct[:, :, :, :], io["ct"])
            load("x0", x[:, 0, :, :], io["x"][0:S, :].rearrange("(t p) d -> p t d", p=P))
            load("wmod0", wmod[0][:, :, :], io["wmod0"].rearrange("(k p) n -> p k n", p=P))
            load("ident", ident[:, :], io["ident"])
            load("x1", x[:, 1, :, :], io["x"][S:2 * S, :].rearrange("(t p) d -> p t d", p=P))
            load("wqkv", w_raw[:, :, :], io["wqkv"].rearrange("k p n -> p k n"))
            load("mask", mask_raw, io["mask"])
            load("wmod1", wmod[1][:, :, :], io["wmod1"].rearrange("(k p) n -> p k n", p=P))
            load("tri", tri[:, :, :], io["tri"])
            load("esel", esel[:, :], io["esel"])
            for l in range(2):
                load(f"wg{l}", wg[l][:, :, :], io[f"wg{l}"].rearrange("k p n -> p k n"))
            load("wkv1", wkv1[:, :, :], io["wkv1"].rearrange("k p n -> p k n"))
            load("bq", bq[:, :], io["bq"])
            load("bk", bk[:, :], io["bk"])
            load("bv", bv[:, :], io["bv"].partition_broadcast(P))
            load("bo", bo[:, :], io["bo"].partition_broadcast(P))
            load("ebias", ebias[:, :], io["ebias"].partition_broadcast(P))
            for n, (name, w) in enumerate((("wout0", OC), ("wq1", KC), ("wout1", OC))):
                sp.wait_ge(split, n + 1)
                load(name, w_flat[:, 0:w, :], io[name].rearrange("k p n -> p k n"))

            PLACES = (((0, 3), (1, 2)), ((0, 2), (1, 3)))

            for b in range(B):
                for m in range(4):
                    u = b * H + 8 * (m % 2)
                    for part, done in ((0, qhi), (1, qlo)):
                        sp.wait_ge(done, 4 * b + m + 1)
                        for row in PLACES[m // 2][part]:
                            sp.dma_start(qk0_scr[u:u + 8, row * DH:(row + 1) * DH, m // 2, :],
                                         qkR[part][:, m, :].bitcast(F32)).then_inc(scr0_written[m], 16)

            def load_scores(l, g, s):
                per = (1, 3)[l]
                if not (isinstance(g, int) and g == 0):
                    sp.wait_ge(at[l]["s"], per * (4 * g + s - 3))
                load_rows(l, 4 * g + s, s)

            def load_rows(l, u, s):
                if l == 0:
                    dst = qk[s][0:ROWS, :].bitcast(F32)
                    src = qk0_scr[bass.ds(u, 1), :, :, :].rearrange("u r a t -> (u r) a t")
                    both = bass.AP(dst.tensor, dst.offset, [dst.ap[0], [S + WIN, 2], [1, S]])
                    sp.dma_start(both, src).then_inc(at[l][f"qk{s}"], 16)
                else:
                    sp.dma_start(qk[s][0:ROWS, 0:S].bitcast(F32),
                                 q1_scr[bass.ds(u, 1), :, :].rearrange("u r t -> (u r) t")).then_inc(at[l][f"qk{s}"], 16)

            def load_keys_major(l, g, s):
                per = (1, 2)[l]
                if isinstance(g, int) and g == 0:
                    sp.wait_ge(at[l]["s"], (1, 3)[l] * (UNITS - 3 + s))
                else:
                    sp.wait_ge(at[l]["st"], per * (4 * g + s - 3))
                u = 4 * g + s
                load_rows(l, u, s)
                sp.dma_start(qk[s][ROWS:ROWSM, 0:S].bitcast(F32),
                             mx_scr[l][bass.ds(u, 1), :, :].rearrange("u r t -> (u r) t")).then_inc(at[l][f"qk{s}"], 16)

            def load_attention(l):
                for s in range(SLOTS):
                    load_scores(l, 0, s)
                with sp.Fori(1, BQ) as g:
                    for s in range(SLOTS):
                        load_scores(l, g, s)
                if l == 0:
                    for m in range(4):
                        sp.wait_ge(scr0_written[m], 16 * 4 * B)
                with sp.Fori(BQ, QUADS) as g:
                    for s in range(SLOTS):
                        load_scores(l, g, s)
                sp.wait_ge(at[l]["mw0"], 16 * 2)
                for s in range(SLOTS):
                    load_keys_major(l, 0, s)
                with sp.Fori(1, BQ) as g:
                    for s in range(SLOTS):
                        load_keys_major(l, g, s)
                sp.wait_ge(at[l]["mw1"], 16 * 2)
                with sp.Fori(BQ, QUADS) as g:
                    for s in range(SLOTS):
                        load_keys_major(l, g, s)

            for m in range(4):
                sp.wait_ge(scr0_written[m], 16 * 4)
            load_attention(0)

            def load_ffn(l, p, s, i):
                if not (isinstance(p, int) and p == 0):
                    sp.wait_ge(ff[l]["split"], 2 * p + s - 1)
                sp.dma_start(fw[s][:, :], io[f"ffn{l}"][bass.ds(i, 1), :, :].rearrange("a p n -> (a p) n"))\
                    .then_inc(ff[l][f"w{s}"], 16)

            def load_ffn_all(l):
                for s in range(2):
                    load_ffn(l, 0, s, s)
                with sp.Fori(1, TILES[l] // 2) as p:
                    for s in range(2):
                        load_ffn(l, p, s, 2 * p + s)
                if TILES[l] % 2:
                    load_ffn(l, TILES[l] // 2, 0, TILES[l] - 1)

            load_ffn_all(0)

            for b in range(B):
                for part, done in ((0, qhi), (1, qlo)):
                    sp.wait_ge(done, 4 * B + 3 * b + 3)
                    for c in range(KC):
                        u = b * H + 8 * c
                        for row in PLACES[0][part]:
                            sp.dma_start(q1_scr[u:u + 8, row * DH:(row + 1) * DH, :], qkR[part][:, c, :].bitcast(F32))\
                                .then_inc(scr1_written, 16)
                    sp.dma_start(k1_scr[b, part, :, :], qkR[part][0:DH, 2, :].bitcast(F32)).then_inc(scr1_written, 16)
            sp.wait_ge(scr1_written, 16 * 10 * B)
            for b in range(B):
                for r in range(2):
                    sp.dma_start(k1[32 * r:32 * r + 32, b, :].bitcast(F32),
                                 k1_scr[b, :, :, :].rearrange("l r t -> (l r) t")).then_inc(k1_loaded, 16)
            sp.wait_ge(q_cleared, SLOTS)
            load_attention(1)

            load_ffn_all(1)
            for b in range(B):
                sp.wait_ge(x_new, 3 * B + b + 1)
                sp.dma_start(out[b * S:(b + 1) * S, :].rearrange("(t p) d -> p t d", p=P), x[:, b, :, :])\
                    .then_inc(out_written, 16)
            sp.wait_ge(out_written, 16 * B)

        @block.gpsimd
        def _(pool):
            order = [0]

            def then(ins):
                order[0] += 1
                ins.then_inc(pool_order, 1)
                pool.wait_ge(pool_order, order[0])

            for tile in [cparts[:, :, :, :], V1[:, :, :, :], zeroR[:, :].bitcast(F32), k1[:, :, :].bitcast(F32)] \
                    + [t[:, :].bitcast(F32) for t in qk] + [t[:, :, :] for t in Vs]:
                nc.gpsimd.memset(tile, 0.0).then_inc(consts, 1)
            pool.wait_ge(loaded["ident"], 16)
            nc.gpsimd.tensor_copy(identR[:, :], ident[:, :]).then_inc(consts, 1)
            pool.wait_ge(loaded["mask"], 16)
            nc.gpsimd.tensor_copy(maskR[:, :], mask_raw).then_inc(consts, 1)
            pool.wait_ge(consts, CONSTS - 11)
            for tile in [cparts[:, :, :, ONES_ROW:ONES_ROW + 1], V1[:, :, :, DH:DH + 1]] \
                    + [t[:, :, DH:DH + 1] for t in Vs]:
                nc.gpsimd.memset(tile, 1.0).then_inc(consts, 1)
            for i, rows in enumerate([k1[ROWS:ROWSM, :, :]] + [t[ROWS:ROWSM, S + WIN:] for t in qk]):
                pool.wait_ge(consts, CONSTS - 5 + i)
                nc.gpsimd.memset(rows.bitcast(F32), 1.0).then_inc(consts, 1)
            pool.wait_ge(consts, CONSTS)

            for name, pair, raw in (("wqkv", wqkv, w_raw[:, :, :]), ("wout0", wout[0], w_flat[:, 0:OC, :]),
                                    ("wq1", wq1, w_flat[:, 0:KC, :]), ("wout1", wout[1], w_flat[:, 0:OC, :])):
                pool.wait_ge(loaded[name], 16)
                then(nc.gpsimd.tensor_copy(pair[0][:, :, :], raw))
                nc.gpsimd.tensor_tensor(pair[1][:, :, :], raw, pair[0][:, :, :].bitcast(F32), ALU.subtract)\
                    .then_inc(split, 1)

            def split_tile(l, p, s):
                f = ff[l]
                pool.wait_ge(f[f"w{s}"], 16 * (p + 1))
                if not (isinstance(p, int) and p == 0):
                    pool.wait_ge(f["w2"], 2 * (2 * p + s - 1))
                nc.gpsimd.tensor_tensor(fsel[s][:, :], fw[s][0:SELK, TW:SELW], zeroR[0:SELK, :].bitcast(F32), ALU.add)
                nc.gpsimd.tensor_copy(fwR[s][0], fw[s][:, 0:TW]).then_inc(f["hi_w"], 1)
                pool.wait_ge(f["hi_w"], 2 * p + s + 1)
                nc.gpsimd.tensor_tensor(fwR[s][1], fw[s][:, 0:TW], fwR[s][0].bitcast(F32), ALU.subtract)\
                    .then_inc(f["split"], 1)

            for l in range(2):
                if l == 0:
                    pool.wait_ge(proj, 6 * B)
                else:
                    pool.wait_ge(ff[0]["w2"], 2 * TILES[0])
                for s in range(2):
                    split_tile(l, 0, s)
                with pool.Fori(1, TILES[l] // 2) as p:
                    for s in range(2):
                        split_tile(l, p, s)
                if TILES[l] % 2:
                    split_tile(l, TILES[l] // 2, 0)
                if l == 0:
                    pool.wait_ge(at[0]["st"], UNITS)
                    pool.wait_ge(ff[0]["split"], TILES[0])
                    for s in range(SLOTS):
                        if s:
                            pool.wait_ge(q_cleared, s)
                        nc.gpsimd.memset(qk[s][ROWS:ROWSM, 0:S].bitcast(F32), 0.0).then_inc(q_cleared, 1)
                    pool.wait_ge(q_cleared, SLOTS)

        @block.tensor
        def _(pe):
            def ge(s, value):
                if not (isinstance(value, int) and value <= 0):
                    pe.wait_ge(s, value)

            PASSES = ((0, 0), (0, 1), (1, 0))

            def product(dst, left, right, chunks, **flags):
                n, total = 0, chunks * len(PASSES)
                for c in range(chunks):
                    for a, b in PASSES:
                        ins = nc.tensor.matmul(dst, left(a, c), right(b, c), start=n == 0, stop=n == total - 1)
                        n += 1
                return ins

            pe.wait_ge(sc_done, 1)
            for l in range(2):
                pe.wait_ge(loaded[f"wmod{l}"], 16)
                for j in range(8):
                    col = (0, 1, 3, 4)[j // 2] * D + (j % 2) * P
                    for k in range(KC):
                        ins = nc.tensor.matmul(PS[:, 7, (l * 8 + j) * B:(l * 8 + j + 1) * B],
                                               wmod[l][:, k, col:col + P], sc[:, l, k, :], start=k == 0, stop=k == KC - 1)
                ins.then_inc(mod_ps, 1)
                if l == 0:
                    pe.wait_ge(scb_done, 1)
                for g in range(2):
                    for b in range(B):
                        col = (2, 5)[g] * D
                        for k in range(KC):
                            ins = nc.tensor.matmul(PS[:, 2 * l + g, b * D:(b + 1) * D], scb[:, (l * KC + k) * B + b, :],
                                                   wmod[l][:, k, col:col + D], start=k == 0, stop=k == KC - 1)
                ins.then_inc(mod_ps, 1)

            def norm_transposes(n):
                for b in range(B):
                    pe.wait_ge(xn_ready, 2 * n + b + 1)
                    if n == 0:
                        pe.wait_ge(loaded["ident"], 16)
                        if b == 1:
                            pe.wait_ge(modT_taken, 2)
                    for c in range(KC):
                        for t in range(NT):
                            ins = nc.tensor.transpose(PS[:, 4 + 2 * b + c, t * P:(t + 1) * P],
                                                      xn[:, t, c * P:(c + 1) * P], ident[:, :])
                    ins.then_inc(xt_ready, 1)

            norm_transposes(0)

            for b in range(B):
                pe.wait_ge(hl_ready, 2 * b + 2)
                pe.wait_ge(split, 1)
                for m in range(4):
                    if b == 0:
                        pe.wait_ge(gate_taken, 4)
                    else:
                        pe.wait_ge(qlo, m + 1)
                    product(PS[:, m, :], lambda a, c: wqkv[a][:, c, m * P:(m + 1) * P],
                            lambda a, c: hR[a][:, c, b, :], KC).then_inc(proj, 1)
                for t in range(NT):
                    ins = product(PS[:, 4 + 2 * b + t // 2, (t % 2) * D:(t % 2 + 1) * D],
                                  lambda a, c: hR[a][:, c, b, t * P:(t + 1) * P],
                                  lambda a, c: wqkv[a][:, c, 2 * D:3 * D], KC)
                    if t % 2:
                        ins.then_inc(proj, 1)

            def scores(l, g, s, b):
                a = at[l]
                u = 4 * g + s
                ge(a[f"qk{s}"], 16 * (g + 1))
                if l == 0:
                    ge(a["mxd"], u - 1)
                    for t in range(NT):
                        dst = PS[:, 2 * (s % 2) + t // 2, (t % 2) * KEYS0:(t % 2 + 1) * KEYS0]
                        nc.tensor.matmul(dst, qk[s][:, t * P:(t + 1) * P],
                                         qk[s][:, S + t * P:S + t * P + KEYS0], start=True, stop=False)
                        ins = nc.tensor.matmul(dst, identR[:, :], mask0[t == 0], start=False, stop=True)
                    ins.then_inc(a["s"], 1)
                    return
                ge(a["mxd"], 3 * (u - 1))
                for qt in range(NT):
                    bank, col = BANK1[qt]
                    bank += 3 * (s % 2)
                    diagonal = WIDTH1[qt] - qt * P
                    nc.tensor.matmul(PS[:, bank, col:col + WIDTH1[qt]], qk[s][:, qt * P:(qt + 1) * P],
                                     k1[:, b, 0:WIDTH1[qt]], start=True, stop=True)
                    ins = nc.tensor.matmul(PS[:, bank, col + qt * P:col + WIDTH1[qt]], identR[:, :],
                                           mask1[:, 0:diagonal], start=False, stop=True, skip_group_check=True)
                    if qt:
                        ins.then_inc(a["s"], 1)

            def max_rows(l, b):
                a = at[l]
                pe.wait_ge(a["mxd"], (1, 3)[l] * H * (b + 1))
                if b:
                    pe.wait_ge(a["mlo"], 1)
                nc.tensor.transpose(PS[0:H * NT, 6, 0:P], nmx[:, b * H * NT:(b + 1) * H * NT], ident[:, :])\
                    .then_inc(a["mt"], 1)

            def keys_major(l, g, s, b):
                a = at[l]
                u = 4 * g + s
                ge(a[f"qk{s}"], 16 * QUADS + 32 * (g + 1))
                if l == 0:
                    ge(a["p"], u - 1)
                    for kb in range(NT):
                        dst = PS[:, 2 * (s % 2) + kb // 2, (kb % 2) * KEYS0:(kb % 2 + 1) * KEYS0]
                        nc.tensor.matmul(dst, qk[s][:, S + WIN + kb * P:S + WIN + (kb + 1) * P],
                                         qk[s][:, kb * P:kb * P + KEYS0], start=True, stop=False)
                        ins = nc.tensor.matmul(dst, identR[:, :], mask0T, start=False, stop=True)
                    ins.then_inc(a["st"], 1)
                    return
                for i, kb in enumerate(ORDER1):
                    if i < 2:
                        ge(a["p"], 2 * (u - 2) + i + 1)
                    n = (NT - kb) * P
                    bank, col = 3 * (s % 2) + START1[kb] // S, START1[kb] % S
                    nc.tensor.matmul(PS[:, bank, col:col + n], k1[:, b, kb * P:(kb + 1) * P], qk[s][:, kb * P:S],
                                     start=True, stop=True)
                    ins = nc.tensor.matmul(PS[:, bank, col:col + P], identR[:, :], mask1T, start=False, stop=True,
                                           skip_group_check=True)
                    if i in (0, NT - 1):
                        ins.then_inc(a["st"], 1)

            def values(l, g, s, b):
                a = at[l]
                u = 4 * g + s
                h = s % 2
                if s == 0:
                    ge(a["oe"], g)
                if l == 0:
                    ge(a["vs"], u + 1)
                ge(a["p"], (l + 1) * (u + 1))
                for kb in range(NT):
                    if l == 0:
                        col, n = kb * KEYS0, min(KEYS0, S - kb * P)
                        v = Vs[s][:, kb, :]
                    else:
                        col, n = START1[kb], S - kb * P
                        v = V1[:, kb, b, :]
                    ins = nc.tensor.matmul(PS[s * VW:(s + 1) * VW, 6, kb * P:kb * P + n], v, pr[h][:, col:col + n],
                                           start=kb == 0, stop=kb == NT - 1, skip_group_check=True,
                                           tile_position=(0, s * VW))
                ins.then_inc(a["o"], 1)

            def denominators(l, g):
                a = at[l]
                ge(a["od"], g)
                ge(a["oe"], g + 1)
                nc.tensor.matmul(PS[:, 7, :], esel[:, 0:P], oF[:, :], start=True, stop=True).then_inc(a["den"], 1)

            def attention(l):
                def first(g, b):
                    for s in range(SLOTS):
                        scores(l, g, s, b)

                def second(g, b):
                    for s in range(SLOTS):
                        if s < SLOTS - 1:
                            keys_major(l, g, s + 1, b)
                        elif isinstance(g, int) and g == BQ - 1:
                            keys_major(l, g + 1, 0, 1)
                        elif not (isinstance(g, int) and g == QUADS - 1):
                            keys_major(l, g + 1, 0, b)
                        values(l, g, s, b)
                        if s == 1 and not (isinstance(g, int) and g == 0):
                            denominators(l, g - 1)

                first(0, 0)
                with pe.Fori(1, BQ) as g:
                    first(g, 0)
                first(BQ, 1)
                max_rows(l, 0)
                with pe.Fori(BQ + 1, QUADS) as g:
                    first(g, 1)
                max_rows(l, 1)

                keys_major(l, 0, 0, 0)
                pe.wait_ge(at[l]["mlo"], B)
                second(0, 0)
                with pe.Fori(1, BQ - 1) as g:
                    second(g, 0)
                second(BQ - 1, 0)
                with pe.Fori(BQ, QUADS - 1) as g:
                    second(g, 1)
                second(QUADS - 1, 1)
                denominators(l, QUADS - 1)

            pe.wait_ge(qlo, 4 * B)
            pe.wait_ge(v_taken, 2 * B)
            pe.wait_ge(consts, CONSTS)
            attention(0)

            def out_projection(l):
                pe.wait_ge(split, (2, 4)[l])
                for b in range(B):
                    pe.wait_ge(at[l]["ol"], BQ * (b + 1))
                    for t in range(NT):
                        ins = product(PS[:, 4 + 2 * b + t // 2, (t % 2) * D:(t % 2 + 1) * D],
                                      lambda a, c: oT[b][a][:, c, t * P:(t + 1) * P],
                                      lambda a, c: wout[l][a][:, c, :], OC)
                        if t % 2:
                            ins.then_inc(y_ps, 1)

            def router(l):
                E = EXPERTS[l]
                n = 2 * l + 1
                pe.wait_ge(loaded[f"wg{l}"], 16)
                for b in range(B):
                    pe.wait_ge(h_ready, 2 * (2 * n + b) + 2)
                    for t in range(NT):
                        for c in range(KC):
                            ins = nc.tensor.matmul(PS[:, 2 * b, t * E:(t + 1) * E], hF[:, c, b, t * P:(t + 1) * P],
                                                   wg[l][:, c, :], start=c == 0, stop=c == KC - 1)
                    ins.then_inc(lg_ps, 1)
                for b in range(B):
                    pe.wait_ge(cp_ready, 2 * l + b + 1)
                    for t in range(NT):
                        ins = nc.tensor.transpose(PS[0:SELK, 2 * b + 1, t * P:(t + 1) * P], cparts[:, b, t, :], ident[:, :])
                    ins.then_inc(cT_ps, 1)

            def ffn(l):
                f = ff[l]
                pe.wait_ge(hl_ready, 2 * (2 * (2 * l + 1) + 1) + 2)
                pe.wait_ge(cT_ready, 2 * l + 2)
                for bank in range(4):
                    nc.tensor.matmul(PS[:, bank, :], zeroR[:, :], hR[0][:, 0, 0, :], start=True, stop=True)

                def down(p, s, b):
                    u = 4 * p + 2 * s + b
                    ge(f["lo"], u + 1)
                    for t in range(NT):
                        for i, (a, w) in enumerate(PASSES):
                            ins = nc.tensor.matmul(PS[:, 2 * b + t // 2, (t % 2) * D:(t % 2 + 1) * D],
                                                   hidR[b][a][:, t * P:(t + 1) * P], fwR[s][w][:, 2 * D:],
                                                   start=False, stop=True, skip_group_check=True)
                    ins.then_inc(f["w2"], 1)

                def up(p, s, b):
                    u = 4 * p + 2 * s + b
                    if b == 0:
                        ge(f["split"], 2 * p + s + 1)
                    for i, (name, taken) in enumerate((("g", "silu"), ("u", "gu"))):
                        ge(f[taken], u)
                        product(PS[:, 4 + i, :], lambda a, c: fwR[s][a][:, i * D + c * P:i * D + (c + 1) * P],
                                lambda a, c: hR[a][:, c, b, :], KC).then_inc(f[name], 1)
                    ge(f["hid"], u)
                    nc.tensor.matmul(PS[:, 6, :], fsel[s][:, :], cT[:, b, :], start=True, stop=True).then_inc(f["c"], 1)

                def pair(p):
                    for s in range(2):
                        up(p, s, 0)
                        if s == 1:
                            down(p, 0, 1)
                        elif not (isinstance(p, int) and p == 0):
                            down(p - 1, 1, 1)
                        up(p, s, 1)
                        down(p, s, 0)

                pair(0)
                with pe.Fori(1, TILES[l] // 2) as p:
                    pair(p)
                p = TILES[l] // 2
                if TILES[l] % 2:
                    up(p, 0, 0)
                    down(p - 1, 1, 1)
                    up(p, 0, 1)
                    down(p, 0, 0)
                    down(p, 0, 1)
                else:
                    down(p - 1, 1, 1)

            out_projection(0)
            norm_transposes(1)
            router(0)
            ffn(0)
            norm_transposes(2)

            pe.wait_ge(x_new, 4)
            pe.wait_ge(loaded["wkv1"], 16)
            pe.wait_ge(split, 3)
            for b in range(B):
                pe.wait_ge(hl_ready, 2 * (4 + b) + 2)
                if b:
                    pe.wait_ge(qF_ready, 3)
                    pe.wait_ge(v1_taken, 1)
                for m in range(KC):
                    product(PS[:, m, :], lambda a, c: wq1[a][:, c, m * P:(m + 1) * P],
                            lambda a, c: hR[a][:, c, b, :], KC).then_inc(proj, 1)
                for c in range(KC):
                    ins = nc.tensor.matmul(PS[0:DH, 2, :], wkv1[:, c, 0:DH], hF[:, c, b, :],
                                           start=c == 0, stop=c == KC - 1)
                ins.then_inc(proj, 1)
                for t in range(NT):
                    for c in range(KC):
                        ins = nc.tensor.matmul(PS[:, 3, t * DH:(t + 1) * DH], hF[:, c, b, t * P:(t + 1) * P],
                                               wkv1[:, c, DH:2 * DH], start=c == 0, stop=c == KC - 1)
                ins.then_inc(proj, 1)

            pe.wait_ge(k1_loaded, 16 * 2 * B)
            pe.wait_ge(v1_taken, B)
            attention(1)
            out_projection(1)
            norm_transposes(3)
            router(1)
            ffn(1)

        @block.scalar
        def _(act):
            def ge(s, value):
                if not (isinstance(value, int) and value <= 0):
                    act.wait_ge(s, value)

            act.wait_ge(loaded["ct"], 16)
            nc.scalar.activation(sc[:, :, :, :], ct[:, :, :, :], ACT.Silu).then_inc(sc_done, 1)
            for l in range(2):
                act.wait_ge(mod_ps, 2 * l + 2)
                for g in range(2):
                    nc.scalar.activation(gate[:, l, g, :, :].rearrange("p b d -> p (b d)"), PS[:, 2 * l + g, :],
                                         ACT.Copy, scale=2.0).then_inc(gate_taken, 1)

            def norm_high(n):
                for b in range(B):
                    for c in range(KC):
                        act.wait_ge(h_ready, 2 * (2 * n + b) + c + 1)
                        nc.scalar.activation(hR[0][:, c, b, :], hF[:, c, b, :], ACT.Copy).then_inc(hi_ready, 1)

            norm_high(0)
            for b in range(B):
                for m in range(4):
                    act.wait_ge(proj, 6 * b + m + 1)
                    if b:
                        act.wait_ge(scr0_written[m], 16 * 4)
                    nc.scalar.activation(qkR[0][:, m, :], PS[:, m, :], ACT.Copy, scale=SCALE if m < 2 else 1.0)\
                        .then_inc(qhi, 1)
                for i in range(2):
                    act.wait_ge(proj, 6 * b + 4 + i + 1)
                    act.wait_ge(consts, CONSTS)
                    for j in range(2):
                        ins = nc.scalar.activation(
                            V[:, 2 * i + j, b * H:(b + 1) * H, 0:DH],
                            PS[:, 4 + 2 * b + i, j * D:(j + 1) * D].rearrange("p (h d) -> p h d", d=DH), ACT.Copy)
                    ins.then_inc(v_taken, 1)

            def max_high(l, b):
                a = at[l]
                act.wait_ge(a["mt"], b + 1)
                nc.scalar.activation(mxT[0][:, b, :], PS[0:H * NT, 6, 0:P], ACT.Copy).then_inc(a["mhi"], 1)
                for part, done in ((0, "mhi"), (1, "mlo")):
                    act.wait_ge(a[done], b + 1)
                    act.dma_start(mx_scr[l][b * H:(b + 1) * H, part, :].rearrange("u (t q) -> u t q", q=P),
                                  mxT[part][:, b, :].bitcast(F32)).then_inc(a[f"mw{b}"], 16)

            def exponentials(l, g, s):
                a = at[l]
                u = 4 * g + s
                h = s % 2
                ge(a["o"], u - 1)
                if l == 0:
                    ge(a["st"], u + 1)
                    nc.scalar.activation(
                        pr[h][:, 0:NT * KEYS0].rearrange("p (a k) -> p a k", k=2 * KEYS0),
                        PS[:, 2 * h:2 * h + 2, 0:2 * KEYS0], ACT.Exp)\
                        .then_inc(a["p"], 1)
                    return
                flat = PS[:, 3 * h:3 * h + 3, :].rearrange("p a q -> p (a q)")
                for i, (lo, hi) in enumerate(((0, S), (S, SPAN1))):
                    ge(a["st"], 2 * u + i + 1)
                    nc.scalar.activation(pr[h][:, lo:hi], flat[:, lo:hi], ACT.Exp).then_inc(a["p"], 1)

            def out_high(l, b, g):
                ge(at[l]["od"], g + 1)
                nc.scalar.activation(oT[b][0][:, bass.ds(g - BQ * b, 1), :].rearrange("p c t -> p (c t)"), oN[:, :],
                                     ACT.Copy).then_inc(at[l]["oh"], 1)

            def attention(l):
                def quad(g):
                    for s in range(SLOTS):
                        exponentials(l, g, s)

                for b in range(B):
                    max_high(l, b)
                quad(0)
                for b in range(B):
                    with act.Fori(BQ * b + 1, min(BQ * (b + 1) + 1, QUADS)) as g:
                        quad(g)
                        out_high(l, b, g - 1)
                out_high(l, B - 1, QUADS - 1)

            attention(0)

            def combine(l):
                for b in range(B):
                    act.wait_ge(cT_ps, 2 * l + b + 1)
                    nc.scalar.activation(cT[:, b, :], PS[0:SELK, 2 * b + 1, :], ACT.Copy).then_inc(cT_ready, 1)

            def ffn(l):
                f = ff[l]

                def unit(p, s, b):
                    u = 4 * p + 2 * s + b
                    ge(f["g"], u + 1)
                    ge(f["gu"], u - 1)
                    nc.scalar.activation(gact[b], PS[:, 4, :], ACT.Silu).then_inc(f["silu"], 1)
                    ge(f["hid"], u + 1)
                    ge(f["w2"], u - 1)
                    nc.scalar.activation(hidR[b][0], hid[b], ACT.Copy).then_inc(f["hi"], 1)

                def pair(p):
                    for s in range(2):
                        for b in range(B):
                            unit(p, s, b)

                pair(0)
                with act.Fori(1, TILES[l] // 2) as p:
                    pair(p)
                if TILES[l] % 2:
                    for b in range(B):
                        unit(TILES[l] // 2, 0, b)

            norm_high(1)
            for b in range(B):
                act.wait_ge(z_ready, b + 1)
                nc.scalar.activation(ez[:, :, :], lg[:, :, :], ACT.Exp).then_inc(ez_ready, 1)
            combine(0)
            ffn(0)
            norm_high(2)

            act.wait_ge(loaded["bq"], 16)
            act.wait_ge(loaded["bk"], 16)
            nc.scalar.activation(bqs[:, :], bq[:, :], ACT.Copy, scale=SCALE).then_inc(act_order, 1)
            act.wait_ge(act_order, 1)
            for b in range(B):
                if b:
                    act.wait_ge(qlo, 4 * B + 3)
                    act.wait_ge(scr1_written, 16 * 10)
                for m in range(KC):
                    act.wait_ge(proj, 6 * B + 4 * b + m + 1)
                    nc.scalar.activation(qF[:, m, :], PS[:, m, :], ACT.Identity, bias=bqs[:, m:m + 1], scale=SCALE)\
                        .then_inc(qF_ready, 1)
                act.wait_ge(proj, 6 * B + 4 * b + 3)
                nc.scalar.activation(qF[0:DH, 2, :], PS[0:DH, 2, :], ACT.Identity, bias=bk[:, :]).then_inc(qF_ready, 1)
                for m in range(3):
                    rows = P if m < 2 else DH
                    act.wait_ge(qF_ready, 3 * b + m + 1)
                    nc.scalar.activation(qkR[0][0:rows, m, :], qF[0:rows, m, :], ACT.Copy).then_inc(qhi, 1)

            attention(1)
            norm_high(3)
            for b in range(B):
                act.wait_ge(lg_ps, B + b + 1)
                if b:
                    act.wait_ge(cp_ready, B + 1)
                nc.scalar.activation(ez[:, :, 0:EXPERTS[1]],
                                     PS[:, 2 * b, 0:NT * EXPERTS[1]].rearrange("p (t e) -> p t e", e=EXPERTS[1]),
                                     ACT.Sigmoid).then_inc(ez_ready, 1)
            combine(1)
            ffn(1)

        @block.vector
        def _(dve):
            order = [0]

            def then(ins):
                order[0] += 1
                ins.then_inc(dve_order, 1)
                dve.wait_ge(dve_order, order[0])

            def ge(s, value):
                if not (isinstance(value, int) and value <= 0):
                    dve.wait_ge(s, value)

            tt, ts, stt = nc.vector.tensor_tensor, nc.vector.tensor_scalar, nc.vector.scalar_tensor_tensor

            dve.wait_ge(sc_done, 1)
            nc.vector.tensor_copy(scb[:, :, :], sc[:, :, :, :].rearrange("p l k b -> p (l k b)").unsqueeze(2)
                                  .to_broadcast([P, 2 * KC * B, P]))\
                .then_inc(scb_done, 1)

            def norm(n):
                l = n // 2
                j = 4 * (n % 2)
                for b in range(B):
                    if n == 0:
                        dve.wait_ge(loaded[f"x{b}"], 16)
                    else:
                        dve.wait_ge(x_new, 2 * (n - 1) + b + 1)
                    for t in range(NT):
                        ins = nc.vector.bn_stats(stats[:, b, t, :], x[:, b, t, :])
                    then(ins)
                    for t in range(NT):
                        ins = nc.vector.bn_aggr(mv[:, b, t, :], stats[:, b, t, :])
                    then(ins)
                    v, r, w = ve[:, b, :], rs[:, b, :], nt_[:, b, :]
                    then(ts(v, mv[:, b, :, 1], EPS, None, ALU.add))
                    then(ts(r.bitcast(I32), v.bitcast(I32), 1, None, ALU.logical_shift_right))
                    then(ts(r.bitcast(I32), r.bitcast(I32), -1.0, RSQRT_MAGIC, ALU.mult, ALU.add))
                    for _ in range(4):
                        then(tt(w, r, r, ALU.mult))
                        then(stt(w, w, -0.5, v, ALU.mult, ALU.mult))
                        then(stt(r, w, 1.5, r, ALU.add, ALU.mult))
                    if 2 * n + b:
                        dve.wait_ge(xt_ready, 2 * n + b)
                    for t in range(NT):
                        ins = ts(xn[:, t, :], x[:, b, t, :], mv[:, b, t, 0:1], rs[:, b, t:t + 1], ALU.subtract, ALU.mult)
                    ins.then_inc(xn_ready, 1)
                    if 2 * n + b == 0:
                        modulation()
                    dve.wait_ge(xt_ready, 2 * n + b + 1)
                    for c in range(KC):
                        ts(hF[:, c, b, :], PS[:, 4 + 2 * b + c, :], modT[:, l, j + 2 + c, b:b + 1],
                           modT[:, l, j + c, b:b + 1], ALU.mult, ALU.add).then_inc(h_ready, 1)
                    for c in range(KC):
                        dve.wait_ge(hi_ready, 2 * (2 * n + b) + c + 1)
                        tt(hR[1][:, c, b, :], hF[:, c, b, :], hR[0][:, c, b, :].bitcast(F32), ALU.subtract)\
                            .then_inc(hl_ready, 1)

            def modulation():
                dve.wait_ge(mod_ps, 3)
                then(nc.vector.tensor_copy(modT[:, :, :, :].rearrange("p l j b -> p (l j b)"), PS[:, 7, 0:2 * 8 * B]))
                for i in range(2):
                    scales = modT[:, :, 4 * i + 2:4 * i + 4, :]
                    ts(scales, scales, 1.0, None, ALU.add).then_inc(modT_taken, 1)
                dve.wait_ge(modT_taken, 2)

            norm(0)
            for b in range(B):
                for m in range(4):
                    dve.wait_ge(qhi, 4 * b + m + 1)
                    stt(qkR[1][:, m, :], PS[:, m, :], SCALE if m < 2 else 1.0, qkR[0][:, m, :].bitcast(F32),
                        ALU.mult, ALU.subtract).then_inc(qlo, 1)
            g = gate[:, :, :, :, :].rearrange("p l g b d -> p (l g b d)")
            dve.wait_ge(gate_taken, 4)
            ts(gsign, g, 0.0, 0.5, ALU.is_ge, ALU.subtract)
            then(stt(gabs, g, -1.0, g, ALU.mult, ALU.max))
            then(stt(g, gabs, 0.5, gsign, ALU.max, ALU.mult))

            def maxima(l, g, s):
                a = at[l]
                u = 4 * g + s
                h = s % 2
                if l == 0:
                    ge(a["s"], u + 1)
                    nc.vector.tensor_reduce(
                        nmx[:, bass.ds(NT * u, NT)].rearrange("p (a t) -> p a t", t=2),
                        PS[:, 2 * h:2 * h + 2, 0:2 * KEYS0].rearrange("p a (t k) -> p a t k", k=KEYS0), X, ALU.max,
                        negate=True).then_inc(a["mxd"], 1)
                    return
                for bank, qt, k, w in ((0, 0, 2, 2 * P), (1, 2, 1, 3 * P), (2, 3, 1, 4 * P)):
                    ge(a["s"], 3 * u + bank + 1)
                    nc.vector.tensor_reduce(nmx[:, bass.ds(NT * u + qt, k)],
                                            PS[:, 3 * h + bank, 0:k * w].rearrange("p (t k) -> p t k", k=w),
                                            X, ALU.max, negate=True).then_inc(a["mxd"], 1)

            def max_low(l, b):
                a = at[l]
                dve.wait_ge(a["mhi"], b + 1)
                tt(mxT[1][:, b, :], PS[0:H * NT, 6, 0:P], mxT[0][:, b, :].bitcast(F32), ALU.subtract)\
                    .then_inc(a["mlo"], 1)

            def take_values(g, s):
                a = at[0]
                u = 4 * g + s
                ge(a["o"], u - 3)
                tt(Vs[s][:, :, 0:DH], V[:, :, bass.ds(u, 1), :].rearrange("p t u d -> p t (u d)"),
                   zeroR[:, 0:NT * DH].bitcast(F32).rearrange("p (t d) -> p t d", d=DH), ALU.add).then_inc(a["vs"], 1)

            def take_outputs(l, g):
                a = at[l]
                ge(a["o"], 4 * g + 4)
                nc.vector.tensor_copy(oF[:, l:], PS[:, 6, l:]).then_inc(a["oe"], 1)

            def divide(l, b, g):
                a = at[l]
                ge(a["den"], g + 1)
                nc.vector.reciprocal(oN[:, :], PS[:, 7, :]).then_inc(a["rd"], 1)
                ge(a["rd"], g + 1)
                tt(oN[:, :], oF[:, :], oN[:, :], ALU.mult).then_inc(a["od"], 1)
                ge(a["oh"], g + 1)
                c = bass.ds(g - BQ * b, 1)
                tt(oT[b][1][:, c, :].rearrange("p c t -> p (c t)"), oN[:, :],
                   oT[b][0][:, c, :].rearrange("p c t -> p (c t)").bitcast(F32), ALU.subtract).then_inc(a["ol"], 1)

            def attention(l):
                def first(g):
                    for s in range(SLOTS):
                        maxima(l, g, s)

                def second(b, g):
                    if l == 0:
                        for s in range(SLOTS - 1):
                            take_values(g, s)
                    take_outputs(l, g - 1)
                    if l == 0:
                        take_values(g, SLOTS - 1)
                    divide(l, b, g - 1)

                first(0)
                with dve.Fori(1, BQ) as g:
                    first(g)
                first(BQ)
                max_low(l, 0)
                with dve.Fori(BQ + 1, QUADS) as g:
                    first(g)
                max_low(l, 1)
                if l == 0:
                    dve.wait_ge(consts, CONSTS)
                    dve.wait_ge(v_taken, 2 * B)
                    for s in range(SLOTS):
                        take_values(0, s)
                else:
                    nc.vector.tensor_copy(oF[:, 0:1], esel[:, P:]).then_inc(o_first, 1)
                    dve.wait_ge(o_first, 1)
                for b in range(B):
                    with dve.Fori(BQ * b + 1, min(BQ * (b + 1) + 1, QUADS)) as g:
                        second(b, g)
                take_outputs(l, QUADS - 1)
                divide(l, B - 1, QUADS - 1)

            attention(0)

            def gated(b, l, which, banks, done, count):
                for i in range(2):
                    dve.wait_ge(done, count(i))
                    y = PS[:, banks + i, :].rearrange("p (t d) -> p t d", d=D)
                    tmp = ytmp[:, 2 * i:2 * i + 2, :]
                    if l == 1 and which == 0:
                        dve.wait_ge(loaded["bo"], 16)
                        then(tt(tmp, y, bo[:, :].unsqueeze(1).to_broadcast([P, 2, D]), ALU.add))
                        y = tmp
                    then(tt(tmp, y, gate[:, l, which, b, :].unsqueeze(1).to_broadcast([P, 2, D]), ALU.mult))
                    ins = tt(x[:, b, 2 * i:2 * i + 2, :], x[:, b, 2 * i:2 * i + 2, :], tmp, ALU.add)
                ins.then_inc(x_new, 1)

            def add_attention(l):
                for b in range(B):
                    gated(b, l, 0, 4 + 2 * b, y_ps, lambda i: 4 * l + 2 * b + i + 1)

            def ranks(values, k, m, tril):
                A, Bv = cmpA[:, :, 0:m, 0:m], cmpB[:, :, 0:m, 0:m]
                shape = [P, NT, m, m]
                own = values.unsqueeze(3).to_broadcast(shape)
                other = values.unsqueeze(2).to_broadcast(shape)
                tt(A, other, own, ALU.is_gt)
                then(tt(Bv, other, own, ALU.is_equal))
                then(tt(Bv, Bv, tril[:, 0:m, 0:m].unsqueeze(1).to_broadcast(shape), ALU.mult))
                then(tt(A, A, Bv, ALU.add))
                then(nc.vector.tensor_reduce(rank[:, :, 0:m], A, X, ALU.add))
                then(ts(rank[:, :, 0:m], rank[:, :, 0:m], float(k), None, ALU.is_lt))
                return rank[:, :, 0:m]

            def combine_parts(b, c, E):
                then(nc.vector.tensor_copy(cR[:, :, 0:E], c))
                hi = cR[:, :, 0:E].bitcast(F32)
                nc.vector.tensor_copy(cparts[:, b, :, 0:E], hi)
                tt(cparts[:, b, :, 16:16 + E], c, hi, ALU.subtract).then_inc(cp_ready, 1)

            def router0():
                E, G = EXPERTS[0], 4
                dve.wait_ge(loaded["tri"], 16)
                for b in range(B):
                    dve.wait_ge(lg_ps, b + 1)
                    raw = PS[:, 2 * b, 0:NT * E].rearrange("p (t e) -> p t e", e=E)
                    then(nc.vector.tensor_reduce(r4[0][:, :], raw, X, ALU.max))
                    tt(lg[:, :, :], raw, r4[0][:, :].unsqueeze(2).to_broadcast([P, NT, E]), ALU.subtract)\
                        .then_inc(z_ready, 1)
                    dve.wait_ge(ez_ready, b + 1)
                    then(nc.vector.tensor_reduce(r4[1][:, :], ez[:, :, :], X, ALU.add))
                    then(nc.vector.reciprocal(r4[1][:, :], r4[1][:, :]))
                    then(tt(prob[:, :, :], ez[:, :, :], r4[1][:, :].unsqueeze(2).to_broadcast([P, NT, E]), ALU.mult))
                    then(nc.vector.tensor_reduce(gs[:, :, :], prob[:, :, :].rearrange("p t (g e) -> p t g e", e=E // G),
                                                 X, ALU.max))
                    chosen = ranks(gs[:, :, :], 2, G, tri)
                    spread = chosen.unsqueeze(3).to_broadcast([P, NT, G, E // G])
                    m4 = masked[:, :, :].rearrange("p t (g e) -> p t g e", e=E // G)
                    p4 = prob[:, :, :].rearrange("p t (g e) -> p t g e", e=E // G)
                    then(tt(m4, p4, spread, ALU.mult))
                    then(tt(m4, m4, spread, ALU.add))
                    then(ts(masked[:, :, :], masked[:, :, :], -1.0, None, ALU.add))
                    chosen = ranks(masked[:, :, :], 4, E, tri)
                    then(tt(masked[:, :, :], prob[:, :, :], chosen, ALU.mult))
                    combine_parts(b, masked[:, :, :], E)

            def router1():
                E = EXPERTS[1]
                dve.wait_ge(loaded["ebias"], 16)
                for b in range(B):
                    dve.wait_ge(ez_ready, B + b + 1)
                    s = ez[:, :, 0:E]
                    then(tt(masked[:, :, 0:E], s, ebias[:, :].unsqueeze(1).to_broadcast([P, NT, E]), ALU.add))
                    chosen = ranks(masked[:, :, 0:E], 2, E, tri)
                    then(tt(prob[:, :, 0:E], s, chosen, ALU.mult))
                    then(nc.vector.tensor_reduce(r4[0][:, :], prob[:, :, 0:E], X, ALU.add))
                    then(ts(r4[0][:, :], r4[0][:, :], 1e-9, None, ALU.add))
                    then(nc.vector.reciprocal(r4[0][:, :], r4[0][:, :]))
                    then(tt(masked[:, :, 0:E], prob[:, :, 0:E], r4[0][:, :].unsqueeze(2).to_broadcast([P, NT, E]), ALU.mult))
                    combine_parts(b, masked[:, :, 0:E], E)

            def ffn(l):
                f = ff[l]

                def unit(p, s, b):
                    u = 4 * p + 2 * s + b
                    ge(f["silu"], u + 1)
                    ge(f["u"], u + 1)
                    tt(gu[b], gact[b], PS[:, 5, :], ALU.mult).then_inc(f["gu"], 1)
                    ge(f["gu"], u + 1)
                    ge(f["c"], u + 1)
                    tt(hid[b], gu[b], PS[:, 6, :], ALU.mult).then_inc(f["hid"], 1)
                    ge(f["hi"], u + 1)
                    tt(hidR[b][1], hid[b], hidR[b][0].bitcast(F32), ALU.subtract).then_inc(f["lo"], 1)

                def pair(p):
                    for s in range(2):
                        for b in range(B):
                            unit(p, s, b)

                pair(0)
                with dve.Fori(1, TILES[l] // 2) as p:
                    pair(p)
                if TILES[l] % 2:
                    for b in range(B):
                        unit(TILES[l] // 2, 0, b)
                for b in range(B):
                    gated(b, l, 1, 2 * b, f["w2"], lambda i: 2 * TILES[l])

            add_attention(0)
            norm(1)
            router0()
            ffn(0)
            norm(2)
            dve.wait_ge(loaded["bv"], 16)
            dve.wait_ge(loaded["esel"], 16)
            dve.wait_ge(consts, CONSTS)
            for b in range(B):
                for m in range(3):
                    rows = P if m < 2 else DH
                    dve.wait_ge(qhi, 4 * B + 3 * b + m + 1)
                    tt(qkR[1][0:rows, m, :], qF[0:rows, m, :], qkR[0][0:rows, m, :].bitcast(F32), ALU.subtract)\
                        .then_inc(qlo, 1)
                dve.wait_ge(proj, 6 * B + 4 * b + 4)
                tt(V1[:, :, b, 0:DH], PS[:, 3, 0:NT * DH].rearrange("p (t d) -> p t d", d=DH),
                   bv[:, :].unsqueeze(1).to_broadcast([P, NT, DH]), ALU.add).then_inc(v1_taken, 1)
            attention(1)
            add_attention(1)
            norm(3)
            router1()
            ffn(1)


def shape_tables():
    q = np.arange(P)[:, None]
    c = np.arange(KEYS0)[None, :]
    band = (c >= q) & (c <= q + WIN)
    later = np.where(band, 0.0, NEG)
    first = np.where(band & (c >= WIN), 0.0, NEG)
    causal = np.where(np.arange(P)[None, :] < q, 0.0, NEG)
    bandT = np.where((c >= q) & (c <= q + WIN), 0.0, NEG)
    mask = np.concatenate([first, later, bandT, causal, np.full((P, P), NEG), causal.T], 1).astype(np.float32)
    tri = np.broadcast_to(np.tril(np.ones((16, 16)), -1), (P, 16, 16)).astype(np.float32)
    denominator = (q % VW == DH).astype(np.float32)
    esel = np.concatenate([denominator * (q // VW == np.arange(P)[None, :] // VW), denominator], 1).astype(np.float32)
    sel = []
    for l in range(2):
        s = np.zeros((TILES[l], P, P), np.float32)
        for row in range(EXPERTS[l] * INTER[l] + SHARED[l]):
            e = row // INTER[l]
            for k in ((e, 16 + e) if e < EXPERTS[l] else (ONES_ROW,)):
                s[row // P, k, row % P] = 1.0
        sel.append(s)
    return {"ident": np.eye(P, dtype=np.float32), "mask": mask, "tri": np.ascontiguousarray(tri), "esel": esel}, sel


def chunked_T(w):
    return np.ascontiguousarray(w.T.reshape(KC, P, w.shape[0]))


def by_output_rows(w):
    w = np.pad(w.T.reshape(H, DH, D), ((0, 0), (0, VW - DH), (0, 0)))
    return np.ascontiguousarray(w.reshape(OC, P, D))


def ffn_tiles(w1, w3, w2, sel):
    tiles = sel.shape[0]
    pad = tiles * P - w1.shape[0]
    w1, w3, w2 = (np.pad(w, ((0, pad), (0, 0))).reshape(tiles, P, D) for w in (w1, w3, w2))
    up = [w.transpose(0, 2, 1).reshape(tiles, KC, P, P).transpose(0, 2, 1, 3).reshape(tiles, P, D) for w in (w1, w3)]
    return np.ascontiguousarray(np.concatenate(up + [w2, sel], 2))


def kernel(**inputs):
    import concourse.bacc as bacc
    from concourse.bass_utils import run_bass_kernel_spmd as run

    i = {k: np.asarray(v) for k, v in inputs.items()}
    tables, sel = shape_tables()
    arrays = {
        "x": i["L0_attn_x"].reshape(B * S, D),
        "ct": np.ascontiguousarray(np.stack([i[f"L{l}_c"] for l in range(2)], 0).transpose(2, 0, 1)
                                   .reshape(KC, P, 2, B).transpose(1, 2, 0, 3)),
        "wmod0": i["L0_wmod"], "wmod1": i["L1_wmod"],
        "wqkv": chunked_T(i["L0_attn_w_qkv"]), "wout0": by_output_rows(i["L0_attn_w_out"]),
        "wq1": chunked_T(i["L1_attn_Wq"]),
        "wkv1": chunked_T(np.concatenate([i["L1_attn_Wk"], i["L1_attn_Wv"]], 0)),
        "wout1": by_output_rows(i["L1_attn_Wo"]),
        "wg0": chunked_T(i["L0_ffn_Wg"]), "wg1": chunked_T(i["L1_ffn_router_w"]),
        "bq": np.ascontiguousarray(i["L1_attn_bq"].reshape(KC, P).T), "bk": i["L1_attn_bk"].reshape(DH, 1),
        "bv": i["L1_attn_bv"], "bo": i["L1_attn_bo"], "ebias": i["L1_ffn_expert_bias"],
        "ffn0": ffn_tiles(np.concatenate([i["L0_ffn_W1"].reshape(-1, D), i["L0_ffn_Ws1"]], 0),
                          np.concatenate([i["L0_ffn_W3"].reshape(-1, D), i["L0_ffn_Ws3"]], 0),
                          np.concatenate([i["L0_ffn_W2"].transpose(0, 2, 1).reshape(-1, D), i["L0_ffn_Ws2"].T], 0), sel[0]),
        "ffn1": ffn_tiles(np.concatenate([i["L1_ffn_w12"][:, :INTER[1]].reshape(-1, D), i["L1_ffn_sw1"]], 0),
                          np.concatenate([i["L1_ffn_w12"][:, INTER[1]:].reshape(-1, D), i["L1_ffn_sw2"]], 0),
                          np.concatenate([i["L1_ffn_w3"].transpose(0, 2, 1).reshape(-1, D), i["L1_ffn_sw3"].T], 0), sel[1]),
    }
    arrays.update(tables)
    arrays = {k: np.ascontiguousarray(v) for k, v in arrays.items()}
    nc = bacc.Bacc("TRN2", target_bir_lowering=False, num_devices=1)
    io = {k: nc.dram_tensor(f"in_{k}", v.shape, F32, kind="ExternalInput").ap() for k, v in arrays.items()}
    out = nc.dram_tensor("out", (B * S, D), F32, kind="ExternalOutput").ap()
    build(nc, io, out)
    r = run(nc, [{f"in_{k}": v for k, v in arrays.items()}], core_ids=[0])
    return r.results[0]["out"].reshape(B, S, D)
```

```python
from contextlib import ExitStack

import numpy as np
import concourse.bass as bass
from concourse import mybir

F32 = mybir.dt.float32
F32R = mybir.dt.float32r
I32 = mybir.dt.int32
ACT = mybir.ActivationFunctionType
ALU = mybir.AluOpType
X = mybir.AxisListType.X

P = 128
B, S, D = 2, 512, 256
KC = D // P
NT = S // P
H, DH = 16, 16
UNITS = B * H
WIN = 64
KEYS0 = P + WIN
NEG = -2.0 ** 100
EPS = 1e-5
SCALE = DH ** -0.5
VW = 2 * DH
OC = H * VW // P
ROWS = 4 * DH
ROWSM = ROWS + 2
MAX_BANK = [4, 6]
SLOTS = 4
QUADS = UNITS // SLOTS
BQ = QUADS // B
WIDTH1 = [2 * P, 2 * P, 3 * P, 4 * P]
BANK1 = [(0, 0), (0, 2 * P), (1, 0), (2, 0)]
ORDER1 = [0, 1, 3, 2]
SPAN1 = sum((NT - kb) * P for kb in range(NT))
START1 = {kb: sum((NT - j) * P for j in ORDER1[:i]) for i, kb in enumerate(ORDER1)}
EXPERTS = [16, 8]
INTER = [176, 128]
SHARED = [352, 1024]
TILES = [-(-(EXPERTS[l] * INTER[l] + SHARED[l]) // P) for l in range(2)]
TW = 2 * D + D
SELK = 64
SELW = TW + P
ONES_ROW = 48
EARLY = 2
EU = 2 * EARLY
CONSTS = 27
RSQRT_MAGIC = float(0x5F3759DF)


def build(nc, io, out):
    ctx = ExitStack()
    with ctx:
        def sb(name, shape, dt=F32):
            return ctx.enter_context(nc.sbuf_tensor(name, shape, dt))

        def sem(name):
            return ctx.enter_context(nc.semaphore(name))

        PS = ctx.enter_context(nc.psum_tensor("PS", [P, 8, 512], F32))
        qk0_scr = nc.dram_tensor("qk0_scr", [UNITS, ROWS, 2, S], F32, kind="Internal").ap()
        q1_scr = nc.dram_tensor("q1_scr", [UNITS, ROWS, S], F32, kind="Internal").ap()
        k1_scr = nc.dram_tensor("k1_scr", [B, 2, DH, S], F32, kind="Internal").ap()
        mx_scr = [nc.dram_tensor(f"mx{l}_scr", [UNITS, 2, S], F32, kind="Internal").ap() for l in range(2)]

        x = sb("x", [P, B, NT, D])
        ident = sb("ident", [P, P])
        identR = sb("identR", [P, P], F32R)
        maskR = sb("maskR", [P, 5 * KEYS0 + 3 * P], F32R)
        mask0 = [maskR[:, 0:2 * KEYS0], maskR[:, KEYS0:3 * KEYS0]]
        mask0T = maskR[:, 3 * KEYS0:5 * KEYS0]
        mask1 = maskR[:, 5 * KEYS0:5 * KEYS0 + 2 * P]
        mask1T = maskR[:, 5 * KEYS0 + 2 * P:]
        headmask = sb("headmask", [P, H])
        zeroR = sb("zeroR", [P, P], F32R)
        tri = sb("tri", [P, 16, 16])
        esel = sb("esel", [P, P + 1])
        ct = sb("ct", [P, 2, KC, B])
        sc = sb("sc", [P, 2, KC, B])
        wmod = [sb(f"wmod{l}", [P, KC, 6 * D]) for l in range(2)]
        modT = sb("modT", [P, 2, 8, B])
        gate = sb("gate", [P, 2, 2, B, D])
        gsign, gabs = (wmod[l][:, :, :].rearrange("p k n -> p (k n)")[:, 0:2 * 2 * B * D] for l in range(2))
        cmpA, cmpB = (wmod[l][:, :, :].rearrange("p k n -> p (k n)")[:, 0:B * NT * 16 * 16]
                      .rearrange("p (t a b) -> p t a b", a=16, b=16) for l in range(2))
        w_raw = sb("w_raw", [P, KC, 3 * D])
        w_flat = w_raw[:, :, :].rearrange("p k n -> p (k n)").rearrange("p (c n) -> p c n", n=D)
        wqkv = [sb(f"wqkv_{n}", [P, KC, 3 * D], F32R) for n in ("hi", "lo")]
        wout = [[sb(f"wout{l}_{n}", [P, OC, D], F32R) for n in ("hi", "lo")] for l in range(2)]
        wq1 = [sb(f"wq1_{n}", [P, KC, D], F32R) for n in ("hi", "lo")]
        wkv1 = sb("wkv1", [P, KC, P + DH])
        wg = [sb(f"wg{l}", [P, KC, EXPERTS[l]]) for l in range(2)]
        bq = sb("bq", [P, KC])
        bqs = sb("bqs", [P, KC])
        bk = sb("bk", [P, 1])
        bv = sb("bv", [P, DH])
        bo = sb("bo", [P, D])
        ebias = sb("ebias", [P, EXPERTS[1]])
        stats = sb("stats", [P, B, NT, 6])
        mv = sb("mv", [P, B, NT, 2])
        ve = sb("ve", [P, B, NT])
        rs = sb("rs", [P, B, NT])
        nt_ = sb("nt", [P, B, NT])
        nm = sb("nm", [P, B, NT])
        xn = sb("xn", [P, NT, D])
        hF = sb("hF", [P, KC, B, S])
        hR = [sb(f"h_{n}", [P, KC, B, S], F32R) for n in ("hi", "lo")]
        qkR = [sb(f"qk_{n}", [P, 4, S], F32R) for n in ("hi", "lo")]
        qF = w_raw[:, :, :].rearrange("p k n -> p (k n)").rearrange("p (m t) -> p m t", t=S)
        qk = [sb(f"qk_slot{s}", [P, 2 * S + WIN], F32R) for s in range(SLOTS)]
        k1 = sb("k1", [P, B, S], F32R)
        qm = [sb(f"q_masked{s}", [P, S], F32R) for s in range(SLOTS)]
        V = sb("V", [P, NT, UNITS, DH])
        Vs = [sb(f"V_slot{s}", [P, NT, VW]) for s in range(SLOTS)]
        V1 = sb("V1", [P, NT, B, VW])
        nmx = sb("nmx", [P, UNITS * NT])
        mxT = [sb(f"mxT_{n}", [H * NT, B, P], F32R) for n in ("hi", "lo")]
        pr = [sb(f"pr{s}", [P, SPAN1]) for s in range(2)]
        scb = pr[0][:, 0:2 * KC * B * P].rearrange("p (n q) -> p n q", q=P)
        o_parts = sb("o_parts", [P, 3, S])
        oF, oR, oN = (o_parts[:, i, :] for i in range(3))
        oT = [[w[:, :, :, :].rearrange("p k b t -> p (k b t)").rearrange("p (c t) -> p c t", t=S) for w in hR],
              [w[:, :, :] for w in qkR]]
        mask_raw = pr[1][:, 0:3 * KEYS0 + 3 * P]
        xnb = [xn[:, :, :], o_parts[:, 0:2, :].rearrange("p a t -> p (a t)").rearrange("p (t d) -> p t d", d=D)]
        ytmp = xn
        lg, ez, prob, rank = (oN[:, i * P:(i + 1) * P].rearrange("p (t e) -> p t e", e=16) for i in range(4))
        r4 = [sb(f"r4_{i}", [P, B * NT]) for i in range(2)]
        gs = sb("gs", [P, B * NT, 4])
        masked = sb("masked", [P, B * NT, 16])
        cR = sb("cR", [P, B * NT, 16], F32R)
        cparts = sb("cparts", [P, B, NT, SELK])
        cT = sb("cT", [SELK, B, S], F32R)
        fw = [sb(f"fw_raw{s}", [P, SELW]) for s in range(2)]
        fwR = [[wqkv[s][:, :, :].rearrange("p k n -> p (k n)")[:, a * TW:(a + 1) * TW] for a in range(2)] for s in range(2)]
        fsel = [sb(f"fsel{s}", [SELK, P], F32R) for s in range(2)]
        gact = [pr[b][:, 0:S] for b in range(B)]
        gu = [pr[b][:, S:2 * S] for b in range(B)]
        hid = [xn[:, 2 * b:2 * b + 2, :].rearrange("p t d -> p (t d)") for b in range(B)]
        hidR = [[qkR[a][:, b, :] for a in range(2)] for b in range(B)]

        in_names = ["ct", "wmod0", "wmod1", "x0", "x1", "wqkv", "ident", "mask", "tri", "esel", "headmask", "wout0", "wq1",
                    "wkv1", "wout1", "wg0", "wg1", "bq", "bk", "bv", "bo", "ebias"]
        loaded = {n: sem(f"ld_{n}") for n in in_names}
        consts = sem("consts")
        split = sem("split")
        pool_order = sem("pool_order")
        dve_order = sem("dve_order")
        act_order = sem("act_order")
        sc_done = sem("sc_done")
        scb_done = sem("scb_done")
        mod_ps = sem("mod_ps")
        modT_taken = sem("modT_taken")
        gate_taken = sem("gate_taken")
        rs_ready = sem("rs_ready")
        xn_ready = [sem(f"xn{b}_ready") for b in range(B)]
        xt_ready = sem("xt_ready")
        h_ready = [sem(f"h{b}_ready") for b in range(B)]
        hi_ready = sem("hi_ready")
        hl_ready = sem("hl_ready")
        proj = sem("proj")
        qhi = sem("qhi")
        qlo = sem("qlo")
        v_taken = sem("v_taken")
        v1_taken = sem("v1_taken")
        qF_ready = sem("qF_ready")
        scr0_written = [sem(f"scr0_written{m}") for m in range(4)]
        scr1_written = sem("scr1_written")
        k1_loaded = sem("k1_loaded")
        o_first = sem("o_first")
        y_ps = sem("y_ps")
        x_new = sem("x_new")
        lg_ps = sem("lg_ps")
        z_ready = sem("z_ready")
        ez_ready = sem("ez_ready")
        cp_ready = sem("cp_ready")
        cT_ps = sem("cT_ps")
        cT_ready = sem("cT_ready")
        out_written = sem("out_written")
        at = []
        for l in range(2):
            at.append({n: sem(f"at{l}_{n}") for n in (
                "qk0", "qk1", "qk2", "qk3", "qm", "s", "mxd", "mt", "mhi", "mlo", "mw0", "mw1", "st", "p", "vs", "o", "oe", "den",
                "rd", "od", "oh", "ol")})
        ff = []
        for l in range(2):
            ff.append({n: sem(f"ff{l}_{n}") for n in (
                "w0", "w1", "hi_w", "split", "g", "u", "c", "silu", "gu", "hid", "hi", "lo", "w2",
                "early_u", "early_hid", "early_lo")})

        block = ctx.enter_context(nc.Block())

        @block.sync
        def _(sp):
            def load(name, dst, src):
                sp.dma_start(dst, src).then_inc(loaded[name], 16)

            load("ct", ct[:, :, :, :], io["ct"])
            for b in range(B):
                load(f"x{b}", x[:, b, :, :], io["x"][b * S:(b + 1) * S, :].rearrange("(t p) d -> p t d", p=P))
            load("wmod0", wmod[0][:, :, :], io["wmod0"].rearrange("(k p) n -> p k n", p=P))
            load("ident", ident[:, :], io["ident"])
            load("wqkv", w_raw[:, :, :], io["wqkv"].rearrange("k p n -> p k n"))
            load("mask", mask_raw, io["mask"])
            load("wmod1", wmod[1][:, :, :], io["wmod1"].rearrange("(k p) n -> p k n", p=P))
            load("tri", tri[:, :, :], io["tri"])
            load("headmask", headmask[:, :], io["headmask"])
            load("esel", esel[:, :], io["esel"])
            for l in range(2):
                load(f"wg{l}", wg[l][:, :, :], io[f"wg{l}"].rearrange("k p n -> p k n"))
            load("wkv1", wkv1[:, :, :], io["wkv1"].rearrange("k p n -> p k n"))
            load("bq", bq[:, :], io["bq"])
            load("bk", bk[:, :], io["bk"])
            load("bv", bv[:, :], io["bv"].partition_broadcast(P))
            load("bo", bo[:, :], io["bo"].partition_broadcast(P))
            load("ebias", ebias[:, :], io["ebias"].partition_broadcast(P))
            for n, (name, w) in enumerate((("wout0", OC), ("wq1", KC), ("wout1", OC))):
                sp.wait_ge(split, n + 1)
                load(name, w_flat[:, 0:w, :], io[name].rearrange("k p n -> p k n"))

            PLACES = (((0, 3), (1, 2)), ((0, 2), (1, 3)))

            for b in range(B):
                for m in range(4):
                    u = b * H + 8 * (m % 2)
                    for part, done in ((0, qhi), (1, qlo)):
                        sp.wait_ge(done, 4 * b + m + 1)
                        for row in PLACES[m // 2][part]:
                            sp.dma_start(qk0_scr[u:u + 8, row * DH:(row + 1) * DH, m // 2, :],
                                         qkR[part][:, m, :].bitcast(F32)).then_inc(scr0_written[m], 16)

            def load_rows(l, u, s):
                if l == 0:
                    dst = qk[s][0:ROWS, :].bitcast(F32)
                    src = qk0_scr[bass.ds(u, 1), :, :, :].rearrange("u r a t -> (u r) a t")
                    both = bass.AP(dst.tensor, dst.offset, [dst.ap[0], [S + WIN, 2], [1, S]])
                    sp.dma_start(both, src).then_inc(at[l][f"qk{s}"], 16)
                else:
                    sp.dma_start(qk[s][0:ROWS, 0:S].bitcast(F32),
                                 q1_scr[bass.ds(u, 1), :, :].rearrange("u r t -> (u r) t")).then_inc(at[l][f"qk{s}"], 16)

            def load_keys_major(l, g, s):
                if not (isinstance(g, int) and g == 0):
                    sp.wait_ge(at[l]["st"], (1, 2)[l] * (4 * g + s - 3))
                u = 4 * g + s
                load_rows(l, u, s)
                sp.dma_start(qk[s][ROWS:ROWSM, 0:S].bitcast(F32),
                             mx_scr[l][bass.ds(u, 1), :, :].rearrange("u r t -> (u r) t")).then_inc(at[l][f"qk{s}"], 16)

            def load_attention(l):
                sp.wait_ge(at[l]["mw0"], 16 * 2)
                for s in range(SLOTS):
                    load_keys_major(l, 0, s)
                with sp.Fori(1, BQ) as g:
                    for s in range(SLOTS):
                        load_keys_major(l, g, s)
                sp.wait_ge(at[l]["mw1"], 16 * 2)
                with sp.Fori(BQ, QUADS) as g:
                    for s in range(SLOTS):
                        load_keys_major(l, g, s)

            sp.wait_ge(consts, CONSTS)
            for m in range(4):
                sp.wait_ge(scr0_written[m], 16 * 4 * B)
            load_attention(0)

            def load_ffn(l, p, s, i):
                if not (isinstance(p, int) and p == 0):
                    sp.wait_ge(ff[l]["split"], 2 * p + s - 1)
                sp.dma_start(fw[s][:, :], io[f"ffn{l}"][bass.ds(i, 1), :, :].rearrange("a p n -> (a p) n"))\
                    .then_inc(ff[l][f"w{s}"], 16)

            def load_ffn_all(l):
                for s in range(2):
                    load_ffn(l, 0, s, s)
                with sp.Fori(1, TILES[l] // 2) as p:
                    for s in range(2):
                        load_ffn(l, p, s, 2 * p + s)
                if TILES[l] % 2:
                    load_ffn(l, TILES[l] // 2, 0, TILES[l] - 1)

            load_ffn_all(0)

            for b in range(B):
                for part, done in ((0, qhi), (1, qlo)):
                    sp.wait_ge(done, 4 * B + 3 * b + 3)
                    for c in range(KC):
                        u = b * H + 8 * c
                        for row in PLACES[0][part]:
                            sp.dma_start(q1_scr[u:u + 8, row * DH:(row + 1) * DH, :], qkR[part][:, c, :].bitcast(F32))\
                                .then_inc(scr1_written, 16)
                    sp.dma_start(k1_scr[b, part, :, :], qkR[part][0:DH, 2, :].bitcast(F32)).then_inc(scr1_written, 16)
            sp.wait_ge(scr1_written, 16 * 10 * B)
            for b in range(B):
                for r in range(2):
                    sp.dma_start(k1[32 * r:32 * r + 32, b, :].bitcast(F32),
                                 k1_scr[b, :, :, :].rearrange("l r t -> (l r) t")).then_inc(k1_loaded, 16)
            sp.wait_ge(at[0]["st"], UNITS)
            load_attention(1)

            load_ffn_all(1)
            for b in range(B):
                sp.wait_ge(x_new, 3 * B + b + 1)
                sp.dma_start(out[b * S:(b + 1) * S, :].rearrange("(t p) d -> p t d", p=P), x[:, b, :, :])\
                    .then_inc(out_written, 16)
            sp.wait_ge(out_written, 16 * B)

        @block.gpsimd
        def _(pool):
            order = [0]

            def then(ins):
                order[0] += 1
                ins.then_inc(pool_order, 1)
                pool.wait_ge(pool_order, order[0])

            for tile in [cparts[:, :, :, :], V1[:, :, :, :], zeroR[:, :].bitcast(F32), k1[:, :, :].bitcast(F32)] \
                    + [t[:, :].bitcast(F32) for t in qk] + [t[:, :, :] for t in Vs]:
                nc.gpsimd.memset(tile, 0.0).then_inc(consts, 1)
            pool.wait_ge(loaded["ident"], 16)
            nc.gpsimd.tensor_copy(identR[:, :], ident[:, :]).then_inc(consts, 1)
            pool.wait_ge(loaded["mask"], 16)
            for to, (start, end) in ((0, (0, 2)), (2, (1, 3)), (4, (2, 5))):
                nc.gpsimd.tensor_copy(maskR[:, to * KEYS0:(to + end - start) * KEYS0],
                                      mask_raw[:, start * KEYS0:end * KEYS0]).then_inc(consts, 1)
            pool.wait_ge(consts, CONSTS - 11)
            for tile in [cparts[:, :, :, ONES_ROW:ONES_ROW + 1], V1[:, :, :, DH:DH + 1]] \
                    + [t[:, :, DH:DH + 1] for t in Vs]:
                nc.gpsimd.memset(tile, 1.0).then_inc(consts, 1)
            for i, rows in enumerate([k1[ROWS:ROWSM, :, :]] + [t[ROWS:ROWSM, S + WIN:] for t in qk]):
                pool.wait_ge(consts, CONSTS - 5 + i)
                nc.gpsimd.memset(rows.bitcast(F32), 1.0).then_inc(consts, 1)
            pool.wait_ge(consts, CONSTS)

            for name, pair, raw in (("wqkv", wqkv, w_raw[:, :, :]), ("wout0", wout[0], w_flat[:, 0:OC, :]),
                                    ("wq1", wq1, w_flat[:, 0:KC, :]), ("wout1", wout[1], w_flat[:, 0:OC, :])):
                pool.wait_ge(loaded[name], 16)
                then(nc.gpsimd.tensor_copy(pair[0][:, :, :], raw))
                nc.gpsimd.tensor_tensor(pair[1][:, :, :], raw, pair[0][:, :, :].bitcast(F32), ALU.subtract)\
                    .then_inc(split, 1)

            def ge(s, value):
                if not (isinstance(value, int) and value <= 0):
                    pool.wait_ge(s, value)

            def take_values(g, s):
                u = 4 * g + s
                ge(at[0]["o"], u - 3)
                nc.gpsimd.tensor_tensor(Vs[s][:, :, 0:DH], V[:, :, bass.ds(u, 1), :].rearrange("p t u d -> p t (u d)"),
                                        zeroR[:, 0:NT * DH].bitcast(F32).rearrange("p (t d) -> p t d", d=DH), ALU.add)\
                    .then_inc(at[0]["vs"], 1)

            def out_low(l, b, g):
                ge(at[l]["oh"], g + 1)
                c = bass.ds(g - BQ * b, 1)
                nc.gpsimd.tensor_tensor(oT[b][1][:, c, :].rearrange("p c t -> p (c t)"), oN[:, :],
                                        oT[b][0][:, c, :].rearrange("p c t -> p (c t)").bitcast(F32), ALU.subtract)\
                    .then_inc(at[l]["ol"], 1)

            def attention(l):
                def quad(g, b):
                    if l == 0:
                        for s in range(SLOTS):
                            take_values(g, s)
                    if b is not None:
                        out_low(l, b, g - 2)

                if l == 0:
                    pool.wait_ge(v_taken, 2 * B)
                    quad(0, None)
                    quad(1, None)
                for b, (start, end) in enumerate(((2, BQ + 2), (BQ + 2, QUADS))):
                    with pool.Fori(start, end) as g:
                        quad(g, b)
                out_low(l, B - 1, QUADS - 2)
                out_low(l, B - 1, QUADS - 1)

            def weights_low(l, i, s):
                f = ff[l]
                if isinstance(i, int) and i < 2:
                    pool.wait_ge(f[f"w{s}"], 16)
                    pool.wait_ge(f["hi_w"], i + 1)
                else:
                    pool.wait_ge(f["hi_w"], i + 1)
                nc.gpsimd.tensor_tensor(fsel[s][:, :], fw[s][0:SELK, TW:SELW], zeroR[0:SELK, :].bitcast(F32), ALU.add)
                nc.gpsimd.tensor_tensor(fwR[s][1], fw[s][:, 0:TW], fwR[s][0].bitcast(F32), ALU.subtract)\
                    .then_inc(f["split"], 1)

            def early_unit(l, u, b):
                f = ff[l]
                pool.wait_ge(f["early_u"], u + 1)
                nc.gpsimd.tensor_tensor(hid[b], gact[b], gu[b], ALU.mult).then_inc(f["early_hid"], 1)
                pool.wait_ge(f["hi"], u + 1)
                nc.gpsimd.tensor_tensor(hidR[b][1], hid[b], hidR[b][0].bitcast(F32), ALU.subtract)\
                    .then_inc(f["early_lo"], 1)

            for l in range(2):
                attention(l)
                for i in range(EARLY):
                    weights_low(l, i, i)
                for u in range(EU):
                    early_unit(l, u, u % 2)
                    if u >= EU - 2:
                        weights_low(l, u, u % 2)
                with pool.Fori(EARLY, TILES[l] // 2) as p:
                    for s in range(2):
                        weights_low(l, 2 * p + s, s)
                if TILES[l] % 2:
                    weights_low(l, TILES[l] - 1, 0)
        @block.tensor
        def _(pe):
            def ge(s, value):
                if not (isinstance(value, int) and value <= 0):
                    pe.wait_ge(s, value)

            PASSES = ((0, 0), (0, 1), (1, 0))

            def product(dst, left, right, chunks, **flags):
                n, total = 0, chunks * len(PASSES)
                for c in range(chunks):
                    for a, b in PASSES:
                        ins = nc.tensor.matmul(dst, left(a, c), right(b, c), start=n == 0, stop=n == total - 1)
                        n += 1
                return ins

            def modulation(l):
                pe.wait_ge(loaded[f"wmod{l}"], 16)
                for j in range(8):
                    col = (0, 1, 3, 4)[j // 2] * D + (j % 2) * P
                    for k in range(KC):
                        ins = nc.tensor.matmul(PS[:, 7, (l * 8 + j) * B:(l * 8 + j + 1) * B],
                                               wmod[l][:, k, col:col + P], sc[:, l, k, :], start=k == 0, stop=k == KC - 1)
                ins.then_inc(mod_ps, 1)
                pe.wait_ge(scb_done, 1)
                for g in range(2):
                    for b in range(B):
                        col = (2, 5)[g] * D
                        for k in range(KC):
                            ins = nc.tensor.matmul(PS[:, 2 * l + g, b * D:(b + 1) * D], scb[:, (l * KC + k) * B + b, :],
                                                   wmod[l][:, k, col:col + D], start=k == 0, stop=k == KC - 1)
                ins.then_inc(mod_ps, 1)

            pe.wait_ge(sc_done, 1)
            modulation(0)

            def norm_transposes(n):
                for b in range(B):
                    pe.wait_ge(xn_ready[b], n + 1)
                    if n == 0:
                        pe.wait_ge(loaded["ident"], 16)
                        if b == 1:
                            pe.wait_ge(modT_taken, 2)
                    for c in range(KC):
                        for t in range(NT):
                            ins = nc.tensor.transpose(PS[:, 4 + 2 * b + c, t * P:(t + 1) * P],
                                                      xnb[b][:, t, c * P:(c + 1) * P], ident[:, :])
                    ins.then_inc(xt_ready, 1)

            norm_transposes(0)

            def project0(b):
                pe.wait_ge(hl_ready, 2 * b + 2)
                pe.wait_ge(split, 1)
                if b == 0:
                    pe.wait_ge(gate_taken, 2)
                else:
                    pe.wait_ge(at[0]["mxd"], H)
                for m in range(4):
                    product(PS[:, m, :], lambda a, c: wqkv[a][:, c, m * P:(m + 1) * P],
                            lambda a, c: hR[a][:, c, b, :], KC).then_inc(proj, 1)
                for t in range(NT):
                    ins = product(PS[:, 4 + 2 * b + t // 2, (t % 2) * D:(t % 2 + 1) * D],
                                  lambda a, c: hR[a][:, c, b, t * P:(t + 1) * P],
                                  lambda a, c: wqkv[a][:, c, 2 * D:3 * D], KC)
                    if t % 2:
                        ins.then_inc(proj, 1)

            def project1(b):
                pe.wait_ge(hl_ready, 2 * (4 + b) + 2)
                if b == 0:
                    pe.wait_ge(x_new, 4)
                    pe.wait_ge(loaded["wkv1"], 16)
                    pe.wait_ge(split, 3)
                else:
                    pe.wait_ge(at[1]["mxd"], 3 * H)
                for m in range(KC):
                    product(PS[:, m, :], lambda a, c: wq1[a][:, c, m * P:(m + 1) * P],
                            lambda a, c: hR[a][:, c, b, :], KC).then_inc(proj, 1)
                for c in range(KC):
                    ins = nc.tensor.matmul(PS[:, 2, :], wkv1[:, c, 0:P], hF[:, c, b, :],
                                           start=c == 0, stop=c == KC - 1)
                ins.then_inc(proj, 1)
                for t in range(NT):
                    for c in range(KC):
                        ins = nc.tensor.matmul(PS[:, 3, t * DH:(t + 1) * DH], hF[:, c, b, t * P:(t + 1) * P],
                                               wkv1[:, c, P:], start=c == 0, stop=c == KC - 1)
                ins.then_inc(proj, 1)

            def scores(l, g, s, b):
                a = at[l]
                u = 4 * g + s
                ge(a["qm"], u + 1)
                if l == 0:
                    ge(a["mxd"], u - 1)
                    k = qkR[0][:, bass.ds(2 + (g - BQ * b) // 2, 1), :].rearrange("p m t -> p (m t)")
                    for t in range(NT):
                        bank, col = 2 * (s % 2) + t // 2, (t % 2) * KEYS0
                        if t % 2 == 0:
                            nc.tensor.matmul(PS[:, bank, 0:2 * KEYS0], identR[:, :], mask0[t // 2], start=True, stop=True)
                        before = WIN * (t > 0)
                        ins = nc.tensor.matmul(PS[:, bank, col + WIN - before:col + KEYS0], qm[s][:, t * P:(t + 1) * P],
                                               k[:, t * P - before:(t + 1) * P], start=False, stop=True,
                                               skip_group_check=True)
                    ins.then_inc(a["s"], 1)
                    return
                ge(a["mxd"], 3 * (u - 1))
                for qt in range(NT):
                    bank, col = BANK1[qt]
                    bank += 3 * (s % 2)
                    diagonal = WIDTH1[qt] - qt * P
                    nc.tensor.matmul(PS[:, bank, col:col + WIDTH1[qt]], qm[s][:, qt * P:(qt + 1) * P],
                                     qkR[0][:, 2, 0:WIDTH1[qt]], start=True, stop=True)
                    ins = nc.tensor.matmul(PS[:, bank, col + qt * P:col + WIDTH1[qt]], identR[:, :],
                                           mask1[:, 0:diagonal], start=False, stop=True, skip_group_check=True)
                    if qt:
                        ins.then_inc(a["s"], 1)

            def max_rows(l, b):
                a = at[l]
                pe.wait_ge(a["mxd"], (1, 3)[l] * H * (b + 1))
                if b:
                    pe.wait_ge(a["mlo"], 1)
                nc.tensor.transpose(PS[0:H * NT, MAX_BANK[l], 0:P], nmx[:, b * H * NT:(b + 1) * H * NT], ident[:, :])\
                    .then_inc(a["mt"], 1)

            def maxima_pass(l, b):
                pe.wait_ge(consts, CONSTS)
                if l == 0:
                    pe.wait_ge(qhi, 4 * (b + 1))
                    pe.wait_ge(qlo, 4 * (b + 1))
                    pe.wait_ge(v_taken, 2 * (b + 1))
                else:
                    pe.wait_ge(qhi, 4 * B + 3 * (b + 1))
                    pe.wait_ge(v1_taken, b + 1)
                if b == 0:
                    for s in range(SLOTS):
                        scores(l, 0, s, 0)
                with pe.Fori(BQ * b + (b == 0), BQ * (b + 1)) as g:
                    for s in range(SLOTS):
                        scores(l, g, s, b)
                max_rows(l, b)

            def keys_major(l, g, s, b):
                a = at[l]
                u = 4 * g + s
                ge(a[f"qk{s}"], 32 * (g + 1))
                if l == 0:
                    ge(a["p"], u - 1)
                    for kb in range(NT):
                        bank, col = 2 * (s % 2) + kb // 2, (kb % 2) * KEYS0
                        if kb % 2 == 0:
                            nc.tensor.matmul(PS[:, bank, 0:2 * KEYS0], identR[:, :], mask0T, start=True, stop=True)
                        ins = nc.tensor.matmul(PS[:, bank, col:col + KEYS0], qk[s][:, S + WIN + kb * P:S + WIN + (kb + 1) * P],
                                               qk[s][:, kb * P:kb * P + KEYS0], start=False, stop=True,
                                               skip_group_check=True)
                    ins.then_inc(a["st"], 1)
                    return
                for i, kb in enumerate(ORDER1):
                    if i < 2:
                        ge(a["p"], 2 * (u - 2) + i + 1)
                    n = (NT - kb) * P
                    bank, col = 3 * (s % 2) + START1[kb] // S, START1[kb] % S
                    nc.tensor.matmul(PS[:, bank, col:col + n], k1[:, b, kb * P:(kb + 1) * P], qk[s][:, kb * P:S],
                                     start=True, stop=True)
                    ins = nc.tensor.matmul(PS[:, bank, col:col + P], identR[:, :], mask1T, start=False, stop=True,
                                           skip_group_check=True)
                    if i in (0, NT - 1):
                        ins.then_inc(a["st"], 1)

            def values(l, g, s, b):
                a = at[l]
                u = 4 * g + s
                h = s % 2
                if s == 0:
                    ge(a["oe"], g)
                if l == 0:
                    ge(a["vs"], u + 1)
                ge(a["p"], (l + 1) * (u + 1))
                for kb in range(NT):
                    if l == 0:
                        col, n = kb * KEYS0, min(KEYS0, S - kb * P)
                        v = Vs[s][:, kb, :]
                    else:
                        col, n = START1[kb], S - kb * P
                        v = V1[:, kb, b, :]
                    ins = nc.tensor.matmul(PS[s * VW:(s + 1) * VW, 6, kb * P:kb * P + n], v, pr[h][:, col:col + n],
                                           start=kb == 0, stop=kb == NT - 1, skip_group_check=True,
                                           tile_position=(0, s * VW))
                ins.then_inc(a["o"], 1)

            def denominators(l, g):
                a = at[l]
                ge(a["od"], g)
                ge(a["oe"], g + 1)
                nc.tensor.matmul(PS[:, 7, :], esel[:, 0:P], oF[:, :], start=True, stop=True).then_inc(a["den"], 1)

            def values_pass(l):
                def second(g, b):
                    for s in range(SLOTS):
                        if s < SLOTS - 1:
                            keys_major(l, g, s + 1, b)
                        elif isinstance(g, int) and g == BQ - 1:
                            keys_major(l, g + 1, 0, 1)
                        elif not (isinstance(g, int) and g == QUADS - 1):
                            keys_major(l, g + 1, 0, b)
                        if s == 0 and not (isinstance(g, int) and g == 0):
                            denominators(l, g - 1)
                        values(l, g, s, b)

                keys_major(l, 0, 0, 0)
                pe.wait_ge(at[l]["mlo"], B)
                second(0, 0)
                with pe.Fori(1, BQ - 1) as g:
                    second(g, 0)
                second(BQ - 1, 0)
                with pe.Fori(BQ, QUADS - 1) as g:
                    second(g, 1)
                second(QUADS - 1, 1)
                denominators(l, QUADS - 1)

            for b in range(B):
                project0(b)
                maxima_pass(0, b)
            modulation(1)
            pe.wait_ge(gate_taken, 4)
            pe.wait_ge(modT_taken, 4)
            values_pass(0)

            def out_projection(l):
                pe.wait_ge(split, (2, 4)[l])
                for b in range(B):
                    pe.wait_ge(at[l]["ol"], BQ * (b + 1))
                    for t in range(NT):
                        ins = product(PS[:, 4 + 2 * b + t // 2, (t % 2) * D:(t % 2 + 1) * D],
                                      lambda a, c: oT[b][a][:, c, t * P:(t + 1) * P],
                                      lambda a, c: wout[l][a][:, c, :], OC)
                        if t % 2:
                            ins.then_inc(y_ps, 1)

            def logits(l):
                E = EXPERTS[l]
                pe.wait_ge(loaded[f"wg{l}"], 16)
                for b in range(B):
                    pe.wait_ge(h_ready[b], 2 * (2 * l + 1) + 2)
                for b in range(B):
                    for t in range(NT):
                        for c in range(KC):
                            ins = nc.tensor.matmul(PS[:, 7, (b * NT + t) * E:(b * NT + t + 1) * E],
                                                   hF[:, c, b, t * P:(t + 1) * P], wg[l][:, c, :],
                                                   start=c == 0, stop=c == KC - 1)
                ins.then_inc(lg_ps, 1)

            def combine_transposes(l):
                pe.wait_ge(cp_ready, l + 1)
                for b in range(B):
                    for t in range(NT):
                        ins = nc.tensor.transpose(PS[0:SELK, 6 + b, t * P:(t + 1) * P], cparts[:, b, t, :], ident[:, :])
                    ins.then_inc(cT_ps, 1)

            def ffn(l):
                f = ff[l]
                pe.wait_ge(hl_ready, 2 * (2 * (2 * l + 1) + 1) + 2)
                for bank in range(4):
                    nc.tensor.matmul(PS[:, bank, :], zeroR[:, :], hR[0][:, 0, 0, :], start=True, stop=True)

                def down(p, s, b):
                    u = 4 * p + 2 * s + b
                    if isinstance(u, int) and u < EU:
                        ge(f["early_lo"], u + 1)
                    else:
                        ge(f["lo"], u + 1 - EU)
                    for t in range(NT):
                        for i, (a, w) in enumerate(PASSES):
                            ins = nc.tensor.matmul(PS[:, 2 * b + t // 2, (t % 2) * D:(t % 2 + 1) * D],
                                                   hidR[b][a][:, t * P:(t + 1) * P], fwR[s][w][:, 2 * D:],
                                                   start=False, stop=True, skip_group_check=True)
                    ins.then_inc(f["w2"], 1)

                def up(p, s, b):
                    u = 4 * p + 2 * s + b
                    if b == 0:
                        ge(f["split"], 2 * p + s + 1)
                    for i, name in enumerate("gu"):
                        if i == 0:
                            ge(f["silu"], u)
                        elif isinstance(u, int) and u <= EU:
                            ge(f["early_u"], u)
                        else:
                            ge(f["gu"], u - EU)
                        product(PS[:, 4 + i, :], lambda a, c: fwR[s][a][:, i * D + c * P:i * D + (c + 1) * P],
                                lambda a, c: hR[a][:, c, b, :], KC).then_inc(f[name], 1)
                    if isinstance(u, int) and u < EU:
                        return
                    ge(f["hid"], u - EU)
                    nc.tensor.matmul(PS[:, 6, :], fsel[s][:, :], cT[:, b, :], start=True, stop=True).then_inc(f["c"], 1)

                def pair(p):
                    for s in range(2):
                        up(p, s, 0)
                        if s == 1:
                            down(p, 0, 1)
                        elif not (isinstance(p, int) and p == 0):
                            down(p - 1, 1, 1)
                        up(p, s, 1)
                        down(p, s, 0)

                pair(0)
                combine_transposes(l)
                pe.wait_ge(cT_ready, 2 * l + 2)
                pair(1)
                with pe.Fori(2, TILES[l] // 2) as p:
                    pair(p)
                p = TILES[l] // 2
                if TILES[l] % 2:
                    up(p, 0, 0)
                    down(p - 1, 1, 1)
                    up(p, 0, 1)
                    down(p, 0, 0)
                    down(p, 0, 1)
                else:
                    down(p - 1, 1, 1)

            out_projection(0)
            norm_transposes(1)
            logits(0)
            ffn(0)
            norm_transposes(2)

            for b in range(B):
                project1(b)
                maxima_pass(1, b)
            pe.wait_ge(k1_loaded, 16 * 2 * B)
            values_pass(1)
            out_projection(1)
            norm_transposes(3)
            logits(1)
            ffn(1)

        @block.scalar
        def _(act):
            def ge(s, value):
                if not (isinstance(value, int) and value <= 0):
                    act.wait_ge(s, value)

            act.wait_ge(loaded["ct"], 16)
            nc.scalar.activation(sc[:, :, :, :], ct[:, :, :, :], ACT.Silu).then_inc(sc_done, 1)

            def gates(l):
                act.wait_ge(mod_ps, 2 * l + 2)
                for g in range(2):
                    nc.scalar.activation(gate[:, l, g, :, :].rearrange("p b d -> p (b d)"), PS[:, 2 * l + g, :],
                                         ACT.Copy, scale=2.0).then_inc(gate_taken, 1)

            def norm(n):
                l, j = n // 2, 4 * (n % 2)
                act.wait_ge(rs_ready, n + 1)
                for t in range(NT):
                    ins = nc.scalar.activation(xnb[1][:, t, :], x[:, 1, t, :], ACT.Identity, bias=nm[:, 1, t:t + 1],
                                               scale=rs[:, 1, t:t + 1])
                ins.then_inc(xn_ready[1], 1)
                for b in range(B):
                    if b:
                        act.wait_ge(xt_ready, 2 * n + 2)
                        act.wait_ge(modT_taken, 2 * l + 2)
                        for c in range(KC):
                            nc.scalar.activation(hF[:, c, 1, :], PS[:, 6 + c, :], ACT.Identity,
                                                 bias=modT[:, l, j + c, 1:2], scale=modT[:, l, j + 2 + c, 1:2])\
                                .then_inc(h_ready[1], 1)
                    for c in range(KC):
                        act.wait_ge(h_ready[b], 2 * n + c + 1)
                        nc.scalar.activation(hR[0][:, c, b, :], hF[:, c, b, :], ACT.Copy).then_inc(hi_ready, 1)

            gates(0)
            norm(0)

            def mask_q(l, b, g, s):
                a = at[l]
                u = 4 * g + s
                ge(a["s"], (1, 3)[l] * (u - 3))
                head = g - BQ * b
                nc.scalar.activation(qm[s][:, :], qkR[0][:, bass.ds(head // 2, 1), :].rearrange("p m t -> p (m t)").bitcast(F32),
                                     ACT.Copy, scale=headmask[:, bass.ds(4 * head + s, 1)]).then_inc(a["qm"], 1)

            def mask_first(l, b):
                act.wait_ge(qhi, (0, 4 * B)[l] + (4, 3)[l] * b + 2)
                act.wait_ge(loaded["headmask"], 16)
                for s in range(SLOTS):
                    mask_q(l, b, BQ * b, s)

            def mask_rest(l, b):
                with act.Fori(BQ * b + 1, BQ * (b + 1)) as g:
                    for s in range(SLOTS):
                        mask_q(l, b, g, s)

            def max_high(l, b):
                a = at[l]
                act.wait_ge(a["mt"], b + 1)
                nc.scalar.activation(mxT[0][:, b, :], PS[0:H * NT, MAX_BANK[l], 0:P], ACT.Copy).then_inc(a["mhi"], 1)
                for part, done in ((0, "mhi"), (1, "mlo")):
                    act.wait_ge(a[done], b + 1)
                    act.dma_start(mx_scr[l][b * H:(b + 1) * H, part, :].rearrange("u (t q) -> u t q", q=P),
                                  mxT[part][:, b, :].bitcast(F32)).then_inc(a[f"mw{b}"], 16)

            for b in range(B):
                for m in range(4):
                    act.wait_ge(proj, 6 * b + m + 1)
                    if b:
                        act.wait_ge(scr0_written[m], 16 * 4)
                        act.wait_ge(at[0]["s"], H)
                    nc.scalar.activation(qkR[0][:, m, :], PS[:, m, :], ACT.Copy, scale=SCALE if m < 2 else 1.0)\
                        .then_inc(qhi, 1)
                mask_first(0, b)
                for i in range(2):
                    act.wait_ge(proj, 6 * b + 4 + i + 1)
                    for j in range(2):
                        ins = nc.scalar.activation(
                            V[:, 2 * i + j, b * H:(b + 1) * H, 0:DH],
                            PS[:, 4 + 2 * b + i, j * D:(j + 1) * D].rearrange("p (h d) -> p h d", d=DH), ACT.Copy)
                    ins.then_inc(v_taken, 1)
                mask_rest(0, b)
                max_high(0, b)
            gates(1)

            def exponentials(l, g, s):
                a = at[l]
                u = 4 * g + s
                h = s % 2
                ge(a["o"], u - 1)
                if l == 0:
                    ge(a["st"], u + 1)
                    nc.scalar.activation(
                        pr[h][:, 0:NT * KEYS0].rearrange("p (a k) -> p a k", k=2 * KEYS0),
                        PS[:, 2 * h:2 * h + 2, 0:2 * KEYS0], ACT.Exp)\
                        .then_inc(a["p"], 1)
                    return
                flat = PS[:, 3 * h:3 * h + 3, :].rearrange("p a q -> p (a q)")
                for i, (lo, hi) in enumerate(((0, S), (S, SPAN1))):
                    ge(a["st"], 2 * u + i + 1)
                    nc.scalar.activation(pr[h][:, lo:hi], flat[:, lo:hi], ACT.Exp).then_inc(a["p"], 1)

            def out_high(l, b, g):
                ge(at[l]["od"], g + 1)
                nc.scalar.activation(oT[b][0][:, bass.ds(g - BQ * b, 1), :].rearrange("p c t -> p (c t)"), oN[:, :],
                                     ACT.Copy).then_inc(at[l]["oh"], 1)

            def attention(l):
                def quad(g, b):
                    for s in range(SLOTS):
                        exponentials(l, g, s)
                        if s == 0 and b is not None:
                            out_high(l, b, g - 2)

                quad(0, None)
                quad(1, None)
                for b, (start, end) in enumerate(((2, BQ + 2), (BQ + 2, QUADS))):
                    with act.Fori(start, end) as g:
                        quad(g, b)
                out_high(l, B - 1, QUADS - 2)
                out_high(l, B - 1, QUADS - 1)

            attention(0)

            def combine(l):
                for b in range(B):
                    act.wait_ge(cT_ps, 2 * l + b + 1)
                    nc.scalar.activation(cT[:, b, :], PS[0:SELK, 6 + b, :], ACT.Copy).then_inc(cT_ready, 1)

            def weights_high(l, p, s):
                f = ff[l]
                i = 2 * p + s
                ge(f[f"w{s}"], 16 * (p + 1))
                if isinstance(i, int) and i < 2:
                    if l:
                        act.wait_ge(ff[0]["w2"], 2 * TILES[0])
                else:
                    ge(f["w2"], 2 * (i - 1))
                nc.scalar.activation(fwR[s][0], fw[s][:, 0:TW], ACT.Copy).then_inc(f["hi_w"], 1)

            def ffn(l):
                f = ff[l]

                def silu(u, b):
                    ge(f["g"], u + 1)
                    nc.scalar.activation(gact[b], PS[:, 4, :], ACT.Silu).then_inc(f["silu"], 1)

                def high(u, b):
                    ge(f["w2"], u - 1)
                    nc.scalar.activation(hidR[b][0], hid[b], ACT.Copy).then_inc(f["hi"], 1)

                def early_unit(u, b):
                    ge(f["early_hid"], u - 1)
                    silu(u, b)
                    ge(f["u"], u + 1)
                    nc.scalar.activation(gu[b], PS[:, 5, :], ACT.Copy).then_inc(f["early_u"], 1)
                    ge(f["early_hid"], u + 1)
                    high(u, b)

                def unit(u, b):
                    if isinstance(u, int) and u < EU + B:
                        ge(f["early_hid"], u - 1)
                    else:
                        ge(f["gu"], u - 1 - EU)
                    silu(u, b)
                    ge(f["hid"], u + 1 - EU)
                    high(u, b)

                def pair(p, one, following):
                    for s in range(2):
                        for b in range(B):
                            one(4 * p + 2 * s + b, b)
                            if b == 0 and (one is unit or s == 1) and (s == 0 or following):
                                weights_high(l, p + s, 1 - s)

                pair(0, early_unit, True)
                combine(l)
                pairs = TILES[l] // 2
                pair(1, unit, True)
                with act.Fori(2, pairs - 1) as p:
                    pair(p, unit, True)
                pair(pairs - 1, unit, TILES[l] % 2)
                if TILES[l] % 2:
                    for b in range(B):
                        unit(4 * pairs + b, b)

            for i in range(2):
                weights_high(0, 0, i)
            norm(1)
            act.wait_ge(z_ready, 1)
            nc.scalar.activation(ez[:, :, :], lg[:, :, :], ACT.Exp).then_inc(ez_ready, 1)
            ffn(0)
            norm(2)

            act.wait_ge(loaded["bq"], 16)
            act.wait_ge(loaded["bk"], 16)
            nc.scalar.activation(bqs[:, :], bq[:, :], ACT.Copy, scale=SCALE).then_inc(act_order, 1)
            act.wait_ge(act_order, 1)
            for b in range(B):
                if b:
                    act.wait_ge(qlo, 4 * B + 3)
                    act.wait_ge(scr1_written, 16 * 10)
                    act.wait_ge(at[1]["s"], 3 * H)
                for m in range(KC):
                    act.wait_ge(proj, 6 * B + 4 * b + m + 1)
                    nc.scalar.activation(qF[:, m, :], PS[:, m, :], ACT.Identity, bias=bqs[:, m:m + 1], scale=SCALE)\
                        .then_inc(qF_ready, 1)
                act.wait_ge(proj, 6 * B + 4 * b + 3)
                nc.scalar.activation(qF[:, 2, :], PS[:, 2, :], ACT.Identity, bias=bk[:, :]).then_inc(qF_ready, 1)
                for m in range(3):
                    act.wait_ge(qF_ready, 3 * b + m + 1)
                    nc.scalar.activation(qkR[0][:, m, :], qF[:, m, :], ACT.Copy).then_inc(qhi, 1)
                mask_first(1, b)
                mask_rest(1, b)
                max_high(1, b)

            attention(1)
            for i in range(2):
                weights_high(1, 0, i)
            norm(3)
            act.wait_ge(lg_ps, 2)
            nc.scalar.activation(ez[:, :, 0:EXPERTS[1]],
                                 PS[:, 7, 0:B * NT * EXPERTS[1]].rearrange("p (t e) -> p t e", e=EXPERTS[1]),
                                 ACT.Sigmoid).then_inc(ez_ready, 1)
            ffn(1)

        @block.vector
        def _(dve):
            order = [0]

            def then(ins):
                order[0] += 1
                ins.then_inc(dve_order, 1)
                dve.wait_ge(dve_order, order[0])

            def ge(s, value):
                if not (isinstance(value, int) and value <= 0):
                    dve.wait_ge(s, value)

            tt, ts, stt = nc.vector.tensor_tensor, nc.vector.tensor_scalar, nc.vector.scalar_tensor_tensor

            dve.wait_ge(sc_done, 1)
            nc.vector.tensor_copy(scb[:, :, :], sc[:, :, :, :].rearrange("p l k b -> p (l k b)").unsqueeze(2)
                                  .to_broadcast([P, 2 * KC * B, P]))\
                .then_inc(scb_done, 1)

            def norm(n):
                l, j = n // 2, 4 * (n % 2)
                for b in range(B):
                    if n == 0:
                        dve.wait_ge(loaded[f"x{b}"], 16)
                    else:
                        dve.wait_ge(x_new, 2 * (n - 1) + b + 1)
                    for t in range(NT):
                        ins = nc.vector.bn_stats(stats[:, b, t, :], x[:, b, t, :])
                then(ins)
                for b in range(B):
                    for t in range(NT):
                        ins = nc.vector.bn_aggr(mv[:, b, t, :], stats[:, b, t, :])
                then(ins)
                v, r, w = ve[:, :, :], rs[:, :, :], nt_[:, :, :]
                then(ts(v, mv[:, :, :, 1], EPS, None, ALU.add))
                then(ts(r.bitcast(I32), v.bitcast(I32), 1, None, ALU.logical_shift_right))
                then(ts(r.bitcast(I32), r.bitcast(I32), -1.0, RSQRT_MAGIC, ALU.mult, ALU.add))
                for _ in range(3):
                    then(tt(w, r, r, ALU.mult))
                    then(stt(w, w, -0.5, v, ALU.mult, ALU.mult))
                    then(stt(r, w, 1.5, r, ALU.add, ALU.mult))
                stt(nm[:, :, :], mv[:, :, :, 0], -1.0, r, ALU.mult, ALU.mult).then_inc(rs_ready, 1)
                for t in range(NT):
                    ins = ts(xnb[0][:, t, :], x[:, 0, t, :], mv[:, 0, t, 0:1], rs[:, 0, t:t + 1], ALU.subtract, ALU.mult)
                ins.then_inc(xn_ready[0], 1)
                if n == 0:
                    modulation(0)
                dve.wait_ge(xt_ready, 2 * n + 1)
                for c in range(KC):
                    ts(hF[:, c, 0, :], PS[:, 4 + c, :], modT[:, l, j + 2 + c, 0:1], modT[:, l, j + c, 0:1],
                       ALU.mult, ALU.add).then_inc(h_ready[0], 1)
                for b in range(B):
                    for c in range(KC):
                        dve.wait_ge(hi_ready, 2 * (2 * n + b) + c + 1)
                        tt(hR[1][:, c, b, :], hF[:, c, b, :], hR[0][:, c, b, :].bitcast(F32), ALU.subtract)\
                            .then_inc(hl_ready, 1)

            def modulation(l):
                dve.wait_ge(mod_ps, 2 * l + 1)
                then(nc.vector.tensor_copy(modT[:, l, :, :].rearrange("p j b -> p (j b)"),
                                           PS[:, 7, l * 8 * B:(l + 1) * 8 * B]))
                for i in range(2):
                    scales = modT[:, l, 4 * i + 2:4 * i + 4, :]
                    ts(scales, scales, 1.0, None, ALU.add).then_inc(modT_taken, 1)
                dve.wait_ge(modT_taken, 2 * l + 2)

            norm(0)

            def maxima(l, g, s):
                a = at[l]
                u = 4 * g + s
                h = s % 2
                if l == 0:
                    ge(a["s"], u + 1)
                    nc.vector.tensor_reduce(
                        nmx[:, bass.ds(NT * u, NT)].rearrange("p (a t) -> p a t", t=2),
                        PS[:, 2 * h:2 * h + 2, 0:2 * KEYS0].rearrange("p a (t k) -> p a t k", k=KEYS0), X, ALU.max,
                        negate=True).then_inc(a["mxd"], 1)
                    return
                for bank, qt, k, w in ((0, 0, 2, 2 * P), (1, 2, 1, 3 * P), (2, 3, 1, 4 * P)):
                    ge(a["s"], 3 * u + bank + 1)
                    nc.vector.tensor_reduce(nmx[:, bass.ds(NT * u + qt, k)],
                                            PS[:, 3 * h + bank, 0:k * w].rearrange("p (t k) -> p t k", k=w),
                                            X, ALU.max, negate=True).then_inc(a["mxd"], 1)

            def max_low(l, b):
                a = at[l]
                dve.wait_ge(a["mhi"], b + 1)
                tt(mxT[1][:, b, :], PS[0:H * NT, MAX_BANK[l], 0:P], mxT[0][:, b, :].bitcast(F32), ALU.subtract)\
                    .then_inc(a["mlo"], 1)

            def take_outputs(l, g):
                a = at[l]
                ge(a["od"], g)
                ge(a["o"], 4 * g + 4)
                nc.vector.tensor_copy(oF[:, l:], PS[:, 6, l:]).then_inc(a["oe"], 1)

            def divide(l, g):
                a = at[l]
                ge(a["den"], g + 1)
                nc.vector.reciprocal(oR[:, :], PS[:, 7, :]).then_inc(a["rd"], 1)
                ge(a["rd"], g + 1)
                ge(a["ol"], g)
                tt(oN[:, :], oF[:, :], oR[:, :], ALU.mult).then_inc(a["od"], 1)

            def maxima_pass(l, b):
                if b == 0:
                    for s in range(SLOTS):
                        maxima(l, 0, s)
                with dve.Fori(BQ * b + (b == 0), BQ * (b + 1)) as g:
                    for s in range(SLOTS):
                        maxima(l, g, s)
                max_low(l, b)

            def outputs_pass(l):
                if l:
                    nc.vector.tensor_copy(oF[:, 0:1], esel[:, P:]).then_inc(o_first, 1)
                    dve.wait_ge(o_first, 1)
                take_outputs(l, 0)
                divide(l, 0)
                with dve.Fori(1, QUADS) as g:
                    take_outputs(l, g)
                    divide(l, g)

            for b in range(B):
                for m in range(4):
                    dve.wait_ge(qhi, 4 * b + m + 1)
                    stt(qkR[1][:, m, :], PS[:, m, :], SCALE if m < 2 else 1.0, qkR[0][:, m, :].bitcast(F32),
                        ALU.mult, ALU.subtract).then_inc(qlo, 1)
                maxima_pass(0, b)
            modulation(1)
            g = gate[:, :, :, :, :].rearrange("p l g b d -> p (l g b d)")
            dve.wait_ge(gate_taken, 4)
            ts(gsign, g, 0.0, 0.5, ALU.is_ge, ALU.subtract)
            then(stt(gabs, g, -1.0, g, ALU.mult, ALU.max))
            then(stt(g, gabs, 0.5, gsign, ALU.max, ALU.mult))
            outputs_pass(0)

            def gated(b, l, which, banks, done, count):
                for i in range(2):
                    dve.wait_ge(done, count(i))
                    y = PS[:, banks + i, :].rearrange("p (t d) -> p t d", d=D)
                    tmp = ytmp[:, 2 * i:2 * i + 2, :]
                    if l == 1 and which == 0:
                        dve.wait_ge(loaded["bo"], 16)
                        then(tt(tmp, y, bo[:, :].unsqueeze(1).to_broadcast([P, 2, D]), ALU.add))
                        y = tmp
                    then(tt(tmp, y, gate[:, l, which, b, :].unsqueeze(1).to_broadcast([P, 2, D]), ALU.mult))
                    ins = tt(x[:, b, 2 * i:2 * i + 2, :], x[:, b, 2 * i:2 * i + 2, :], tmp, ALU.add)
                ins.then_inc(x_new, 1)

            def add_attention(l):
                for b in range(B):
                    gated(b, l, 0, 4 + 2 * b, y_ps, lambda i: 4 * l + 2 * b + i + 1)

            def ranks(values, k, m, tril):
                A, Bv = cmpA[:, :, 0:m, 0:m], cmpB[:, :, 0:m, 0:m]
                shape = [P, B * NT, m, m]
                own = values.unsqueeze(3).to_broadcast(shape)
                other = values.unsqueeze(2).to_broadcast(shape)
                tt(A, other, own, ALU.is_gt)
                then(tt(Bv, other, own, ALU.is_equal))
                then(tt(Bv, Bv, tril[:, 0:m, 0:m].unsqueeze(1).to_broadcast(shape), ALU.mult))
                then(tt(A, A, Bv, ALU.add))
                then(nc.vector.tensor_reduce(rank[:, :, 0:m], A, X, ALU.add))
                then(ts(rank[:, :, 0:m], rank[:, :, 0:m], float(k), None, ALU.is_lt))
                return rank[:, :, 0:m]

            def combine_parts(c, E):
                rows = cparts[:, :, :, :].rearrange("p b t k -> p (b t) k")
                then(nc.vector.tensor_copy(cR[:, :, 0:E], c))
                hi = cR[:, :, 0:E].bitcast(F32)
                nc.vector.tensor_copy(rows[:, :, 0:E], hi)
                tt(rows[:, :, 16:16 + E], c, hi, ALU.subtract).then_inc(cp_ready, 1)

            def router0():
                E, G, T = EXPERTS[0], 4, B * NT
                dve.wait_ge(loaded["tri"], 16)
                dve.wait_ge(lg_ps, 1)
                raw = PS[:, 7, 0:T * E].rearrange("p (t e) -> p t e", e=E)
                then(nc.vector.tensor_reduce(r4[0][:, :], raw, X, ALU.max))
                tt(lg[:, :, :], raw, r4[0][:, :].unsqueeze(2).to_broadcast([P, T, E]), ALU.subtract).then_inc(z_ready, 1)
                dve.wait_ge(ez_ready, 1)
                then(nc.vector.tensor_reduce(r4[1][:, :], ez[:, :, :], X, ALU.add))
                then(nc.vector.reciprocal(r4[1][:, :], r4[1][:, :]))
                then(tt(prob[:, :, :], ez[:, :, :], r4[1][:, :].unsqueeze(2).to_broadcast([P, T, E]), ALU.mult))
                p4 = prob[:, :, :].rearrange("p t (g e) -> p t g e", e=E // G)
                then(nc.vector.tensor_reduce(gs[:, :, :], p4, X, ALU.max))
                chosen = ranks(gs[:, :, :], 2, G, tri)
                spread = chosen.unsqueeze(3).to_broadcast([P, T, G, E // G])
                m4 = masked[:, :, :].rearrange("p t (g e) -> p t g e", e=E // G)
                then(tt(m4, p4, spread, ALU.mult))
                then(tt(m4, m4, spread, ALU.add))
                then(ts(masked[:, :, :], masked[:, :, :], -1.0, None, ALU.add))
                chosen = ranks(masked[:, :, :], 4, E, tri)
                then(tt(masked[:, :, :], prob[:, :, :], chosen, ALU.mult))
                combine_parts(masked[:, :, :], E)

            def router1():
                E, T = EXPERTS[1], B * NT
                dve.wait_ge(loaded["ebias"], 16)
                dve.wait_ge(ez_ready, 2)
                s = ez[:, :, 0:E]
                then(tt(masked[:, :, 0:E], s, ebias[:, :].unsqueeze(1).to_broadcast([P, T, E]), ALU.add))
                chosen = ranks(masked[:, :, 0:E], 2, E, tri)
                then(tt(prob[:, :, 0:E], s, chosen, ALU.mult))
                then(nc.vector.tensor_reduce(r4[0][:, :], prob[:, :, 0:E], X, ALU.add))
                then(ts(r4[0][:, :], r4[0][:, :], 1e-9, None, ALU.add))
                then(nc.vector.reciprocal(r4[0][:, :], r4[0][:, :]))
                then(tt(masked[:, :, 0:E], prob[:, :, 0:E], r4[0][:, :].unsqueeze(2).to_broadcast([P, T, E]), ALU.mult))
                combine_parts(masked[:, :, 0:E], E)

            def ffn(l):
                f = ff[l]

                def unit(u, b):
                    n = u + 1 - EU
                    ge(f["silu"], u + 1)
                    ge(f["u"], u + 1)
                    tt(gu[b], gact[b], PS[:, 5, :], ALU.mult).then_inc(f["gu"], 1)
                    ge(f["gu"], n)
                    ge(f["c"], n)
                    tt(hid[b], gu[b], PS[:, 6, :], ALU.mult).then_inc(f["hid"], 1)
                    ge(f["hi"], u + 1)
                    tt(hidR[b][1], hid[b], hidR[b][0].bitcast(F32), ALU.subtract).then_inc(f["lo"], 1)

                def pair(p):
                    for s in range(2):
                        for b in range(B):
                            unit(4 * p + 2 * s + b, b)

                pair(1)
                with dve.Fori(2, TILES[l] // 2) as p:
                    pair(p)
                if TILES[l] % 2:
                    for b in range(B):
                        unit(4 * (TILES[l] // 2) + b, b)
                for b in range(B):
                    gated(b, l, 1, 2 * b, f["w2"], lambda i: 2 * TILES[l])

            add_attention(0)
            norm(1)
            router0()
            ffn(0)
            norm(2)
            dve.wait_ge(loaded["bv"], 16)
            dve.wait_ge(loaded["esel"], 16)
            dve.wait_ge(consts, CONSTS)
            for b in range(B):
                for m in range(3):
                    dve.wait_ge(qhi, 4 * B + 3 * b + m + 1)
                    tt(qkR[1][:, m, :], qF[:, m, :], qkR[0][:, m, :].bitcast(F32), ALU.subtract).then_inc(qlo, 1)
                dve.wait_ge(proj, 6 * B + 4 * b + 4)
                tt(V1[:, :, b, 0:DH], PS[:, 3, 0:NT * DH].rearrange("p (t d) -> p t d", d=DH),
                   bv[:, :].unsqueeze(1).to_broadcast([P, NT, DH]), ALU.add).then_inc(v1_taken, 1)
                maxima_pass(1, b)
            outputs_pass(1)
            add_attention(1)
            norm(3)
            router1()
            ffn(1)


def shape_tables():
    q = np.arange(P)[:, None]
    c = np.arange(KEYS0)[None, :]
    band = (c >= q) & (c <= q + WIN)
    later = np.where(band, 0.0, NEG)
    first = np.where(band & (c >= WIN), 0.0, NEG)
    causal = np.where(np.arange(P)[None, :] < q, 0.0, NEG)
    bandT = np.where((c >= q) & (c <= q + WIN), 0.0, NEG)
    mask = np.concatenate([first, later, bandT, causal, np.full((P, P), NEG), causal.T], 1).astype(np.float32)
    headmask = (q // DH == np.arange(H)[None, :] % (P // DH)).astype(np.float32)
    tri = np.broadcast_to(np.tril(np.ones((16, 16)), -1), (P, 16, 16)).astype(np.float32)
    denominator = (q % VW == DH).astype(np.float32)
    esel = np.concatenate([denominator * (q // VW == np.arange(P)[None, :] // VW), denominator], 1).astype(np.float32)
    sel = []
    for l in range(2):
        s = np.zeros((TILES[l], P, P), np.float32)
        for row in range(EXPERTS[l] * INTER[l] + SHARED[l]):
            e = (row - SHARED[l]) // INTER[l]
            for k in ((e, 16 + e) if row >= SHARED[l] else (ONES_ROW,)):
                s[row // P, k, row % P] = 1.0
        sel.append(s)
    return {"ident": np.eye(P, dtype=np.float32), "mask": mask, "tri": np.ascontiguousarray(tri), "esel": esel, "headmask": headmask}, sel


def chunked_T(w):
    return np.ascontiguousarray(w.T.reshape(KC, P, w.shape[0]))


def by_output_rows(w):
    w = np.pad(w.T.reshape(H, DH, D), ((0, 0), (0, VW - DH), (0, 0)))
    return np.ascontiguousarray(w.reshape(OC, P, D))


def ffn_tiles(w1, w3, w2, sel):
    tiles = sel.shape[0]
    pad = tiles * P - w1.shape[0]
    w1, w3, w2 = (np.pad(w, ((0, pad), (0, 0))).reshape(tiles, P, D) for w in (w1, w3, w2))
    up = [w.transpose(0, 2, 1).reshape(tiles, KC, P, P).transpose(0, 2, 1, 3).reshape(tiles, P, D) for w in (w1, w3)]
    return np.ascontiguousarray(np.concatenate(up + [w2, sel], 2))


def kernel(**inputs):
    import concourse.bacc as bacc
    from concourse.bass_utils import run_bass_kernel_spmd as run

    i = {k: np.asarray(v) for k, v in inputs.items()}
    tables, sel = shape_tables()
    arrays = {
        "x": i["L0_attn_x"].reshape(B * S, D),
        "ct": np.ascontiguousarray(np.stack([i[f"L{l}_c"] for l in range(2)], 0).transpose(2, 0, 1)
                                   .reshape(KC, P, 2, B).transpose(1, 2, 0, 3)),
        "wmod0": i["L0_wmod"], "wmod1": i["L1_wmod"],
        "wqkv": chunked_T(i["L0_attn_w_qkv"]), "wout0": by_output_rows(i["L0_attn_w_out"]),
        "wq1": chunked_T(i["L1_attn_Wq"]),
        "wkv1": chunked_T(np.concatenate([np.tile(i["L1_attn_Wk"], (P // DH, 1)), i["L1_attn_Wv"]], 0)),
        "wout1": by_output_rows(i["L1_attn_Wo"]),
        "wg0": chunked_T(i["L0_ffn_Wg"]), "wg1": chunked_T(i["L1_ffn_router_w"]),
        "bq": np.ascontiguousarray(i["L1_attn_bq"].reshape(KC, P).T), "bk": np.tile(i["L1_attn_bk"], P // DH).reshape(P, 1),
        "bv": i["L1_attn_bv"], "bo": i["L1_attn_bo"], "ebias": i["L1_ffn_expert_bias"],
        "ffn0": ffn_tiles(np.concatenate([i["L0_ffn_Ws1"], i["L0_ffn_W1"].reshape(-1, D)], 0),
                          np.concatenate([i["L0_ffn_Ws3"], i["L0_ffn_W3"].reshape(-1, D)], 0),
                          np.concatenate([i["L0_ffn_Ws2"].T, i["L0_ffn_W2"].transpose(0, 2, 1).reshape(-1, D)], 0), sel[0]),
        "ffn1": ffn_tiles(np.concatenate([i["L1_ffn_sw1"], i["L1_ffn_w12"][:, :INTER[1]].reshape(-1, D)], 0),
                          np.concatenate([i["L1_ffn_sw2"], i["L1_ffn_w12"][:, INTER[1]:].reshape(-1, D)], 0),
                          np.concatenate([i["L1_ffn_sw3"].T, i["L1_ffn_w3"].transpose(0, 2, 1).reshape(-1, D)], 0), sel[1]),
    }
    arrays.update(tables)
    arrays = {k: np.ascontiguousarray(v) for k, v in arrays.items()}
    nc = bacc.Bacc("TRN2", target_bir_lowering=False, num_devices=1)
    io = {k: nc.dram_tensor(f"in_{k}", v.shape, F32, kind="ExternalInput").ap() for k, v in arrays.items()}
    out = nc.dram_tensor("out", (B * S, D), F32, kind="ExternalOutput").ap()
    build(nc, io, out)
    r = run(nc, [{f"in_{k}": v for k, v in arrays.items()}], core_ids=[0])
    return r.results[0]["out"].reshape(B, S, D)
```

```python
from contextlib import ExitStack

import numpy as np
import concourse.bass as bass
from concourse import mybir

F32 = mybir.dt.float32
F32R = mybir.dt.float32r
I32 = mybir.dt.int32
ACT = mybir.ActivationFunctionType
ALU = mybir.AluOpType
X = mybir.AxisListType.X

P = 128
B, S, D = 2, 512, 256
KC = D // P
NT = S // P
H, DH = 16, 16
UNITS = B * H
WIN = 64
KEYS0 = P + WIN
NEG = -2.0 ** 100
EPS = 1e-5
SCALE = DH ** -0.5
VW = 2 * DH
OC = H * VW // P
ROWS = 4 * DH
ROWSM = ROWS + 2
MAX_BANK = [4, 6]
Y_BANK = [0, 2]
DEN = [[(0, S // 2, 7), (S // 2, S, 5)], [(0, S, 7)]]
LOGIT_BANK = 5
GATE_BANK = [6, 5]
SLOTS = 4
QUADS = UNITS // SLOTS
BQ = QUADS // B
WIDTH1 = [2 * P, 2 * P, 3 * P, 4 * P]
BANK1 = [(0, 0), (0, 2 * P), (1, 0), (2, 0)]
ORDER1 = [0, 1, 3, 2]
SPAN1 = sum((NT - kb) * P for kb in range(NT))
START1 = {kb: sum((NT - j) * P for j in ORDER1[:i]) for i, kb in enumerate(ORDER1)}
EXPERTS = [16, 8]
INTER = [176, 128]
SHARED = [352, 1024]
SHT = [-(-n // P) for n in SHARED]
TILES = [SHT[l] + EXPERTS[l] * INTER[l] // P for l in range(2)]
GR = 16
EG = P // GR
HALVES = [n // EG for n in EXPERTS]
TW = 2 * D + D
SELK = 32
EARLY = 2
EU = 2 * EARLY
CONSTS = 27
RSQRT_MAGIC = float(0x5F3759DF)


def build(nc, io, out):
    ctx = ExitStack()
    with ctx:
        def sb(name, shape, dt=F32):
            return ctx.enter_context(nc.sbuf_tensor(name, shape, dt))

        def sem(name):
            return ctx.enter_context(nc.semaphore(name))

        PS = ctx.enter_context(nc.psum_tensor("PS", [P, 8, 512], F32))
        q_scr = [nc.dram_tensor(f"q{l}_scr", [UNITS, ROWSM, S], F32, kind="Internal").ap() for l in range(2)]
        k0_scr = nc.dram_tensor("k0_scr", [UNITS, 2, DH, S], F32, kind="Internal").ap()
        k1_scr = nc.dram_tensor("k1_scr", [B, 2, DH, S], F32, kind="Internal").ap()

        x = sb("x", [P, B, NT, D])
        ident = sb("ident", [P, P])
        identR = sb("identR", [P, P], F32R)
        maskR = sb("maskR", [P, 5 * KEYS0 + 3 * P], F32R)
        mask0 = [maskR[:, 0:2 * KEYS0], maskR[:, KEYS0:3 * KEYS0]]
        mask0T = maskR[:, 3 * KEYS0:5 * KEYS0]
        mask1 = maskR[:, 5 * KEYS0:5 * KEYS0 + 2 * P]
        mask1T = maskR[:, 5 * KEYS0 + 2 * P:]
        headmask = sb("headmask", [P, H])
        zeroR = sb("zeroR", [P, P], F32R)
        tri = sb("tri", [P, 16, 16])
        esel = sb("esel", [P, P + 1])
        ct = sb("ct", [P, 2, KC, B])
        sc = sb("sc", [P, 2, KC, B])
        wmod = [sb(f"wmod{l}", [P, KC, 6 * D]) for l in range(2)]
        modT = sb("modT", [P, 2, 8, B])
        gate = sb("gate", [P, 2, 2, B, D])
        w_raw = sb("w_raw", [P, KC, 3 * D])
        w_flat = w_raw[:, :, :].rearrange("p k n -> p (k n)").rearrange("p (c n) -> p c n", n=D)
        wqkv = [sb(f"wqkv_{n}", [P, KC, 3 * D], F32R) for n in ("hi", "lo")]
        wout = [[sb(f"wout{l}_{n}", [P, OC, D], F32R) for n in ("hi", "lo")] for l in range(2)]
        wq1 = [sb(f"wq1_{n}", [P, KC, D], F32R) for n in ("hi", "lo")]
        wkv1 = sb("wkv1", [P, KC, P + DH])
        wg = [sb(f"wg{l}", [P, KC, EXPERTS[l]]) for l in range(2)]
        bq = sb("bq", [P, KC])
        bqs = sb("bqs", [P, KC])
        bk = sb("bk", [P, 1])
        bv = sb("bv", [P, DH])
        bo = sb("bo", [P, D])
        ebias = sb("ebias", [P, EXPERTS[1]])
        stats = sb("stats", [P, B, NT, 6])
        mv = sb("mv", [P, B, NT, 2])
        ve = sb("ve", [P, B, NT])
        rs = sb("rs", [P, B, NT])
        nt_ = sb("nt", [P, B, NT])
        nm = sb("nm", [P, B, NT])
        xn = sb("xn", [P, NT, D])
        hF = sb("hF", [P, KC, B, S])
        scb = hF[:, 0, 0, :].rearrange("p (n q) -> p n q", q=P)
        gsign = [hF[:, 1, :, :].rearrange("p b t -> p (b t)"),
                 wmod[0][:, :, :].rearrange("p k n -> p (k n)")[:, 0:2 * B * D]]
        cmpA, cmpB = (w.rearrange("p (t a b) -> p t a b", a=16, b=16)
                      for w in (wmod[0][:, :, :].rearrange("p k n -> p (k n)")[:, 0:B * NT * 16 * 16],
                                hF[:, :, :, :].rearrange("p k b t -> p (k b t)")))
        hR = [sb(f"h_{n}", [P, KC, B, S], F32R) for n in ("hi", "lo")]
        qkR = [sb(f"qk_{n}", [P, 4, S], F32R) for n in ("hi", "lo")]
        q0F = hF[:, :, :, :].rearrange("p k b t -> p (k b) t")
        qF = w_raw[:, :, :].rearrange("p k n -> p (k n)").rearrange("p (m t) -> p m t", t=S)
        qk = [sb(f"qk_slot{s}", [P, 2 * S + WIN], F32R) for s in range(SLOTS)]
        k1 = sb("k1", [P, B, S], F32R)
        qm = [sb(f"q_masked{s}", [P, S], F32R) for s in range(SLOTS)]
        V = sb("V", [P, NT, UNITS, DH])
        Vs = [sb(f"V_slot{s}", [P, NT, VW]) for s in range(SLOTS)]
        V1 = sb("V1", [P, NT, B, VW])
        nmx = sb("nmx", [P, UNITS * NT])
        mxT = [sb(f"mxT_{n}", [H * NT, B, P], F32R) for n in ("hi", "lo")]
        pr = [sb(f"pr{s}", [P, SPAN1]) for s in range(2)]
        probs = [[pr[0], pr[1]] + [w_raw[:, i, :] for i in range(KC)],
                 [pr[0], pr[1]] + [wmod[1][:, :, :].rearrange("p k n -> p (k n)")[:, i * SPAN1:(i + 1) * SPAN1]
                                   for i in range(2)]]
        o_parts = sb("o_parts", [P, 3, S])
        oF, oR, oN = (o_parts[:, i, :] for i in range(3))
        oT = [[w[:, :, :, :].rearrange("p k b t -> p (k b t)").rearrange("p (c t) -> p c t", t=S) for w in hR],
              [w[:, :, :] for w in qkR]]
        mask_raw = pr[1][:, 0:3 * KEYS0 + 3 * P]
        xnb = [xn[:, :, :], o_parts[:, 0:2, :].rearrange("p a t -> p (a t)").rearrange("p (t d) -> p t d", d=D)]
        ytmp = xn
        lg, ez, prob, rank = (oN[:, i * P:(i + 1) * P].rearrange("p (t e) -> p t e", e=16) for i in range(4))
        r4 = [sb(f"r4_{i}", [P, B * NT]) for i in range(2)]
        gs = sb("gs", [P, B * NT, 4])
        masked = sb("masked", [P, B * NT, 16])
        cR = sb("cR", [P, B * NT, 16], F32R)
        cparts = sb("cparts", [P, B, NT, SELK])
        cT = sb("cT", [SELK, B, S], F32R)
        fw = [sb(f"fw_raw{s}", [P, TW]) for s in range(2)]
        fwR = [[wqkv[s][:, :, :].rearrange("p k n -> p (k n)")[:, a * TW:(a + 1) * TW] for a in range(2)] for s in range(2)]
        cselR = sb("cselR", [SELK, 2, P], F32R)
        cB = [[V[:, 2 * b + h, :, :].rearrange("p u d -> p (u d)") for h in range(2)] for b in range(B)]
        csel_raw = pr[1][0:SELK, 3 * KEYS0 + 3 * P:3 * KEYS0 + 5 * P]
        gact = [pr[b][:, 0:S] for b in range(B)]
        gu = [pr[b][:, S:2 * S] for b in range(B)]
        hid = [xn[:, 2 * b:2 * b + 2, :].rearrange("p t d -> p (t d)") for b in range(B)]
        hidR = [[qkR[a][:, b, :] for a in range(2)] for b in range(B)]

        in_names = ["ct", "wmod0a", "wmod0b", "wmod1", "x0", "x1", "wqkv", "ident", "mask", "csel", "tri", "esel", "headmask", "wout0", "wq1",
                    "wkv1", "wout1", "wg0", "wg1", "bq", "bk", "bv", "bo", "ebias"]
        loaded = {n: sem(f"ld_{n}") for n in in_names}
        consts = sem("consts")
        wqkv_high = sem("wqkv_high")
        wqkv_ready = sem("wqkv_ready")
        split = sem("split")
        pool_order = sem("pool_order")
        dve_order = sem("dve_order")
        act_order = sem("act_order")
        sc_done = sem("sc_done")
        scb_done = sem("scb_done")
        mod_ps = sem("mod_ps")
        modT_taken = sem("modT_taken")
        gate_taken = sem("gate_taken")
        shifts1_taken = sem("shifts1_taken")
        stats_done = sem("stats_done")
        mv_done = sem("mv_done")
        rs_ready = sem("rs_ready")
        xn_ready = [sem(f"xn{b}_ready") for b in range(B)]
        xt_ready = sem("xt_ready")
        h_ready = [sem(f"h{b}_ready") for b in range(B)]
        hi_ready = sem("hi_ready")
        hl_ready = sem("hl_ready")
        proj = sem("proj")
        qhi = sem("qhi")
        qlo = sem("qlo")
        v_taken = sem("v_taken")
        v1_taken = sem("v1_taken")
        q0F_ready = sem("q0F_ready")
        qF_ready = sem("qF_ready")
        scr0_written = [sem(f"scr0_written{m}") for m in range(4)]
        scr1_written = sem("scr1_written")
        k1_loaded = sem("k1_loaded")
        o_first = sem("o_first")
        y_ps = sem("y_ps")
        y_gated = sem("y_gated")
        x_new = sem("x_new")
        lg_ps = sem("lg_ps")
        z_ready = sem("z_ready")
        ez_ready = sem("ez_ready")
        cp_ready = sem("cp_ready")
        cT_ps = sem("cT_ps")
        cT_ready = sem("cT_ready")
        cB_ps = sem("cB_ps")
        cB_ready = sem("cB_ready")
        out_written = sem("out_written")
        at = []
        for l in range(2):
            at.append({n: sem(f"at{l}_{n}") for n in (
                "qk0", "qk1", "qk2", "qk3", "qm", "s", "mxd", "mt", "mhi", "mlo", "mw0", "mw1", "st", "p", "vs", "o", "oe", "den",
                "rd", "od", "oh", "ol")})
        ff = []
        for l in range(2):
            ff.append({n: sem(f"ff{l}_{n}") for n in (
                "w0", "w1", "hi_w", "split", "g", "u", "silu", "gu", "hid", "hi", "lo", "w2",
                "early_hid", "early_lo")})

        ORDER0 = ((0, 1, 2, 3), (0, 2, 1, 3))
        SPANS = [[(2, TILES[0] // 2)], [(2, SHT[1] // 2), (SHT[1] // 2, TILES[1] // 2)]]

        def routed(l, p, s):
            return 2 * p + s >= SHT[l]

        block = ctx.enter_context(nc.Block())

        def store_maxima(eng, l, b):
            for part, done in ((0, "mhi"), (1, "mlo")):
                eng.wait_ge(at[l][done], b + 1)
                eng.dma_start(q_scr[l][b * H:(b + 1) * H, ROWS + part, :].rearrange("u (t q) -> u t q", q=P),
                              mxT[part][:, b, :].bitcast(F32)).then_inc(at[l][f"mw{b}"], 16)

        @block.sync
        def _(sp):
            def load(name, dst, src):
                sp.dma_start(dst, src).then_inc(loaded[name], 16)

            load("ct", ct[:, :, :, :], io["ct"])
            for b in range(B):
                load(f"x{b}", x[:, b, :, :], io["x"][b * S:(b + 1) * S, :].rearrange("(t p) d -> p t d", p=P))
            w0 = io["wmod0"].rearrange("(k p) n -> p k n", p=P)
            load("wmod0a", wmod[0][:, :, 0:2 * D], w0[:, :, 0:2 * D])
            load("ident", ident[:, :], io["ident"])
            load("wqkv", w_raw[:, :, :], io["wqkv"].rearrange("k p n -> p k n"))
            load("wmod0b", wmod[0][:, :, 2 * D:], w0[:, :, 2 * D:])
            load("mask", mask_raw, io["mask"])
            load("csel", csel_raw, io["csel"])
            load("wmod1", wmod[1][:, :, :], io["wmod1"].rearrange("(k p) n -> p k n", p=P))
            load("tri", tri[:, :, :], io["tri"])
            load("headmask", headmask[:, :], io["headmask"])
            load("esel", esel[:, :], io["esel"])
            for l in range(2):
                load(f"wg{l}", wg[l][:, :, :], io[f"wg{l}"].rearrange("k p n -> p k n"))
            load("wkv1", wkv1[:, :, :], io["wkv1"].rearrange("k p n -> p k n"))
            load("bq", bq[:, :], io["bq"])
            load("bk", bk[:, :], io["bk"])
            load("bv", bv[:, :], io["bv"].partition_broadcast(P))
            load("bo", bo[:, :], io["bo"].partition_broadcast(P))
            load("ebias", ebias[:, :], io["ebias"].partition_broadcast(P))
            for n, (name, w) in enumerate((("wout0", OC), ("wq1", KC), ("wout1", OC))):
                if n:
                    sp.wait_ge(split, n)
                else:
                    sp.wait_ge(wqkv_ready, 1)
                load(name, w_flat[:, 0:w, :], io[name].rearrange("k p n -> p k n"))

            for b in range(B):
                for i, m in enumerate(ORDER0[b]):
                    u = b * H + 8 * (m % 2)
                    for part, done in ((0, qhi), (1, qlo)):
                        sp.wait_ge(done, 4 * b + i + 1)
                        src = qkR[part][:, m, :].bitcast(F32)
                        if m >= 2:
                            sp.dma_start(k0_scr[u:u + 8, part, :, :], src).then_inc(scr0_written[m], 16)
                        else:
                            for row in (2 * part, 2 * part + 1):
                                sp.dma_start(q_scr[0][u:u + 8, row * DH:(row + 1) * DH, :], src)\
                                    .then_inc(scr0_written[m], 16)

            def load_keys_major(l, g, s):
                if not (isinstance(g, int) and g == 0):
                    sp.wait_ge(at[l]["st"], (1, 2)[l] * (4 * g + s - 3))
                u = 4 * g + s
                sp.dma_start(qk[s][0:ROWSM, 0:S].bitcast(F32),
                             q_scr[l][bass.ds(u, 1), :, :].rearrange("u r t -> (u r) t")).then_inc(at[l][f"qk{s}"], 16)
                if l == 0:
                    rows = k0_scr[bass.ds(u, 1), :, :, :].rearrange("u r d t -> (u r d) t")
                    twice = bass.AP(rows.tensor, rows.offset, [[0, 2]] + list(rows.ap))
                    sp.dma_start(qk[s][0:ROWS, S + WIN:].bitcast(F32), twice).then_inc(at[l][f"qk{s}"], 16)

            def load_attention(l):
                sp.wait_ge(at[l]["mw0"], 16 * 2)
                for s in range(SLOTS):
                    load_keys_major(l, 0, s)
                with sp.Fori(1, BQ) as g:
                    for s in range(SLOTS):
                        load_keys_major(l, g, s)
                sp.wait_ge(at[l]["mw1"], 16 * 2)
                with sp.Fori(BQ, QUADS) as g:
                    for s in range(SLOTS):
                        load_keys_major(l, g, s)

            store_maxima(sp, 0, 0)
            sp.wait_ge(consts, CONSTS)
            for m in range(4):
                sp.wait_ge(scr0_written[m], 16 * (4, 2)[m // 2] * B)
            load_attention(0)

            def load_ffn(l, p, s, i):
                if not (isinstance(p, int) and p == 0):
                    sp.wait_ge(ff[l]["split"], 2 * p + s - 1)
                sp.dma_start(fw[s][:, :], io[f"ffn{l}"][bass.ds(i, 1), :, :].rearrange("a p n -> (a p) n"))\
                    .then_inc(ff[l][f"w{s}"], 16)

            def load_ffn_all(l):
                for s in range(2):
                    load_ffn(l, 0, s, s)
                with sp.Fori(1, TILES[l] // 2) as p:
                    for s in range(2):
                        load_ffn(l, p, s, 2 * p + s)
                if TILES[l] % 2:
                    load_ffn(l, TILES[l] // 2, 0, TILES[l] - 1)

            load_ffn_all(0)

            for b in range(B):
                for part, done in ((0, qhi), (1, qlo)):
                    sp.wait_ge(done, 4 * B + 3 * b + 3)
                    for c in range(KC):
                        u = b * H + 8 * c
                        for row in (2 * part, 2 * part + 1):
                            sp.dma_start(q_scr[1][u:u + 8, row * DH:(row + 1) * DH, :], qkR[part][:, c, :].bitcast(F32))\
                                .then_inc(scr1_written, 16)
                    sp.dma_start(k1_scr[b, part, :, :], qkR[part][0:DH, 2, :].bitcast(F32)).then_inc(scr1_written, 16)
            sp.wait_ge(scr1_written, 16 * 10 * B)
            for b in range(B):
                for r in range(2):
                    sp.dma_start(k1[32 * r:32 * r + 32, b, :].bitcast(F32),
                                 k1_scr[b, :, :, :].rearrange("l r t -> (l r) t")).then_inc(k1_loaded, 16)
            store_maxima(sp, 1, 0)
            sp.wait_ge(at[0]["st"], UNITS)
            load_attention(1)

            load_ffn_all(1)
            for b in range(B):
                for i in range(2):
                    sp.wait_ge(x_new, 2 * B * 3 + 2 * b + i + 1)
                    rows = slice(b * S + i * S // 2, b * S + (i + 1) * S // 2)
                    sp.dma_start(out[rows, :].rearrange("(t p) d -> p t d", p=P), x[:, b, 2 * i:2 * i + 2, :])\
                        .then_inc(out_written, 16)
            sp.wait_ge(out_written, 16 * 2 * B)

        @block.gpsimd
        def _(pool):
            order = [0]

            def then(ins):
                order[0] += 1
                ins.then_inc(pool_order, 1)
                pool.wait_ge(pool_order, order[0])

            for tile in [cparts[:, :, :, :], V1[:, :, :, :], zeroR[:, :].bitcast(F32), k1[:, :, :].bitcast(F32)] \
                    + [t[:, :].bitcast(F32) for t in qk] + [t[:, :, :] for t in Vs]:
                nc.gpsimd.memset(tile, 0.0).then_inc(consts, 1)
            pool.wait_ge(loaded["ident"], 16)
            nc.gpsimd.tensor_copy(identR[:, :], ident[:, :]).then_inc(consts, 1)
            pool.wait_ge(loaded["mask"], 16)
            for to, (start, end) in ((0, (0, 2)), (2, (1, 3)), (4, (2, 5))):
                nc.gpsimd.tensor_copy(maskR[:, to * KEYS0:(to + end - start) * KEYS0],
                                      mask_raw[:, start * KEYS0:end * KEYS0]).then_inc(consts, 1)
            pool.wait_ge(loaded["csel"], 16)
            nc.gpsimd.tensor_copy(cselR[:, :, :].rearrange("p h q -> p (h q)"), csel_raw).then_inc(consts, 1)
            pool.wait_ge(consts, CONSTS - 10)
            for tile in [V1[:, :, :, DH:DH + 1]] + [t[:, :, DH:DH + 1] for t in Vs]:
                nc.gpsimd.memset(tile, 1.0).then_inc(consts, 1)
            for i, rows in enumerate([k1[ROWS:ROWSM, :, :]] + [t[ROWS:ROWSM, S + WIN:] for t in qk]):
                pool.wait_ge(consts, CONSTS - 5 + i)
                nc.gpsimd.memset(rows.bitcast(F32), 1.0).then_inc(consts, 1)
            pool.wait_ge(consts, CONSTS)

            for name, pair, raw in (("wout0", wout[0], w_flat[:, 0:OC, :]), ("wq1", wq1, w_flat[:, 0:KC, :]),
                                    ("wout1", wout[1], w_flat[:, 0:OC, :])):
                pool.wait_ge(loaded[name], 16)
                then(nc.gpsimd.tensor_copy(pair[0][:, :, :], raw))
                nc.gpsimd.tensor_tensor(pair[1][:, :, :], raw, pair[0][:, :, :].bitcast(F32), ALU.subtract)\
                    .then_inc(split, 1)

            def ge(s, value):
                if not (isinstance(value, int) and value <= 0):
                    pool.wait_ge(s, value)

            def take_values(g, s):
                u = 4 * g + s
                ge(at[0]["o"], u - 3)
                nc.gpsimd.tensor_tensor(Vs[s][:, :, 0:DH], V[:, :, bass.ds(u, 1), :].rearrange("p t u d -> p t (u d)"),
                                        zeroR[:, 0:NT * DH].bitcast(F32).rearrange("p (t d) -> p t d", d=DH), ALU.add)\
                    .then_inc(at[0]["vs"], 1)

            def out_low(l, b, g):
                ge(at[l]["oh"], g + 1)
                c = bass.ds(g - BQ * b, 1)
                nc.gpsimd.tensor_tensor(oT[b][1][:, c, :].rearrange("p c t -> p (c t)"), oN[:, :],
                                        oT[b][0][:, c, :].rearrange("p c t -> p (c t)").bitcast(F32), ALU.subtract)\
                    .then_inc(at[l]["ol"], 1)

            def attention(l):
                def quad(g, b):
                    if l == 0:
                        for s in range(SLOTS):
                            take_values(g, s)
                    if b is not None:
                        out_low(l, b, g - 2)

                if l == 0:
                    pool.wait_ge(v_taken, 2 * B)
                    quad(0, None)
                    quad(1, None)
                for b, (start, end) in enumerate(((2, BQ + 2), (BQ + 2, QUADS))):
                    with pool.Fori(start, end) as g:
                        quad(g, b)
                out_low(l, B - 1, QUADS - 2)
                out_low(l, B - 1, QUADS - 1)

            def weights_low(l, i, s):
                f = ff[l]
                if isinstance(i, int) and i < 2:
                    pool.wait_ge(f[f"w{s}"], 16)
                    pool.wait_ge(f["hi_w"], i + 1)
                else:
                    pool.wait_ge(f["hi_w"], i + 1)
                nc.gpsimd.tensor_tensor(fwR[s][1], fw[s][:, :], fwR[s][0].bitcast(F32), ALU.subtract)\
                    .then_inc(f["split"], 1)

            def early_unit(l, u, b):
                f = ff[l]
                pool.wait_ge(f["hi"], u + 1)
                nc.gpsimd.tensor_tensor(hidR[b][1], hid[b], hidR[b][0].bitcast(F32), ALU.subtract)\
                    .then_inc(f["early_lo"], 1)

            for l in range(2):
                attention(l)
                for i in range(EARLY):
                    weights_low(l, i, i)
                for u in range(EU):
                    early_unit(l, u, u % 2)
                    if u >= EU - 2:
                        weights_low(l, u, u % 2)
                with pool.Fori(EARLY, TILES[l] // 2) as p:
                    for s in range(2):
                        weights_low(l, 2 * p + s, s)
                if TILES[l] % 2:
                    weights_low(l, TILES[l] - 1, 0)
        @block.tensor
        def _(pe):
            def ge(s, value):
                if not (isinstance(value, int) and value <= 0):
                    pe.wait_ge(s, value)

            PASSES = ((0, 0), (0, 1), (1, 0))

            def product(dst, left, right, chunks, **flags):
                n, total = 0, chunks * len(PASSES)
                for c in range(chunks):
                    for a, b in PASSES:
                        ins = nc.tensor.matmul(dst, left(a, c), right(b, c), start=n == 0, stop=n == total - 1)
                        n += 1
                return ins

            def shifts(l, j, bank):
                col = (0, 1, 3, 4)[j // 2] * D + (j % 2) * P
                for k in range(KC):
                    ins = nc.tensor.matmul(PS[:, bank, (l * 8 + j) * B:(l * 8 + j + 1) * B], wmod[l][:, k, col:col + P],
                                           sc[:, l, k, :], start=k == 0, stop=k == KC - 1)
                return ins

            pe.wait_ge(sc_done, 1)
            pe.wait_ge(loaded["wmod0a"], 16)
            for j in range(4):
                ins = shifts(0, j, 7)
            ins.then_inc(mod_ps, 1)

            def shifts_rest0():
                pe.wait_ge(loaded["wmod0b"], 16)
                for j in range(4, 8):
                    ins = shifts(0, j, 7)
                ins.then_inc(mod_ps, 1)

            def shifts1():
                pe.wait_ge(loaded["wmod1"], 16)
                for j in range(8):
                    ins = shifts(1, j, 7)
                ins.then_inc(mod_ps, 1)

            def gates(l):
                pe.wait_ge(scb_done, l + 1)
                if l == 0:
                    pe.wait_ge(loaded["wmod0b"], 16)
                    pe.wait_ge(v_taken, 2 * B)
                for g in range(2):
                    for b in range(B):
                        col = (2, 5)[g] * D
                        for k in range(KC):
                            ins = nc.tensor.matmul(PS[:, GATE_BANK[l] + g, b * D:(b + 1) * D],
                                                   scb[:, k * B + b, :],
                                                   wmod[l][:, k, col:col + D], start=k == 0, stop=k == KC - 1)
                ins.then_inc(mod_ps, 1)

            def norm_transposes(n):
                for b in range(B):
                    pe.wait_ge(xn_ready[b], n + 1)
                    if n == 0:
                        pe.wait_ge(loaded["ident"], 16)
                    if n == 2 and b == 0:
                        pe.wait_ge(gate_taken, 4)
                    if b == 1 and n < 3:
                        pe.wait_ge((modT_taken, modT_taken, shifts1_taken)[n], (1, 2, 1)[n])
                    for c in range(KC):
                        for t in range(NT):
                            ins = nc.tensor.transpose(PS[:, 4 + 2 * b + c, t * P:(t + 1) * P],
                                                      xnb[b][:, t, c * P:(c + 1) * P], ident[:, :])
                    ins.then_inc(xt_ready, 1)

            norm_transposes(0)

            BANK0 = ((0, 1, 2, 3, 4, 5), (5, 6, 7, 5, 6, 7))

            def project0(b, m):
                if m == 0:
                    pe.wait_ge(hl_ready, 2 * b + 2)
                    pe.wait_ge(wqkv_ready, 1)
                if b and m == 0:
                    pe.wait_ge(v_taken, 2)
                if b and m >= 3:
                    pe.wait_ge(q0F_ready, m - 2)
                bank = BANK0[b][m]
                if m < 4:
                    product(PS[:, bank, :], lambda a, c: wqkv[a][:, c, m * P:(m + 1) * P],
                            lambda a, c: hR[a][:, c, b, :], KC).then_inc(proj, 1)
                    return
                for j in range(2):
                    t = 2 * (m - 4) + j
                    ins = product(PS[:, bank, j * D:(j + 1) * D], lambda a, c: hR[a][:, c, b, t * P:(t + 1) * P],
                                  lambda a, c: wqkv[a][:, c, 2 * D:3 * D], KC)
                ins.then_inc(proj, 1)

            BANKS1 = ((0, 1, 2, 3), (7, 6, 7, 6))

            def project1(b, m):
                if m == 0:
                    pe.wait_ge(hl_ready, 2 * (4 + b) + 2)
                    if b == 0:
                        pe.wait_ge(x_new, 2 * B * 2)
                        pe.wait_ge(loaded["wkv1"], 16)
                        pe.wait_ge(split, 2)
                if b and m >= 2:
                    pe.wait_ge(qF_ready, 3 + m - 1)
                bank = BANKS1[b][m]
                if m < 2:
                    ins = product(PS[:, bank, :], lambda a, c: wq1[a][:, c, m * P:(m + 1) * P],
                                  lambda a, c: hR[a][:, c, b, :], KC)
                elif m == 2:
                    for c in range(KC):
                        ins = nc.tensor.matmul(PS[:, bank, :], wkv1[:, c, 0:P], hF[:, c, b, :],
                                               start=c == 0, stop=c == KC - 1)
                else:
                    for t in range(NT):
                        for c in range(KC):
                            ins = nc.tensor.matmul(PS[:, bank, t * DH:(t + 1) * DH], hF[:, c, b, t * P:(t + 1) * P],
                                                   wkv1[:, c, P:], start=c == 0, stop=c == KC - 1)
                ins.then_inc(proj, 1)

            def scores(l, g, s, b):
                a = at[l]
                u = 4 * g + s
                ge(a["qm"], u + 1)
                if l == 0:
                    k = qkR[0][:, bass.ds(2 + (g - BQ * b) // 2, 1), :].rearrange("p m t -> p (m t)")
                    for t in range(NT):
                        bank, col = 2 * (s % 2) + t // 2, (t % 2) * KEYS0
                        if t % 2 == 0:
                            ge(a["mxd"], 2 * (u - 2) + t // 2 + 1)
                            nc.tensor.matmul(PS[:, bank, 0:2 * KEYS0], identR[:, :], mask0[t // 2], start=True, stop=True)
                        before = WIN * (t > 0)
                        ins = nc.tensor.matmul(PS[:, bank, col + WIN - before:col + KEYS0], qm[s][:, t * P:(t + 1) * P],
                                               k[:, t * P - before:(t + 1) * P], start=False, stop=True,
                                               skip_group_check=True)
                        if t % 2:
                            ins.then_inc(a["s"], 1)
                    return
                ge(a["mxd"], 3 * (u - 1))
                for qt in range(NT):
                    bank, col = BANK1[qt]
                    bank += 3 * (s % 2)
                    diagonal = WIDTH1[qt] - qt * P
                    nc.tensor.matmul(PS[:, bank, col:col + WIDTH1[qt]], qm[s][:, qt * P:(qt + 1) * P],
                                     qkR[0][:, 2, 0:WIDTH1[qt]], start=True, stop=True)
                    ins = nc.tensor.matmul(PS[:, bank, col + qt * P:col + WIDTH1[qt]], identR[:, :],
                                           mask1[:, 0:diagonal], start=False, stop=True, skip_group_check=True)
                    if qt:
                        ins.then_inc(a["s"], 1)

            def max_rows(l, b):
                a = at[l]
                pe.wait_ge(a["mxd"], (2, 3)[l] * H * (b + 1))
                if b:
                    pe.wait_ge(a["mlo"], 1)
                nc.tensor.transpose(PS[0:H * NT, MAX_BANK[l], 0:P], nmx[:, b * H * NT:(b + 1) * H * NT], ident[:, :])\
                    .then_inc(a["mt"], 1)

            def maxima_pass(l, beside):
                pe.wait_ge(consts, CONSTS)
                if l == 0:
                    pe.wait_ge(qlo, 4)
                else:
                    pe.wait_ge(v1_taken, 1)
                for b in range(B):
                    pe.wait_ge(qhi, (4, 6)[b] if l == 0 else 4 * B + 3 * (b + 1))
                    for s in range(SLOTS):
                        scores(l, BQ * b, s, b)
                        for work in beside[b][s]:
                            work()
                    if b:
                        if l:
                            pe.wait_ge(v1_taken, 2)
                        max_rows(l, 0)
                        if l == 0:
                            pe.wait_ge(qhi, 4 * B)
                    with pe.Fori(BQ * b + 1, BQ * (b + 1)) as g:
                        for s in range(SLOTS):
                            scores(l, g, s, b)
                max_rows(l, 1)

            def keys_major(l, g, s, b):
                a = at[l]
                u = 4 * g + s
                ge(a[f"qk{s}"], (32, 16)[l] * (g + 1))
                if l == 0:
                    ge(a["p"], u - 1)
                    for kb in range(NT):
                        bank, col = 2 * (s % 2) + kb // 2, (kb % 2) * KEYS0
                        if kb % 2 == 0:
                            nc.tensor.matmul(PS[:, bank, 0:2 * KEYS0], identR[:, :], mask0T, start=True, stop=True)
                        ins = nc.tensor.matmul(PS[:, bank, col:col + KEYS0], qk[s][:, S + WIN + kb * P:S + WIN + (kb + 1) * P],
                                               qk[s][:, kb * P:kb * P + KEYS0], start=False, stop=True,
                                               skip_group_check=True)
                    ins.then_inc(a["st"], 1)
                    return
                for i, kb in enumerate(ORDER1):
                    if i < 2:
                        ge(a["p"], 2 * (u - 2) + i + 1)
                    n = (NT - kb) * P
                    bank, col = 3 * (s % 2) + START1[kb] // S, START1[kb] % S
                    nc.tensor.matmul(PS[:, bank, col:col + n], k1[:, b, kb * P:(kb + 1) * P], qk[s][:, kb * P:S],
                                     start=True, stop=True)
                    ins = nc.tensor.matmul(PS[:, bank, col:col + P], identR[:, :], mask1T, start=False, stop=True,
                                           skip_group_check=True)
                    if i in (0, NT - 1):
                        ins.then_inc(a["st"], 1)

            def values(l, g, s, b):
                a = at[l]
                u = 4 * g + s
                if s == 0:
                    ge(a["oe"], g)
                if l == 0:
                    ge(a["vs"], u + 1)
                ge(a["p"], (l + 1) * (u + 1))
                for kb in range(NT):
                    if l == 0:
                        col, n = kb * KEYS0, min(KEYS0, S - kb * P)
                        v = Vs[s][:, kb, :]
                    else:
                        col, n = START1[kb], S - kb * P
                        v = V1[:, kb, b, :]
                    ins = nc.tensor.matmul(PS[s * VW:(s + 1) * VW, 6, kb * P:kb * P + n], v, probs[l][s][:, col:col + n],
                                           start=kb == 0, stop=kb == NT - 1, skip_group_check=True,
                                           tile_position=(0, s * VW))
                ins.then_inc(a["o"], 1)

            def denominators(l, g):
                a = at[l]
                ge(a["od"], g)
                ge(a["oe"], g + 1)
                for lo, hi, bank in DEN[l]:
                    nc.tensor.matmul(PS[:, bank, 0:hi - lo], esel[:, 0:P], oF[:, lo:hi], start=True, stop=True)\
                        .then_inc(a["den"], 1)

            def project_out(l, b, chunks, first, tiles=range(NT)):
                for t in tiles:
                    dst = PS[:, Y_BANK[b] + t // 2, (t % 2) * D:(t % 2 + 1) * D]
                    for c in chunks:
                        for i, (a, w) in enumerate(PASSES):
                            start = first and c == chunks[0] and i == 0
                            ins = nc.tensor.matmul(dst, oT[b][a][:, c, t * P:(t + 1) * P], wout[l][w][:, c, :],
                                                   start=start, stop=c == OC - 1 and i == len(PASSES) - 1,
                                                   skip_group_check=not first)
                    if t % 2 and chunks[-1] == OC - 1:
                        ins.then_inc(y_ps, 1)

            def values_pass(l):
                def second(g, b):
                    for s in range(SLOTS):
                        if s < SLOTS - 2:
                            keys_major(l, g, s + 2, b)
                        elif isinstance(g, int) and g == BQ - 1:
                            keys_major(l, g + 1, s + 2 - SLOTS, 1)
                        elif not (isinstance(g, int) and g == QUADS - 1):
                            keys_major(l, g + 1, s + 2 - SLOTS, b)
                        if s == 0 and not (isinstance(g, int) and g == 0):
                            denominators(l, g - 1)
                        if l == 0 and isinstance(g, int) and g == 0 and s == 0:
                            pe.wait_ge(gate_taken, 2)
                        values(l, g, s, b)

                for s in range(2):
                    keys_major(l, 0, s, 0)
                if l == 0:
                    gates(0)
                pe.wait_ge(at[l]["mlo"], B)
                second(0, 0)
                with pe.Fori(1, BQ - 1) as g:
                    second(g, 0)
                second(BQ - 1, 0)
                with pe.Fori(BQ, QUADS - 1) as g:
                    second(g, 1)
                second(QUADS - 1, 1)
                pe.wait_ge(split, (1, 3)[l])
                project_out(l, 0, range(OC), True, (0,))
                denominators(l, QUADS - 1)

            def next0(*ms):
                return [lambda m=m: project0(1, m) for m in ms]

            for m in range(6):
                project0(0, m)
            maxima_pass(0, ([next0(m) for m in range(4)], [next0(4), [], next0(5), []]))
            values_pass(0)

            def out_projection(l):
                zero(*range(Y_BANK[1], Y_BANK[1] + 2))
                project_out(l, 0, range(OC), True, range(1, NT))
                pe.wait_ge(at[l]["ol"], QUADS - 1)
                project_out(l, 1, range(OC - 1), False)
                pe.wait_ge(at[l]["ol"], QUADS)
                project_out(l, 1, range(OC - 1, OC), False)

            def logits(l):
                E = EXPERTS[l]
                pe.wait_ge(loaded[f"wg{l}"], 16)
                for b in range(B):
                    pe.wait_ge(h_ready[b], 2 * (2 * l + 1) + 2)
                    for t in range(NT):
                        for c in range(KC):
                            ins = nc.tensor.matmul(PS[:, LOGIT_BANK, (b * NT + t) * E:(b * NT + t + 1) * E],
                                                   hF[:, c, b, t * P:(t + 1) * P], wg[l][:, c, :],
                                                   start=c == 0, stop=c == KC - 1)
                ins.then_inc(lg_ps, 1)

            def combine_rows(l):
                pe.wait_ge(cp_ready, l + 1)
                for b in range(B):
                    for t in range(NT):
                        ins = nc.tensor.transpose(PS[0:SELK, 6 + b, t * P:(t + 1) * P], cparts[:, b, t, :], ident[:, :])
                    ins.then_inc(cT_ps, 1)

            def combine_table(l, h):
                for b in range(B):
                    if h == 0:
                        pe.wait_ge(cT_ready, 2 * l + 2)
                    else:
                        pe.wait_ge(cB_ready, b + 1)
                    nc.tensor.matmul(PS[:, 6 + b, :], cselR[:, h, :], cT[:, b, :], start=True, stop=True)\
                        .then_inc(cB_ps, 1)

            def zero(*banks):
                for bank in banks:
                    nc.tensor.matmul(PS[:, bank, :], zeroR[:, :], maskR[:, 0:S], start=True, stop=True)

            def ffn(l):
                f = ff[l]
                pe.wait_ge(hl_ready, 2 * (2 * (2 * l + 1) + 1) + 2)

                def down(p, s, b):
                    u = 4 * p + 2 * s + b
                    if isinstance(u, int) and u < EU:
                        ge(f["early_lo"], u + 1)
                    else:
                        ge(f["lo"], u + 1 - EU)
                    for t in range(NT):
                        for i, (a, w) in enumerate(PASSES):
                            ins = nc.tensor.matmul(PS[:, 2 * b + t // 2, (t % 2) * D:(t % 2 + 1) * D],
                                                   hidR[b][a][:, t * P:(t + 1) * P], fwR[s][w][:, 2 * D:],
                                                   start=False, stop=True, skip_group_check=True)
                    ins.then_inc(f["w2"], 1)

                def up(p, s, b):
                    u = 4 * p + 2 * s + b
                    if b == 0:
                        ge(f["split"], 2 * p + s + 1)
                    for i, name in enumerate("gu"):
                        if i == 0:
                            ge(f["silu"], u)
                        elif isinstance(u, int) and u == 0:
                            pe.wait_ge((z_ready, ez_ready)[l], l + 1)
                        elif isinstance(u, int) and u <= EU:
                            ge(f["early_hid"], u)
                        else:
                            ge(f["gu"], u - EU)
                        product(PS[:, 4 + i, :], lambda a, c: fwR[s][a][:, i * D + c * P:i * D + (c + 1) * P],
                                lambda a, c: hR[a][:, c, b, :], KC).then_inc(f[name], 1)

                def pair(p):
                    for s in range(2):
                        up(p, s, 0)
                        if s == 1:
                            down(p, 0, 1)
                        else:
                            down(p - 1, 1, 1)
                        up(p, s, 1)
                        down(p, s, 0)

                up(0, 0, 0)
                up(0, 0, 1)
                down(0, 0, 0)
                up(0, 1, 0)
                down(0, 0, 1)
                up(0, 1, 1)
                down(0, 1, 0)
                up(1, 0, 0)
                down(0, 1, 1)
                combine_rows(l)
                up(1, 0, 1)
                combine_table(l, 0)
                down(1, 0, 0)
                if HALVES[l] > 1:
                    combine_table(l, 1)
                up(1, 1, 0)
                down(1, 0, 1)
                up(1, 1, 1)
                down(1, 1, 0)
                with pe.Fori(2, TILES[l] // 2) as p:
                    pair(p)
                p = TILES[l] // 2
                if TILES[l] % 2:
                    up(p, 0, 0)
                    down(p - 1, 1, 1)
                    up(p, 0, 1)
                    down(p, 0, 0)
                    down(p, 0, 1)
                else:
                    down(p - 1, 1, 1)

            out_projection(0)
            shifts_rest0()
            norm_transposes(1)
            zero(0, 1, 2, 3)
            logits(0)
            ffn(0)
            shifts1()
            gates(1)
            norm_transposes(2)

            for m in range(4):
                project1(0, m)
            maxima_pass(1, ([[lambda m=m: project1(1, m)] for m in range(4)], [[]] * SLOTS))
            pe.wait_ge(k1_loaded, 16 * 2 * B)
            values_pass(1)
            out_projection(1)
            norm_transposes(3)
            zero(0, 1, 2, 3)
            logits(1)
            ffn(1)

        @block.scalar
        def _(act):
            def ge(s, value):
                if not (isinstance(value, int) and value <= 0):
                    act.wait_ge(s, value)

            act.wait_ge(loaded["ct"], 16)
            nc.scalar.activation(sc[:, :, :, :], ct[:, :, :, :], ACT.Silu).then_inc(sc_done, 1)

            def gates(l):
                act.wait_ge(mod_ps, (2, 5)[l])
                bank = GATE_BANK[l]
                for g in range(2):
                    nc.scalar.activation(gate[:, l, g, :, :].rearrange("p b d -> p (b d)"), PS[:, bank + g, :],
                                         ACT.Copy, scale=2.0).then_inc(gate_taken, 1)

            def norm(n):
                l, j = n // 2, 4 * (n % 2)
                act.wait_ge(rs_ready, n + 1)
                for t in range(NT):
                    ins = nc.scalar.activation(xnb[1][:, t, :], x[:, 1, t, :], ACT.Identity, bias=nm[:, 1, t:t + 1],
                                               scale=rs[:, 1, t:t + 1])
                ins.then_inc(xn_ready[1], 1)
                for b in range(B):
                    if b:
                        act.wait_ge(xt_ready, 2 * n + 2)
                        act.wait_ge(modT_taken, (1, 2, 4, 4)[n])
                        for c in range(KC):
                            nc.scalar.activation(hF[:, c, 1, :], PS[:, 6 + c, :], ACT.Identity,
                                                 bias=modT[:, l, j + c, 1:2], scale=modT[:, l, j + 2 + c, 1:2])\
                                .then_inc(h_ready[1], 1)
                    for c in range(KC):
                        act.wait_ge(h_ready[b], 2 * n + c + 1)
                        nc.scalar.activation(hR[0][:, c, b, :], hF[:, c, b, :], ACT.Copy).then_inc(hi_ready, 1)

            act.wait_ge(loaded["wqkv"], 16)
            nc.scalar.activation(wqkv[0][:, :, :], w_raw[:, :, :], ACT.Copy).then_inc(wqkv_high, 1)
            norm(0)

            def mask_q(l, b, g, s):
                a = at[l]
                u = 4 * g + s
                ge(a["s"], (2, 3)[l] * (u - 3))
                head = g - BQ * b
                nc.scalar.activation(qm[s][:, :], qkR[0][:, bass.ds(head // 2, 1), :].rearrange("p m t -> p (m t)").bitcast(F32),
                                     ACT.Copy, scale=headmask[:, bass.ds(4 * head + s, 1)]).then_inc(a["qm"], 1)

            def mask_first(l, b):
                act.wait_ge(qhi, (0, 4 * B)[l] + (4, 3)[l] * b + 2)
                act.wait_ge(loaded["headmask"], 16)
                for s in range(SLOTS):
                    mask_q(l, b, BQ * b, s)

            def mask_rest(l, b):
                with act.Fori(BQ * b + 1, BQ * (b + 1)) as g:
                    for s in range(SLOTS):
                        mask_q(l, b, g, s)

            def max_high(l, b):
                a = at[l]
                act.wait_ge(a["mt"], b + 1)
                nc.scalar.activation(mxT[0][:, b, :], PS[0:H * NT, MAX_BANK[l], 0:P], ACT.Copy).then_inc(a["mhi"], 1)
                if b:
                    store_maxima(act, l, b)

            def take_v(b):
                for i in range(2):
                    act.wait_ge(proj, 6 * b + 4 + i + 1)
                    for j in range(2):
                        ins = nc.scalar.activation(
                            V[:, 2 * i + j, b * H:(b + 1) * H, 0:DH],
                            PS[:, 4 + 2 * b + i, j * D:(j + 1) * D].rearrange("p (h d) -> p h d", d=DH), ACT.Copy)
                    ins.then_inc(v_taken, 1)

            for m in range(4):
                act.wait_ge(proj, m + 1)
                nc.scalar.activation(qkR[0][:, m, :], PS[:, m, :], ACT.Copy, scale=SCALE if m < 2 else 1.0).then_inc(qhi, 1)
            mask_first(0, 0)
            take_v(0)
            for m in range(4):
                act.wait_ge(proj, 6 + m + 1)
                nc.scalar.activation(q0F[:, m, :], PS[:, (5, 6, 7, 5)[m], :], ACT.Copy, scale=SCALE if m < 2 else 1.0)\
                    .then_inc(q0F_ready, 1)
            mask_rest(0, 0)
            act.wait_ge(at[0]["s"], 2 * H)

            def q0_high(ms):
                for m in ms:
                    act.wait_ge(scr0_written[m], 16 * (4, 2)[m // 2])
                    act.wait_ge(q0F_ready, m + 1)
                    nc.scalar.activation(qkR[0][:, m, :], q0F[:, m, :], ACT.Copy).then_inc(qhi, 1)

            q0_high(ORDER0[1][:2])
            mask_first(0, 1)
            q0_high(ORDER0[1][2:])
            take_v(1)
            max_high(0, 0)
            mask_rest(0, 1)
            max_high(0, 1)

            def exponentials(l, g, s):
                a = at[l]
                u = 4 * g + s
                h = s % 2
                ge(a["o"], u + 1 - SLOTS)
                if l == 0:
                    ge(a["st"], u + 1)
                    nc.scalar.activation(
                        probs[l][s][:, 0:NT * KEYS0].rearrange("p (a k) -> p a k", k=2 * KEYS0),
                        PS[:, 2 * h:2 * h + 2, 0:2 * KEYS0], ACT.Exp)\
                        .then_inc(a["p"], 1)
                    return
                flat = PS[:, 3 * h:3 * h + 3, :].rearrange("p a q -> p (a q)")
                for i, (lo, hi) in enumerate(((0, S), (S, SPAN1))):
                    ge(a["st"], 2 * u + i + 1)
                    nc.scalar.activation(probs[l][s][:, lo:hi], flat[:, lo:hi], ACT.Exp).then_inc(a["p"], 1)

            def out_high(l, b, g):
                ge(at[l]["od"], g + 1)
                nc.scalar.activation(oT[b][0][:, bass.ds(g - BQ * b, 1), :].rearrange("p c t -> p (c t)"), oN[:, :],
                                     ACT.Copy).then_inc(at[l]["oh"], 1)

            def attention(l):
                def quad(g, b):
                    for s in range(SLOTS):
                        exponentials(l, g, s)
                        if l == 0 and isinstance(g, int) and g == 0 and s == 1:
                            gates(0)
                        if s == 0 and b is not None:
                            out_high(l, b, g - 2)

                if l == 0:
                    act.wait_ge(split, 3)
                quad(0, None)
                quad(1, None)
                for b, (start, end) in enumerate(((2, BQ + 2), (BQ + 2, QUADS))):
                    with act.Fori(start, end) as g:
                        quad(g, b)
                out_high(l, B - 1, QUADS - 2)
                out_high(l, B - 1, QUADS - 1)

            attention(0)

            def take_rows(l):
                for b in range(B):
                    act.wait_ge(cT_ps, 2 * l + b + 1)
                    nc.scalar.activation(cT[:, b, :], PS[0:SELK, 6 + b, :], ACT.Copy).then_inc(cT_ready, 1)

            def take_table(l):
                for i in range(HALVES[l] * B):
                    act.wait_ge(cB_ps, l * HALVES[0] * B + i + 1)
                    nc.scalar.activation(cB[i % B][i // B], PS[:, 6 + i % B, :], ACT.Copy).then_inc(cB_ready, 1)

            def weights_high(l, p, s):
                f = ff[l]
                i = 2 * p + s
                ge(f[f"w{s}"], 16 * (p + 1))
                if isinstance(i, int) and i < 2:
                    if l:
                        act.wait_ge(ff[0]["w2"], 2 * TILES[0])
                else:
                    ge(f["w2"], 2 * (i - 1))
                nc.scalar.activation(fwR[s][0], fw[s][:, :], ACT.Copy).then_inc(f["hi_w"], 1)

            def ffn(l):
                f = ff[l]

                def silu(u, b):
                    ge(f["g"], u + 1)
                    nc.scalar.activation(gact[b], PS[:, 4, :], ACT.Silu).then_inc(f["silu"], 1)

                def high(u, b):
                    ge(f["w2"], u - 1)
                    nc.scalar.activation(hidR[b][0], hid[b], ACT.Copy).then_inc(f["hi"], 1)

                def early_unit(u, b):
                    ge(f["early_hid"], u - 1)
                    silu(u, b)
                    ge(f["early_hid"], u + 1)
                    high(u, b)

                def unit(u, b, routed):
                    if isinstance(u, int) and u < EU + B:
                        ge(f["early_hid"], u - 1)
                    else:
                        ge(f["gu"], u - 1 - EU)
                    silu(u, b)
                    if routed:
                        ge(f["hid"], u + 1 - 2 * SHT[l])
                    else:
                        ge(f["gu"], u + 1 - EU)
                    high(u, b)

                def pair(p, one, following, kind=None, beside=(None, None)):
                    for s in range(2):
                        for b in range(B):
                            u = 4 * p + 2 * s + b
                            if one is unit:
                                unit(u, b, routed(l, p if kind is None else kind, s))
                            else:
                                one(u, b)
                            if s == 0 and beside[b]:
                                beside[b](l)
                            if b == 0 and (one is unit or s == 1) and (s == 0 or following):
                                weights_high(l, p + s, 1 - s)

                pair(0, early_unit, True)
                pairs = TILES[l] // 2
                pair(1, unit, True, beside=(take_rows, take_table))
                for start, end in SPANS[l]:
                    with act.Fori(start, end - (end == pairs)) as p:
                        pair(p, unit, True, start)
                pair(pairs - 1, unit, TILES[l] % 2)
                if TILES[l] % 2:
                    for b in range(B):
                        unit(4 * pairs + b, b, True)

            for i in range(2):
                weights_high(0, 0, i)
            norm(1)
            act.wait_ge(z_ready, 1)
            nc.scalar.activation(ez[:, :, :], lg[:, :, :], ACT.Exp).then_inc(ez_ready, 1)
            ffn(0)
            act.wait_ge(mod_ps, 4)
            nc.scalar.activation(modT[:, 1, :, :].rearrange("p j b -> p (j b)"), PS[:, 7, 8 * B:2 * 8 * B], ACT.Copy)\
                .then_inc(shifts1_taken, 1)
            gates(1)
            norm(2)

            act.wait_ge(loaded["bq"], 16)
            act.wait_ge(loaded["bk"], 16)
            nc.scalar.activation(bqs[:, :], bq[:, :], ACT.Copy, scale=SCALE).then_inc(act_order, 1)
            act.wait_ge(act_order, 1)
            def take_q1(b, m):
                act.wait_ge(proj, 6 * B + 4 * b + m + 1)
                bank = ((0, 1, 2), (7, 6, 7))[b][m]
                bias, scale = (bqs[:, m:m + 1], SCALE) if m < KC else (bk[:, :], 1.0)
                nc.scalar.activation(qF[:, m, :], PS[:, bank, :], ACT.Identity, bias=bias, scale=scale).then_inc(qF_ready, 1)

            def q1_high(b, m):
                act.wait_ge(qF_ready, 3 * b + m + 1)
                nc.scalar.activation(qkR[0][:, m, :], qF[:, m, :], ACT.Copy).then_inc(qhi, 1)

            for m in range(3):
                take_q1(0, m)
                q1_high(0, m)
            mask_first(1, 0)
            act.wait_ge(qlo, 4 * B + 3)
            for m in range(3):
                take_q1(1, m)
            mask_rest(1, 0)
            act.wait_ge(scr1_written, 16 * 10)
            act.wait_ge(at[1]["s"], 3 * H)
            for m in range(3):
                q1_high(1, m)
            mask_first(1, 1)
            max_high(1, 0)
            mask_rest(1, 1)
            max_high(1, 1)

            attention(1)
            for i in range(2):
                weights_high(1, 0, i)
            norm(3)
            act.wait_ge(lg_ps, 2)
            nc.scalar.activation(ez[:, :, 0:EXPERTS[1]],
                                 PS[:, LOGIT_BANK, 0:B * NT * EXPERTS[1]].rearrange("p (t e) -> p t e", e=EXPERTS[1]),
                                 ACT.Sigmoid).then_inc(ez_ready, 1)
            ffn(1)

        @block.vector
        def _(dve):
            order = [0]

            def then(ins):
                order[0] += 1
                ins.then_inc(dve_order, 1)
                dve.wait_ge(dve_order, order[0])

            def ge(s, value):
                if not (isinstance(value, int) and value <= 0):
                    dve.wait_ge(s, value)

            tt, ts, stt = nc.vector.tensor_tensor, nc.vector.tensor_scalar, nc.vector.scalar_tensor_tensor

            dve.wait_ge(sc_done, 1)
            def spread_silu(l):
                nc.vector.tensor_copy(scb[:, :, :], sc[:, l, :, :].rearrange("p k b -> p (k b)").unsqueeze(2)
                                      .to_broadcast([P, KC * B, P])).then_inc(scb_done, 1)


            def statistics(b, tiles):
                for t in tiles:
                    ins = nc.vector.bn_stats(stats[:, b, t, :], x[:, b, t, :])
                ins.then_inc(stats_done, 1)

                def aggregate(count):
                    dve.wait_ge(stats_done, count)
                    for t in tiles:
                        ins = nc.vector.bn_aggr(mv[:, b, t, :], stats[:, b, t, :])
                    ins.then_inc(mv_done, 1)
                return aggregate

            def norm(n):
                l, j = n // 2, 4 * (n % 2)
                dve.wait_ge(mv_done, B + 2 * B * n)
                v, r, w = ve[:, :, :], rs[:, :, :], nt_[:, :, :]
                then(ts(v, mv[:, :, :, 1], EPS, None, ALU.add))
                then(ts(r.bitcast(I32), v.bitcast(I32), 1, None, ALU.logical_shift_right))
                then(ts(r.bitcast(I32), r.bitcast(I32), -1.0, RSQRT_MAGIC, ALU.mult, ALU.add))
                for _ in range(3):
                    then(tt(w, r, r, ALU.mult))
                    then(stt(w, w, -0.5, v, ALU.mult, ALU.mult))
                    then(stt(r, w, 1.5, r, ALU.add, ALU.mult))
                stt(nm[:, :, :], mv[:, :, :, 0], -1.0, r, ALU.mult, ALU.mult).then_inc(rs_ready, 1)
                for t in range(NT):
                    ins = ts(xnb[0][:, t, :], x[:, 0, t, :], mv[:, 0, t, 0:1], rs[:, 0, t:t + 1], ALU.subtract, ALU.mult)
                ins.then_inc(xn_ready[0], 1)
                if n == 0:
                    dve.wait_ge(wqkv_high, 1)
                    tt(wqkv[1][:, :, :], w_raw[:, :, :], wqkv[0][:, :, :].bitcast(F32), ALU.subtract).then_inc(wqkv_ready, 1)
                    first_modulation()
                if n == 1:
                    modulation_rest0()
                if n == 2:
                    modulation1()
                dve.wait_ge(xt_ready, 2 * n + 1)
                for c in range(KC):
                    ts(hF[:, c, 0, :], PS[:, 4 + c, :], modT[:, l, j + 2 + c, 0:1], modT[:, l, j + c, 0:1],
                       ALU.mult, ALU.add).then_inc(h_ready[0], 1)
                for b in range(B):
                    for c in range(KC):
                        dve.wait_ge(hi_ready, 2 * (2 * n + b) + c + 1)
                        tt(hR[1][:, c, b, :], hF[:, c, b, :], hR[0][:, c, b, :].bitcast(F32), ALU.subtract)\
                            .then_inc(hl_ready, 1)

            flatT = modT[:, :, :, :].rearrange("p l j b -> p (l j b)")

            def first_modulation():
                dve.wait_ge(mod_ps, 1)
                then(nc.vector.tensor_copy(flatT[:, 0:4 * B], PS[:, 7, 0:4 * B]))
                scales = modT[:, 0, 2:4, :]
                ts(scales, scales, 1.0, None, ALU.add).then_inc(modT_taken, 1)
                dve.wait_ge(modT_taken, 1)

            def modulation_rest0():
                dve.wait_ge(mod_ps, 3)
                then(nc.vector.tensor_copy(flatT[:, 4 * B:8 * B], PS[:, 7, 4 * B:8 * B]))
                scales = modT[:, 0, 6:8, :]
                ts(scales, scales, 1.0, None, ALU.add).then_inc(modT_taken, 1)
                dve.wait_ge(modT_taken, 2)

            def modulation1():
                dve.wait_ge(shifts1_taken, 1)
                for j in (2, 6):
                    scales = modT[:, 1, j:j + 2, :]
                    ts(scales, scales, 1.0, None, ALU.add).then_inc(modT_taken, 1)
                dve.wait_ge(modT_taken, 4)

            def gate_steps(l):
                g = gate[:, l, :, :, :].rearrange("p g b d -> p (g b d)")
                dve.wait_ge(gate_taken, 2 * (l + 1))
                then(ts(gsign[l], g, 0.0, 0.5, ALU.is_ge, ALU.subtract))
                then(stt(g, g, -1.0, g, ALU.mult, ALU.max))
                then(stt(g, g, 0.5, gsign[l], ALU.max, ALU.mult))

            for b in range(B):
                dve.wait_ge(loaded[f"x{b}"], 16)
                statistics(b, range(NT))(b + 1)
            norm(0)

            def maxima(l, g, s):
                a = at[l]
                u = 4 * g + s
                h = s % 2
                if l == 0:
                    for i in range(2):
                        ge(a["s"], 2 * u + i + 1)
                        nc.vector.tensor_reduce(nmx[:, bass.ds(NT * u + 2 * i, 2)],
                                                PS[:, 2 * h + i, 0:2 * KEYS0].rearrange("p (t k) -> p t k", k=KEYS0),
                                                X, ALU.max, negate=True).then_inc(a["mxd"], 1)
                    return
                for bank, qt, k, w in ((0, 0, 2, 2 * P), (1, 2, 1, 3 * P), (2, 3, 1, 4 * P)):
                    ge(a["s"], 3 * u + bank + 1)
                    nc.vector.tensor_reduce(nmx[:, bass.ds(NT * u + qt, k)],
                                            PS[:, 3 * h + bank, 0:k * w].rearrange("p (t k) -> p t k", k=w),
                                            X, ALU.max, negate=True).then_inc(a["mxd"], 1)

            def max_low(l, b):
                a = at[l]
                dve.wait_ge(a["mhi"], b + 1)
                tt(mxT[1][:, b, :], PS[0:H * NT, MAX_BANK[l], 0:P], mxT[0][:, b, :].bitcast(F32), ALU.subtract)\
                    .then_inc(a["mlo"], 1)

            def take_outputs(l, g):
                a = at[l]
                ge(a["od"], g)
                ge(a["o"], 4 * g + 4)
                nc.vector.tensor_copy(oF[:, l:], PS[:, 6, l:]).then_inc(a["oe"], 1)

            def divide(l, g):
                a = at[l]
                n = len(DEN[l])
                for i, (lo, hi, bank) in enumerate(DEN[l]):
                    ge(a["den"], n * g + i + 1)
                    nc.vector.reciprocal(oR[:, lo:hi], PS[:, bank, 0:hi - lo]).then_inc(a["rd"], 1)
                ge(a["rd"], n * (g + 1))
                ge(a["ol"], g)
                tt(oN[:, :], oF[:, :], oR[:, :], ALU.mult).then_inc(a["od"], 1)

            def maxima_first(l, b):
                for s in range(SLOTS):
                    maxima(l, BQ * b, s)

            def maxima_rest(l, b):
                with dve.Fori(BQ * b + 1, BQ * (b + 1)) as g:
                    for s in range(SLOTS):
                        maxima(l, g, s)

            def outputs_pass(l):
                if l:
                    nc.vector.tensor_copy(oF[:, 0:1], esel[:, P:]).then_inc(o_first, 1)
                    dve.wait_ge(o_first, 1)
                take_outputs(l, 0)
                divide(l, 0)
                with dve.Fori(1, QUADS) as g:
                    take_outputs(l, g)
                    divide(l, g)

            for m in range(4):
                dve.wait_ge(qhi, m + 1)
                stt(qkR[1][:, m, :], PS[:, m, :], SCALE if m < 2 else 1.0, qkR[0][:, m, :].bitcast(F32),
                    ALU.mult, ALU.subtract).then_inc(qlo, 1)
            maxima_first(0, 0)
            maxima_rest(0, 0)
            for i, m in enumerate(ORDER0[1]):
                dve.wait_ge(qhi, 4 + i + 1)
                tt(qkR[1][:, m, :], q0F[:, m, :], qkR[0][:, m, :].bitcast(F32), ALU.subtract).then_inc(qlo, 1)
            maxima_first(0, 1)
            spread_silu(0)
            max_low(0, 0)
            maxima_rest(0, 1)
            max_low(0, 1)
            gate_steps(0)
            outputs_pass(0)

            def gated(l, which, banks, done, count):
                n = 2 * l + which
                aggregate = None
                for k in range(2 * B):
                    b, i = k // 2, k % 2
                    dve.wait_ge(done, count(b, i))
                    y = PS[:, banks[b] + i, :].rearrange("p (t d) -> p t d", d=D)
                    tmp = ytmp[:, 2 * i:2 * i + 2, :]
                    tt(tmp, y, gate[:, l, which, b, :].unsqueeze(1).to_broadcast([P, 2, D]), ALU.mult).then_inc(y_gated, 1)
                    if aggregate:
                        aggregate(B + 2 * B * n + k)
                    dve.wait_ge(y_gated, 2 * B * n + k + 1)
                    tt(x[:, b, 2 * i:2 * i + 2, :], x[:, b, 2 * i:2 * i + 2, :], tmp, ALU.add).then_inc(x_new, 1)
                    if n < 3:
                        dve.wait_ge(x_new, 2 * B * n + k + 1)
                        aggregate = statistics(b, (2 * i, 2 * i + 1))
                if aggregate:
                    aggregate(B + 2 * B * (n + 1))

            def add_output_bias():
                dve.wait_ge(loaded["bo"], 16)
                gated_bias = ytmp[:, 0:B, :]
                then(tt(gated_bias, gate[:, 1, 0, :, :], bo[:, :].unsqueeze(1).to_broadcast([P, B, D]), ALU.mult))
                for b in range(B):
                    ins = tt(x[:, b, :, :], x[:, b, :, :], gated_bias[:, b, :].unsqueeze(1).to_broadcast([P, NT, D]), ALU.add)
                then(ins)

            def add_attention(l):
                gated(l, 0, Y_BANK, y_ps, lambda b, i: 4 * l + 2 * b + i + 1)

            def early_product(l, u):
                f = ff[l]
                ge(f["early_lo"], u - 1)
                dve.wait_ge(f["silu"], u + 1)
                dve.wait_ge(f["u"], u + 1)
                tt(hid[u % 2], gact[u % 2], PS[:, 5, :], ALU.mult).then_inc(f["early_hid"], 1)

            def ranks(values, k, m, tril, beside=lambda i: None):
                A, Bv = cmpA[:, :, 0:m, 0:m], cmpB[:, :, 0:m, 0:m]
                shape = [P, B * NT, m, m]
                own = values.unsqueeze(3).to_broadcast(shape)
                other = values.unsqueeze(2).to_broadcast(shape)
                tt(A, other, own, ALU.is_gt)
                beside(0)
                then(tt(Bv, other, own, ALU.is_equal))
                beside(1)
                then(tt(Bv, Bv, tril[:, 0:m, 0:m].unsqueeze(1).to_broadcast(shape), ALU.mult))
                then(tt(A, A, Bv, ALU.add))
                beside(2)
                then(nc.vector.tensor_reduce(rank[:, :, 0:m], A, X, ALU.add))
                then(ts(rank[:, :, 0:m], rank[:, :, 0:m], float(k), None, ALU.is_lt))
                return rank[:, :, 0:m]

            def combine_parts(c, E):
                rows = cparts[:, :, :, :].rearrange("p b t k -> p (b t) k")
                then(nc.vector.tensor_copy(cR[:, :, 0:E], c))
                hi = cR[:, :, 0:E].bitcast(F32)
                nc.vector.tensor_copy(rows[:, :, 0:E], hi)
                tt(rows[:, :, 16:16 + E], c, hi, ALU.subtract).then_inc(cp_ready, 1)

            def router0():
                E, G, T = EXPERTS[0], 4, B * NT
                dve.wait_ge(loaded["tri"], 16)
                dve.wait_ge(lg_ps, 1)
                raw = PS[:, LOGIT_BANK, 0:T * E].rearrange("p (t e) -> p t e", e=E)
                then(nc.vector.tensor_reduce(r4[0][:, :], raw, X, ALU.max))
                tt(lg[:, :, :], raw, r4[0][:, :].unsqueeze(2).to_broadcast([P, T, E]), ALU.subtract).then_inc(z_ready, 1)
                dve.wait_ge(ez_ready, 1)
                then(nc.vector.tensor_reduce(r4[1][:, :], ez[:, :, :], X, ALU.add))
                then(nc.vector.reciprocal(r4[1][:, :], r4[1][:, :]))
                then(tt(prob[:, :, :], ez[:, :, :], r4[1][:, :].unsqueeze(2).to_broadcast([P, T, E]), ALU.mult))
                p4 = prob[:, :, :].rearrange("p t (g e) -> p t g e", e=E // G)
                then(nc.vector.tensor_reduce(gs[:, :, :], p4, X, ALU.max))
                chosen = ranks(gs[:, :, :], 2, G, tri)
                spread = chosen.unsqueeze(3).to_broadcast([P, T, G, E // G])
                m4 = masked[:, :, :].rearrange("p t (g e) -> p t g e", e=E // G)
                then(tt(m4, p4, spread, ALU.mult))
                then(tt(m4, m4, spread, ALU.add))
                then(ts(masked[:, :, :], masked[:, :, :], -1.0, None, ALU.add))
                early_product(0, 0)
                chosen = ranks(masked[:, :, :], 4, E, tri, lambda i: early_product(0, i + 1) if i < EU - 1 else None)
                then(tt(masked[:, :, :], prob[:, :, :], chosen, ALU.mult))
                combine_parts(masked[:, :, :], E)

            def router1():
                E, T = EXPERTS[1], B * NT
                dve.wait_ge(loaded["ebias"], 16)
                dve.wait_ge(ez_ready, 2)
                s = ez[:, :, 0:E]
                then(tt(masked[:, :, 0:E], s, ebias[:, :].unsqueeze(1).to_broadcast([P, T, E]), ALU.add))
                chosen = ranks(masked[:, :, 0:E], 2, E, tri)
                early_product(1, 0)
                then(tt(prob[:, :, 0:E], s, chosen, ALU.mult))
                then(nc.vector.tensor_reduce(r4[0][:, :], prob[:, :, 0:E], X, ALU.add))
                then(ts(r4[0][:, :], r4[0][:, :], 1e-9, None, ALU.add))
                then(nc.vector.reciprocal(r4[0][:, :], r4[0][:, :]))
                then(tt(masked[:, :, 0:E], prob[:, :, 0:E], r4[0][:, :].unsqueeze(2).to_broadcast([P, T, E]), ALU.mult))
                combine_parts(masked[:, :, 0:E], E)
                for u in range(1, EU):
                    early_product(1, u)

            def ffn(l):
                f = ff[l]

                def unit(u, b, half):
                    if isinstance(u, int) and u < EU + B:
                        dve.wait_ge(f["early_lo"], u - 1)
                    ge(f["silu"], u + 1)
                    ge(f["u"], u + 1)
                    tt(hid[b] if half is None else gu[b], gact[b], PS[:, 5, :], ALU.mult).then_inc(f["gu"], 1)
                    if half is not None:
                        ge(f["gu"], u + 1 - EU)
                        tt(hid[b], gu[b], cB[b][half], ALU.mult).then_inc(f["hid"], 1)
                    ge(f["hi"], u + 1)
                    tt(hidR[b][1], hid[b], hidR[b][0].bitcast(F32), ALU.subtract).then_inc(f["lo"], 1)

                def pair(p, kind):
                    for s in range(2):
                        half = (s + SHT[l]) % HALVES[l] if routed(l, kind, s) else None
                        for b in range(B):
                            if half is not None and isinstance(p, int) and b == 0:
                                dve.wait_ge(cB_ready, sum(HALVES[:l + 1]) * B)
                            unit(4 * p + 2 * s + b, b, half)

                pair(1, 1)
                dve.wait_ge(cB_ready, sum(HALVES[:l + 1]) * B)
                for start, end in SPANS[l]:
                    with dve.Fori(start, end) as p:
                        pair(p, start)
                if TILES[l] % 2:
                    for b in range(B):
                        unit(4 * (TILES[l] // 2) + b, b, (TILES[l] - 1 - SHT[l]) % HALVES[l])
                dve.wait_ge(f["lo"], 2 * TILES[l] - EU)
                gated(l, 1, (0, 2), f["w2"], lambda b, i: 2 * TILES[l] - 1 + b)

            add_attention(0)
            norm(1)
            router0()
            spread_silu(1)
            ffn(0)
            norm(2)
            gate_steps(1)
            dve.wait_ge(loaded["bv"], 16)
            dve.wait_ge(loaded["esel"], 16)
            dve.wait_ge(consts, CONSTS)
            def q1_low(b):
                for m in range(3):
                    dve.wait_ge(qhi, 4 * B + 3 * b + m + 1)
                    tt(qkR[1][:, m, :], qF[:, m, :], qkR[0][:, m, :].bitcast(F32), ALU.subtract).then_inc(qlo, 1)

            def take_v1(b):
                dve.wait_ge(proj, 6 * B + 4 * b + 4)
                tt(V1[:, :, b, 0:DH], PS[:, (3, 6)[b], 0:NT * DH].rearrange("p (t d) -> p t d", d=DH),
                   bv[:, :].unsqueeze(1).to_broadcast([P, NT, DH]), ALU.add).then_inc(v1_taken, 1)

            q1_low(0)
            take_v1(0)
            maxima_first(1, 0)
            take_v1(1)
            maxima_rest(1, 0)
            q1_low(1)
            maxima_first(1, 1)
            max_low(1, 0)
            maxima_rest(1, 1)
            max_low(1, 1)
            add_output_bias()
            outputs_pass(1)
            add_attention(1)
            norm(3)
            router1()
            ffn(1)


def shape_tables():
    q = np.arange(P)[:, None]
    c = np.arange(KEYS0)[None, :]
    band = (c >= q) & (c <= q + WIN)
    later = np.where(band, 0.0, NEG)
    first = np.where(band & (c >= WIN), 0.0, NEG)
    causal = np.where(np.arange(P)[None, :] < q, 0.0, NEG)
    bandT = np.where((c >= q) & (c <= q + WIN), 0.0, NEG)
    mask = np.concatenate([first, later, bandT, causal, np.full((P, P), NEG), causal.T], 1).astype(np.float32)
    headmask = (q // DH == np.arange(H)[None, :] % (P // DH)).astype(np.float32)
    tri = np.broadcast_to(np.tril(np.ones((16, 16)), -1), (P, 16, 16)).astype(np.float32)
    denominator = (q % VW == DH).astype(np.float32)
    esel = np.concatenate([denominator * (q // VW == np.arange(P)[None, :] // VW), denominator], 1).astype(np.float32)
    k = np.arange(SELK)[:, None, None]
    expert = np.arange(2)[None, :, None] * EG + np.arange(P)[None, None, :] // GR
    csel = ((k == expert) | (k == 16 + expert)).astype(np.float32).reshape(SELK, 2 * P)
    return {"ident": np.eye(P, dtype=np.float32), "mask": mask, "tri": np.ascontiguousarray(tri), "esel": esel,
            "headmask": headmask, "csel": csel}


def chunked_T(w):
    return np.ascontiguousarray(w.T.reshape(KC, P, w.shape[0]))


def by_output_rows(w):
    w = np.pad(w.T.reshape(H, DH, D), ((0, 0), (0, VW - DH), (0, 0)))
    return np.ascontiguousarray(w.reshape(OC, P, D))


def ffn_tiles(l, routed, shared):
    tiles = []
    for r, sh in zip(routed, shared):
        sh = np.pad(sh, ((0, SHT[l] * P - sh.shape[0]), (0, 0)))
        r = r.reshape(HALVES[l], EG, INTER[l] // GR, GR, D).transpose(2, 0, 1, 3, 4).reshape(-1, D)
        tiles.append(np.concatenate([sh, r], 0).reshape(TILES[l], P, D))
    up = [w.transpose(0, 2, 1).reshape(TILES[l], KC, P, P).transpose(0, 2, 1, 3).reshape(TILES[l], P, D) for w in tiles[:2]]
    return np.ascontiguousarray(np.concatenate(up + [tiles[2]], 2))


def kernel(**inputs):
    import concourse.bacc as bacc
    from concourse.bass_utils import run_bass_kernel_spmd as run

    i = {k: np.asarray(v) for k, v in inputs.items()}
    tables = shape_tables()
    arrays = {
        "x": i["L0_attn_x"].reshape(B * S, D),
        "ct": np.ascontiguousarray(np.stack([i[f"L{l}_c"] for l in range(2)], 0).transpose(2, 0, 1)
                                   .reshape(KC, P, 2, B).transpose(1, 2, 0, 3)),
        "wmod0": i["L0_wmod"], "wmod1": i["L1_wmod"],
        "wqkv": chunked_T(i["L0_attn_w_qkv"]), "wout0": by_output_rows(i["L0_attn_w_out"]),
        "wq1": chunked_T(i["L1_attn_Wq"]),
        "wkv1": chunked_T(np.concatenate([np.tile(i["L1_attn_Wk"], (P // DH, 1)), i["L1_attn_Wv"]], 0)),
        "wout1": by_output_rows(i["L1_attn_Wo"]),
        "wg0": chunked_T(i["L0_ffn_Wg"]), "wg1": chunked_T(i["L1_ffn_router_w"]),
        "bq": np.ascontiguousarray(i["L1_attn_bq"].reshape(KC, P).T), "bk": np.tile(i["L1_attn_bk"], P // DH).reshape(P, 1),
        "bv": i["L1_attn_bv"], "bo": i["L1_attn_bo"], "ebias": i["L1_ffn_expert_bias"],
        "ffn0": ffn_tiles(0, [i["L0_ffn_W1"], i["L0_ffn_W3"], i["L0_ffn_W2"].transpose(0, 2, 1)],
                          [i["L0_ffn_Ws1"], i["L0_ffn_Ws3"], i["L0_ffn_Ws2"].T]),
        "ffn1": ffn_tiles(1, [i["L1_ffn_w12"][:, :INTER[1]], i["L1_ffn_w12"][:, INTER[1]:], i["L1_ffn_w3"].transpose(0, 2, 1)],
                          [i["L1_ffn_sw1"], i["L1_ffn_sw2"], i["L1_ffn_sw3"].T]),
    }
    arrays.update(tables)
    arrays = {k: np.ascontiguousarray(v) for k, v in arrays.items()}
    nc = bacc.Bacc("TRN2", target_bir_lowering=False, num_devices=1)
    io = {k: nc.dram_tensor(f"in_{k}", v.shape, F32, kind="ExternalInput").ap() for k, v in arrays.items()}
    out = nc.dram_tensor("out", (B * S, D), F32, kind="ExternalOutput").ap()
    build(nc, io, out)
    r = run(nc, [{f"in_{k}": v for k, v in arrays.items()}], core_ids=[0])
    return r.results[0]["out"].reshape(B, S, D)
```
